# Optimizing a Trainium2 kernel written in Bass

```python
import numpy as np
import jax
import jax.numpy as jnp

def _softmax(x, axis=-1):
    return jax.nn.softmax(x, axis=axis)

def _gelu(x):
    return jax.nn.gelu(x, approximate=True)

def _silu(x):
    return jax.nn.silu(x)

def _sigmoid(x):
    return jax.nn.sigmoid(x)

def _layernorm(x, axis=-1, eps=1e-05):
    m = jnp.mean(x, axis=axis, keepdims=True)
    v = jnp.var(x, axis=axis, keepdims=True)
    return (x - m) / jnp.sqrt(v + eps)

def _scatter_add(tgt, idx, src, axis=0):
    return tgt.at[idx].add(src)

def _segment_sum(src, seg, n):
    return jax.ops.segment_sum(src, seg, n)
kernel_name = 'mk_perceiver_d1_seqx_r4_f6752c'

def setup_inputs(seed: int=0):
    np.random.seed(seed)
    _w = jnp.asarray

    def _rec_inputs():
        import jax
        import jax.numpy as jnp
        _rk = jax.random.key(seed)
        x = -0.0003929 + 0.9999 * jax.random.normal(jax.random.fold_in(_rk, 1), (64, 32, 256), jnp.float32)
        _lenS = 32 - jax.random.randint(jax.random.fold_in(_rk, 7), (64,), 0, max(1, 32 // 4) + 1, jnp.int32)
        _lenS2 = 257 - jax.random.randint(jax.random.fold_in(_rk, 8), (64,), 0, max(1, 257 // 4) + 1, jnp.int32)
        _ctx_768P = jax.random.normal(jax.random.fold_in(_rk, 11), (64, 16, 192), jnp.float32)
        _ctx_768c = jax.random.dirichlet(jax.random.fold_in(_rk, 511), 0.3 * jnp.ones((16,), jnp.float32), (64, 257))
        _ctx_768t = jnp.einsum('bsk,bkd->bsd', _ctx_768c, _ctx_768P)
        _ctx_768t = _ctx_768t * jax.lax.rsqrt(jnp.mean(jnp.square(_ctx_768t)) + 1e-12) * 0.953939
        ctx_768 = 0.00095986 + 0.999812 * (_ctx_768t + 0.3 * jax.random.normal(jax.random.fold_in(_rk, 611), (64, 257, 192), jnp.float32))
        _validS = jnp.arange(32)[None, :] < _lenS[:, None]
        _validS2 = jnp.arange(257)[None, :] < _lenS2[:, None]
        _causal = jnp.tril(jnp.ones((32, 32), dtype=bool))
        mask_BxS2_bf1 = jnp.ones((64, 257), dtype=bool)
        return (x, ctx_768, mask_BxS2_bf1)
    x, ctx_768, mask_BxS2_bf1 = _rec_inputs()

    def _L0_xattn_setup():
        import jax, jax.numpy as jnp
        import numpy as np
        DIM = 256
        CTX_DIM = 192
        HEADS = 16
        key = jax.random.key(seed)
        ks = jax.random.split(key, 7)
        B, N, M = (4, 1024, 64)
        x = jax.random.normal(ks[0], (B, N, DIM), dtype=jnp.float32)
        context = jax.random.normal(ks[1], (B, M, CTX_DIM), dtype=jnp.float32)
        context_mask = jnp.ones((B, M), dtype=bool)
        s_d = 1.0 / np.sqrt(DIM)
        s_c = 1.0 / np.sqrt(CTX_DIM)
        Wq = jax.random.normal(ks[2], (DIM, DIM), dtype=jnp.float32) * s_d
        Wk = jax.random.normal(ks[3], (CTX_DIM, DIM), dtype=jnp.float32) * s_c
        Wv = jax.random.normal(ks[4], (CTX_DIM, DIM), dtype=jnp.float32) * s_c
        Wo = jax.random.normal(ks[5], (DIM, DIM), dtype=jnp.float32) * s_d
        return {'x': x, 'context': context, 'context_mask': context_mask, 'Wq': Wq, 'Wk': Wk, 'Wv': Wv, 'Wo': Wo}
    _L0_xattn_all = _L0_xattn_setup()
    _L0_xattn_in = {k: v for k, v in _L0_xattn_all.items() if k in ('Wq', 'Wk', 'Wv', 'Wo')}
    del _L0_xattn_all

    def _L0_attn_setup():
        import jax, jax.numpy as jnp
        import numpy as np
        H = 256
        W_CTX = 2

        def _local_attention(x, Wq, bq, Wk, bk, Wv, bv):
            B, S, Hd = x.shape
            Q = x @ Wq + bq
            K = x @ Wk + bk
            V = x @ Wv + bv
            w = W_CTX
            win = 2 * w + 1
            idx = jnp.arange(S)[:, None] + jnp.arange(-w, w + 1)[None, :]
            valid = (idx >= 0) & (idx < S)
            idx_c = jnp.clip(idx, 0, S - 1)
            Kw = K[:, idx_c]
            Vw = V[:, idx_c]
            scores = jnp.einsum('bsh,bswh->bsw', Q, Kw) / jnp.sqrt(jnp.float32(Hd))
            scores = jnp.where(valid[None], scores, -jnp.inf)
            probs = jax.nn.softmax(scores, axis=-1)
            return jnp.einsum('bsw,bswh->bsh', probs, Vw)
        key = jax.random.key(seed)
        ks = jax.random.split(key, 7)
        B, S = (4, 512)
        sd = 1.0 / np.sqrt(H)
        inp = {'sequence_output': jax.random.normal(ks[0], (B, S, H), dtype=jnp.float32), 'Wq': jax.random.uniform(ks[1], (H, H), jnp.float32, -sd, sd), 'bq': jax.random.uniform(ks[2], (H,), jnp.float32, -sd, sd), 'Wk': jax.random.uniform(ks[3], (H, H), jnp.float32, -sd, sd), 'bk': jax.random.uniform(ks[4], (H,), jnp.float32, -sd, sd), 'Wv': jax.random.uniform(ks[5], (H, H), jnp.float32, -sd, sd), 'bv': jax.random.uniform(ks[6], (H,), jnp.float32, -sd, sd)}
        return inp
    _L0_attn_all = _L0_attn_setup()
    _L0_attn_in = {k: v for k, v in _L0_attn_all.items() if k in ('Wq', 'bq', 'Wk', 'bk', 'Wv', 'bv')}
    del _L0_attn_all

    def _L0_ffn_setup():
        import jax, jax.numpy as jnp
        import numpy as np
        B, S, D, E = (4, 512, 256, 8)
        key = jax.random.key(seed)
        ks = jax.random.split(key, 5)
        s = 0.02
        return {'hidden_states': jax.random.normal(ks[0], (B, S, D), dtype=jnp.float32), 'Wr': jax.random.normal(ks[1], (D, E), dtype=jnp.float32) * s, 'br': jnp.zeros((E,), dtype=jnp.float32), 'W1': jax.random.normal(ks[2], (E, D, 4 * D), dtype=jnp.float32) * s, 'b1': jnp.zeros((E, 4 * D), dtype=jnp.float32), 'W2': jax.random.normal(ks[3], (E, 4 * D, 2 * D), dtype=jnp.float32) * s, 'b2': jnp.zeros((E, 2 * D), dtype=jnp.float32), 'W3': jax.random.normal(ks[4], (E, 2 * D, D), dtype=jnp.float32) * s, 'b3': jnp.zeros((E, D), dtype=jnp.float32)}
    _L0_ffn_all = _L0_ffn_setup()
    _L0_ffn_in = {k: v for k, v in _L0_ffn_all.items() if k in ('Wr', 'br', 'W1', 'b1', 'W2', 'b2', 'W3', 'b3')}
    del _L0_ffn_all
    return {'x': x, 'ctx_768': ctx_768, 'mask_BxS2_bf1': mask_BxS2_bf1, 'L0_xattn_Wq': _L0_xattn_in['Wq'], 'L0_xattn_Wk': _L0_xattn_in['Wk'], 'L0_xattn_Wv': _L0_xattn_in['Wv'], 'L0_xattn_Wo': _L0_xattn_in['Wo'], 'L0_attn_Wq': _L0_attn_in['Wq'], 'L0_attn_bq': _L0_attn_in['bq'], 'L0_attn_Wk': _L0_attn_in['Wk'], 'L0_attn_bk': _L0_attn_in['bk'], 'L0_attn_Wv': _L0_attn_in['Wv'], 'L0_attn_bv': _L0_attn_in['bv'], 'L0_ffn_Wr': _L0_ffn_in['Wr'], 'L0_ffn_br': _L0_ffn_in['br'], 'L0_ffn_W1': _L0_ffn_in['W1'], 'L0_ffn_b1': _L0_ffn_in['b1'], 'L0_ffn_W2': _L0_ffn_in['W2'], 'L0_ffn_b2': _L0_ffn_in['b2'], 'L0_ffn_W3': _L0_ffn_in['W3'], 'L0_ffn_b3': _L0_ffn_in['b3']}

def reference(x, ctx_768, mask_BxS2_bf1, L0_xattn_Wq, L0_xattn_Wk, L0_xattn_Wv, L0_xattn_Wo, L0_attn_Wq, L0_attn_bq, L0_attn_Wk, L0_attn_bk, L0_attn_Wv, L0_attn_bv, L0_ffn_Wr, L0_ffn_br, L0_ffn_W1, L0_ffn_b1, L0_ffn_W2, L0_ffn_b2, L0_ffn_W3, L0_ffn_b3):
    import jax
    import jax.numpy as jnp

    def _L0_xattn_ref(x, context, context_mask, Wq, Wk, Wv, Wo):
        import jax, jax.numpy as jnp
        import numpy as np
        DIM = 256
        CTX_DIM = 192
        HEADS = 16
        B, N, _ = x.shape
        M = context.shape[1]
        hd = DIM // HEADS
        scale = hd ** (-0.5)
        q = (x @ Wq).reshape(B, N, HEADS, hd).transpose(0, 2, 1, 3)
        k = (context @ Wk).reshape(B, M, HEADS, hd).transpose(0, 2, 1, 3)
        v = (context @ Wv).reshape(B, M, HEADS, hd).transpose(0, 2, 1, 3)
        scores = jnp.einsum('bhid,bhjd->bhij', q, k) * scale
        max_neg = -jnp.finfo(scores.dtype).max
        scores = jnp.where(context_mask[:, None, None, :], scores, max_neg)
        attn = jax.nn.softmax(scores, axis=-1)
        out = jnp.einsum('bhij,bhjd->bhid', attn, v)
        out = out.transpose(0, 2, 1, 3).reshape(B, N, DIM)
        return out @ Wo

    def _L0_attn_ref(sequence_output, Wq, bq, Wk, bk, Wv, bv):
        import jax, jax.numpy as jnp
        import numpy as np
        H = 256
        W_CTX = 2

        def _local_attention(x, Wq, bq, Wk, bk, Wv, bv):
            B, S, Hd = x.shape
            Q = x @ Wq + bq
            K = x @ Wk + bk
            V = x @ Wv + bv
            w = W_CTX
            win = 2 * w + 1
            idx = jnp.arange(S)[:, None] + jnp.arange(-w, w + 1)[None, :]
            valid = (idx >= 0) & (idx < S)
            idx_c = jnp.clip(idx, 0, S - 1)
            Kw = K[:, idx_c]
            Vw = V[:, idx_c]
            scores = jnp.einsum('bsh,bswh->bsw', Q, Kw) / jnp.sqrt(jnp.float32(Hd))
            scores = jnp.where(valid[None], scores, -jnp.inf)
            probs = jax.nn.softmax(scores, axis=-1)
            return jnp.einsum('bsw,bswh->bsh', probs, Vw)
        return _local_attention(sequence_output, Wq, bq, Wk, bk, Wv, bv)

    def _L0_ffn_ref(hidden_states, Wr, br, W1, b1, W2, b2, W3, b3):
        import jax, jax.numpy as jnp
        import numpy as np
        B, S, D, E = (4, 512, 256, 8)
        b, s, d = hidden_states.shape
        num_experts = Wr.shape[1]
        x = hidden_states.reshape(-1, d)
        router_logits = x @ Wr + br
        expert_mask = jax.nn.one_hot(jnp.argmax(router_logits, axis=-1), num_experts, dtype=x.dtype)
        out = jnp.zeros_like(x)
        for e in range(num_experts):
            h = jax.nn.gelu(x @ W1[e] + b1[e], approximate=False)
            h = jax.nn.gelu(h @ W2[e] + b2[e], approximate=False)
            y = h @ W3[e] + b3[e]
            out = out + expert_mask[:, e:e + 1] * y
        return out.reshape(b, s, d)
    x = x + _L0_xattn_ref(_layernorm(x, axis=-1), ctx_768, mask_BxS2_bf1, L0_xattn_Wq, L0_xattn_Wk, L0_xattn_Wv, L0_xattn_Wo)
    x = x + _L0_attn_ref(_layernorm(x, axis=-1), L0_attn_Wq, L0_attn_bq, L0_attn_Wk, L0_attn_bk, L0_attn_Wv, L0_attn_bv)
    x = x + _L0_ffn_ref(_layernorm(x, axis=-1), L0_ffn_Wr, L0_ffn_br, L0_ffn_W1, L0_ffn_b1, L0_ffn_W2, L0_ffn_b2, L0_ffn_W3, L0_ffn_b3)
    return x

_drawn_inputs = setup_inputs


def setup_inputs(seed=0):
    import zlib

    import numpy as np

    out = dict(_drawn_inputs(seed))
    spreads = {'L0_ffn_br': (0.0, 0.1),
     'L0_ffn_b1': (0.0, 0.8),
     'L0_ffn_b2': (0.0, 0.406),
     'L0_ffn_b3': (0.0, 0.1)}
    factors = {'L0_attn_bq': 8.0, 'L0_attn_bk': 8.0, 'L0_ffn_W1': 2.69}
    for name, (base, spread) in spreads.items():
        noise = np.random.default_rng([zlib.crc32(name.encode()), seed]).standard_normal(out[name].shape)
        drawn = base * np.exp(spread * noise) if base else spread * noise
        out[name] = jnp.asarray(drawn.astype(out[name].dtype))
    for name, factor in factors.items():
        out[name] = (out[name] * factor).astype(out[name].dtype)
    return out
```

```python
from contextlib import ExitStack

import concourse.bass as bass
from concourse import mybir

F32 = mybir.dt.float32
F32R = mybir.dt.float32r
BF16 = mybir.dt.bfloat16
I32 = mybir.dt.int32
U8 = mybir.dt.uint8
ACT = mybir.ActivationFunctionType
ALU = mybir.AluOpType
AX = mybir.AxisListType

P = 128
EPS = 1e-5
MASKED = -1.0e30


def perceiver_kernel(nc, x, ctx_768, mask, Wq, Wk, Wv, Wo, lWq, lbq, lWk, lbk, lWv, lbv,
                     Wr, br, W1, b1, W2, b2, W3, b3, out):
    B, S, D = x.shape
    J, C = ctx_768.shape[1:]
    HEADS, HD = 16, D // 16
    GROUPS = HEADS * S // P
    HG = HEADS // GROUPS
    GC = HG * HD
    BT = P // S
    TILES = B * S // P
    C2 = C - P
    JM = J - 1
    E = Wr.shape[1]

    F1, F2 = W1.shape[2], W2.shape[2]
    SLOTS = (B * S + E * (P - 1)) // P
    ROW = 2 * D + 4
    ID = 2 * D
    N_TOKENS = B * S
    W_COLS = 2 * F1 + F1 // P * F2 + F2 // P * D
    W2_AT, W3_AT = 2 * F1, 2 * F1 + F1 // P * F2

    x_rows = x.rearrange("b s d -> (b s) d")
    out_rows = out.rearrange("b s d -> (b s) d")

    with ExitStack() as stack:
        def sb(name, shape, dt=F32):
            return stack.enter_context(nc.sbuf_tensor(name, shape, dt))

        def sem(name):
            return stack.enter_context(nc.semaphore(name))

        def bank(name):
            return stack.enter_context(nc.psum_tensor(name, [P, 512], F32))

        ps_ctx = bank("ps_ctx")
        ps_k = bank("ps_k")
        ps_v = bank("ps_v")
        ps_s = [bank("ps_s0"), bank("ps_s1")]
        ps_p = bank("ps_p")
        ps_o = bank("ps_o")
        ps_m = bank("ps_m")

        ident = sb("ident", [P, P])
        head_blocks = sb("head_blocks", [P, 8])
        head_mask = sb("head_mask", [P, HG])
        band = sb("band", [P, P])
        neg_half = sb("neg_half", [P, 1])
        wq = sb("wq", [P, 2, D])
        wo = sb("wo", [P, 2, D])
        lw = sb("lw", [P, 3, 2, D])
        wr = sb("wr", [P, 2, E])
        lbias = sb("lbias", [P, 4])
        bv_rows = sb("bv_rows", [P, D])
        br_rows = sb("br_rows", [P, E])
        wkv = sb("wkv", [P, 2, 2, D])
        wkv_hi = sb("wkv_hi", [P, 2, 2, D], F32R)
        wkv_lo = sb("wkv_lo", [P, 2, 2, D], F32R)

        last_ctx = sb("last_ctx", [B, C])
        last_ctxT = sb("last_ctxT", [P, 2, B])
        last_k = [sb("last_k_hi", [P, 2, B], F32R), sb("last_k_lo", [P, 2, B], F32R)]
        last_v_dram = nc.dram_tensor("last_v_dram", (B, GROUPS, D), F32, kind="Internal").ap()

        ctx_raw = sb("ctx_raw", [P, BT, 2, C])
        mask_raw = sb("mask_raw", [P, BT, J], U8)
        ctx_split = sb("ctx_split", [P, BT, 2, 3 * P], F32R)
        ctxT = sb("ctxT", [P, 3, 2 * P], F32R)
        kT = [sb("kT_hi", [P, 2, J + 1], F32R), sb("kT_lo", [P, 2, J + 1], F32R)]
        v = sb("v", [P, 2, 2, D])
        mask_add = sb("mask_add", [P, BT, J])
        xt = sb("xt", [P, D])
        xn1 = sb("xn1", [P, D])
        turned0 = sb("turned0", [P, 3 * P])
        q = [sb("q_hi", [P, 2, P], F32R), sb("q_lo", [P, 2, P], F32R)]
        qd = [sb("qd_hi", [P, BT, 2, P], F32R), sb("qd_lo", [P, BT, 2, P], F32R)]
        prob = sb("prob", [P, GROUPS, J])
        neg_max = sb("neg_max", [P, GROUPS])
        row_sum = sb("row_sum", [P, 2, GROUPS])
        row_inv = sb("row_inv", [P, GROUPS])
        probT = sb("probT", [P, 2, GROUPS * P])
        last_probT = sb("last_probT", [GROUPS, P])
        last_v_rows = sb("last_v_rows", [GROUPS, BT, D])
        attn = sb("attn", [P, D])

        attnT = sb("attnT", [P, 2, P])
        xr = sb("xr", [P, D])
        x2 = sb("x2", [P, D])
        xn2 = sb("xn2", [P, D])
        turned4 = sb("turned4", [P, 4 * P])
        lqk = sb("lqk", [P, 4, P])
        lv = sb("lv", [P, D])
        lprob = sb("lprob", [P, P])
        lneg_max = sb("lneg_max", [P, 1])
        lrow_sum = sb("lrow_sum", [P, 1])
        lrow_inv = sb("lrow_inv", [P, 1])
        x3n = sb("x3n", [P, 2 * D])
        rows = sb("rows", [P, TILES, ROW])
        logits = sb("logits", [P, E, TILES])
        stats = [sb(f"stats{i}", [P, 6]) for i in range(3)]
        moments = [sb(f"moments{i}", [P, 2]) for i in range(3)]
        var_eps = [sb(f"var_eps{i}", [P, 1]) for i in range(3)]
        rstd = [sb(f"rstd{i}", [P, 1]) for i in range(3)]

        fill_row = sb("fill_row", [P, ROW])
        before = sb("before", [P, P], BF16)
        ones_bf = sb("ones_bf", [P, P], BF16)
        expert_rank = sb("expert_rank", [P, E])
        slot_number = sb("slot_number", [P, SLOTS])
        restart = sb("restart", [P, E, TILES])
        ones_row = sb("ones_row", [P, E])
        top = sb("top", [P, TILES])
        tied = sb("tied", [P, E, TILES])
        first = sb("first", [P, TILES])
        chosen = sb("chosen", [P, E, TILES])
        chosen_bf = sb("chosen_bf", [P, E, TILES], BF16)
        tile_counts = sb("tile_counts", [P, E, TILES])
        counts = sb("counts", [P, E, TILES])
        padded = sb("padded", [P, E], I32)
        slots_int = sb("slots_int", [P, E], I32)
        slots = sb("slots", [P, E])
        slot_end = sb("slot_end", [P, E])
        slot_start = sb("slot_start", [P, E])
        place = sb("place", [P, E, TILES])
        target = sb("target", [P, TILES])
        target_int = sb("target_int", [P, TILES], I32)
        past = sb("past", [P, SLOTS, E])
        slot_expert = sb("slot_expert", [P, SLOTS])
        slot_expert_int = sb("slot_expert_int", [P, SLOTS], I32)
        slot_buffer_int = sb("slot_buffer_int", [P, SLOTS], I32)
        slot_end_int = sb("slot_end_int", [P, E], I32)
        sorted_dram = nc.dram_tensor("sorted_dram", ((SLOTS + 1) * P, ROW), F32, kind="Internal").ap()

        weights = sb("weights", [P, 2, W_COLS])
        bias_rows = sb("bias_rows", [E * (F1 + F2) // P, P])
        bias_cols = sb("bias_cols", [P, E * (F1 + F2) // P])
        b3_rows = sb("b3_rows", [P, E, D])
        slot_x = ctx_raw[:, :, :, :].rearrange("p b t c -> p (b t c)")[:, 0:2 * ROW].rearrange("p (s d) -> p s d", s=2)
        slot_xT = attnT
        z1 = prob[:, :, :].rearrange("p g j -> p (g j)")
        h1 = probT[:, :, :].rearrange("p t (f s) -> p (t f) s", s=P)
        z2 = turned4
        h2 = lqk
        residual = v[:, :, 0, :]
        y = v[:, :, 1, :]
        last_v = weights[0:B, 0, 0:GROUPS * D].rearrange("b (g d) -> b g d", g=GROUPS)
        ps_z1 = [ps_ctx, ps_k]
        ps_t1 = [ps_v, ps_s[0]]
        ps_z2, ps_t2, ps_y, ps_xT = ps_s[1], ps_p, ps_o, ps_m

        fill_done = sem("fill_done")
        filled = sem("filled")
        router_consts = sem("router_consts")
        route = sem("route")
        chosen_counted = sem("chosen_counted")
        scattered = sem("scattered")
        expert_in = sem("expert_in")
        expert_ready = sem("expert_ready")
        bias_in = sem("bias_in")
        bias_turned = sem("bias_turned")
        bias_done = sem("bias_done")
        slot_in = [sem(f"slot_in{i}") for i in range(2)]
        xT_filled = sem("xT_filled")
        xT_copied = sem("xT_copied")
        z1_filled = sem("z1_filled")
        z1_copied = [sem("z1_copied_dve"), sem("z1_copied_act")]
        t1_filled = sem("t1_filled")
        h1_done = sem("h1_done")
        z2_filled = sem("z2_filled")
        z2_copied = sem("z2_copied")
        t2_filled = sem("t2_filled")
        h2_done = sem("h2_done")
        residual_done = sem("residual_done")
        y_filled = sem("y_filled")
        y_done = sem("y_done")
        y_stored = [sem(f"y_stored{i}") for i in range(2)]
        w_in = sem("w_in")
        kv_in = sem("kv_in")
        consts = sem("consts")
        zeroed = sem("zeroed")
        wkv_split = sem("wkv_split")
        last_step = sem("last_step")
        last_copied = sem("last_copied")
        last_stored = sem("last_stored")
        x_in = sem("x_in")
        xr_in = sem("xr_in")
        ctx_in = [sem(f"ctx_in{i}") for i in range(BT)]
        lastv_in = [sem(f"lastv_in{i}") for i in range(BT)]
        split_hi = sem("split_hi")
        split_done = sem("split_done")
        mask_done = sem("mask_done")
        ctxT_filled = sem("ctxT_filled")
        ctxT_copied = sem("ctxT_copied")
        k_filled = sem("k_filled")
        k_hi_done = sem("k_hi_done")
        k_lo_done = sem("k_lo_done")
        k_last_done = sem("k_last_done")
        v_filled = sem("v_filled")
        v_copied = sem("v_copied")
        q_hi_done = sem("q_hi_done")
        qd_done = sem("qd_done")
        s_filled = sem("s_filled")
        s_masked = sem("s_masked")
        exp_done = sem("exp_done")
        lastp_filled = sem("lastp_filled")
        p_filled = sem("p_filled")
        p_copied = sem("p_copied")
        o_filled = sem("o_filled")
        inv_done = sem("inv_done")
        o_done = sem("o_done")
        m_filled = sem("m_filled")
        m_emptied = sem("m_emptied")
        xn1_done = sem("xn1_done")
        xn2_done = sem("xn2_done")
        xn3_done = sem("xn3_done")
        rows_done = sem("rows_done")
        linv_done = sem("linv_done")
        lexp_done = sem("lexp_done")
        ln_stats = [sem(f"ln_stats{i}") for i in range(3)]
        ln_moments = [sem(f"ln_moments{i}") for i in range(3)]
        ln_eps = [sem(f"ln_eps{i}") for i in range(3)]
        ln_rstd = [sem(f"ln_rstd{i}") for i in range(3)]
        waits_ended = sem("waits_ended")
        out_stored = sem("out_stored")

        def alone(eng):
            eng.sem_inc(waits_ended, 1)

        def turn(T, e):
            if isinstance(T, int) and T < 1:
                return 2 * (T + 1) + {0: 0, 2: 1}[e]
            if isinstance(T, int) and T == TILES + 1:
                return 8 * T - 4 + e // 2
            return 8 * T - 4 + e

        def parts(T):
            if not isinstance(T, int):
                return True, True, True
            return T + 1 < TILES, 1 <= T <= TILES, 2 <= T <= TILES + 1

        def over_tiles(eng, iteration):
            for T in (-1, 0, 1):
                iteration(T)
            with eng.Fori(2, TILES - 1) as T:
                iteration(T)
            for T in (TILES - 1, TILES, TILES + 1):
                iteration(T)

        def in_tiles(T):
            return not isinstance(T, int) or 0 <= T < TILES

        def exists(T, k):
            return not isinstance(T, int) or 0 <= BT * T + k < B

        def over_slots(eng, step):
            for p in range(2):
                step(p, 0, p, True)
            with eng.Fori(1, SLOTS // 2) as pair:
                for p in range(2):
                    step(2 * pair + p, pair, p, True)
            for i in range(SLOTS // 2 * 2, SLOTS):
                step(i, i // 2, i % 2, i + 1 < SLOTS)

        assert SLOTS % 2 == 1
        ROUTED = 22
        block = stack.enter_context(nc.Block())

        @block.sync
        def _(sp):
            def load_ctx(T, b):
                n = BT * T + b
                sp.dma_start(ctx_raw[:, b, :, :], ctx_768[n, 0:JM, :].rearrange("(p t) c -> p t c", t=2)).then_inc(ctx_in[b], 16)
                sp.dma_start(mask_raw[:, b, :], bcast(mask, n)).then_inc(ctx_in[b], 16)

            def bcast(m, n):
                return m[bass.ds(n, 1), :].to_broadcast([P, J])

            def load_last_v(T, b):
                sp.dma_start(last_v_rows[:, b, :], last_v_dram[BT * T + b]).then_inc(lastv_in[b], 16)

            def load_x(dst, T, s):
                sp.dma_start(dst[:, :], x_rows.rearrange("(t p) d -> t p d", p=P)[T]).then_inc(s, 16)

            load_x(xt, 0, x_in)
            sp.dma_start(last_ctx[:, :], ctx_768[:, JM, :]).then_inc(kv_in, 16)
            for i, w in enumerate((Wk, Wv)):
                sp.dma_start(wkv[:, i, 0, :], w[0:P, :]).then_inc(kv_in, 16)
                sp.dma_start(wkv[0:C2, i, 1, :], w[P:C, :]).then_inc(kv_in, 16)
                sp.dma_start(wkv[C2:P, i, 1, :], w[P:C, :]).then_inc(kv_in, 16)
            for b in range(BT):
                load_ctx(0, b)
            sp.dma_start(bias_rows[0:E * F1 // P, :], b1.rearrange("e (c p) -> (e c) p", p=P)).then_inc(bias_in, 16)
            sp.dma_start(bias_rows[E * F1 // P:, :], b2.rearrange("e (c p) -> (e c) p", p=P)).then_inc(bias_in, 16)
            sp.dma_start(b3_rows[:, :, :].rearrange("p e d -> p (e d)"),
                         b3.rearrange("(o e) d -> o (e d)", o=1).to_broadcast([P, E * D])).then_inc(bias_in, 16)
            for dst, w in ((wq, Wq), (wo, Wo), (wr, Wr)):
                sp.dma_start(dst[:, :, :], w.rearrange("(c p) n -> p c n", p=P)).then_inc(w_in, 16)
            for i, w in enumerate((lWq, lWk, lWv)):
                sp.dma_start(lw[:, i, :, :], w.rearrange("(c p) n -> p c n", p=P)).then_inc(w_in, 16)
            for i, w in enumerate((lbq, lbk)):
                sp.dma_start(lbias[:, 2 * i:2 * i + 2], w.rearrange("(c p) -> p c", p=P), allow_slow_non_contiguous=True).then_inc(w_in, 16)
            sp.dma_start(bv_rows[:, :], lbv.rearrange("(o n) -> o n", o=1).to_broadcast([P, D])).then_inc(w_in, 16)
            sp.dma_start(br_rows[:, :], br.rearrange("(o n) -> o n", o=1).to_broadcast([P, E])).then_inc(w_in, 16)

            sp.wait_ge(fill_done, 2)
            for i in range(SLOTS + 1):
                sp.dma_start(sorted_dram[i * P:(i + 1) * P, :], fill_row[:, :]).then_inc(filled, 16)

            def ahead(T):
                sp.wait_ge(xn1_done, T)
                load_x(xt, T, x_in)
                for b in range(BT):
                    n = BT * (T - 1) + b
                    sp.wait_ge(split_done, n + 1)
                    sp.wait_ge(mask_done, n + 1)
                    load_ctx(T, b)
                    if isinstance(T, int) and T == 1:
                        if b == 0:
                            sp.wait_ge(last_copied, 5)
                            sp.dma_start(last_v_dram, last_v[:, :, :]).then_inc(last_stored, 16)
                            sp.wait_ge(last_stored, 16)
                    else:
                        sp.wait_ge(o_filled, BT * (T - 2) + b + 1)
                    load_last_v(T - 1, b)
                    if b == 1 and not (isinstance(T, int) and T == 1):
                        sp.wait_ge(m_emptied, turn(T - 2, 3) + 1)
                        load_x(xr, T - 2, xr_in)
            ahead(1)
            with sp.Fori(2, TILES) as T:
                ahead(T)
            for b in range(BT):
                sp.wait_ge(o_filled, BT * (TILES - 2) + b + 1)
                load_last_v(TILES - 1, b)
            for T in (TILES - 2, TILES - 1):
                sp.wait_ge(m_emptied, turn(T, 3) + 1)
                load_x(xr, T, xr_in)

            def load_expert(e, p, used):
                for w, at, n in ((W1, 0, F1), (W2, W2_AT, F2), (W3, W3_AT, D)):
                    k = w.shape[1] // P
                    sp.dma_start(weights[:, p, at:at + k * n].rearrange("p (k n) -> p k n", k=k),
                                 w[e].rearrange("(k p) n -> p k n", p=P)).then_inc(expert_in, 16)
                sp.wait_ge(expert_in, 48 * (e + 1))
                sp.sem_inc(expert_ready, 1)
            for e in range(2):
                load_expert(e, e, 0)
            sp.wait_ge(route, ROUTED)
            with sp.Fori(1, E // 2) as pair:
                for p in range(2):
                    last_slot = sp.value_load(slot_end_int[0:1, bass.ds(2 * pair + p - 2, 1)], min_val=0, max_val=SLOTS)
                    sp.wait_ge(y_filled, last_slot)
                    load_expert(2 * pair + p, p, pair)
            for p in range(2):
                sp.wait_ge(y_stored[p], 16 * ((SLOTS + 1 - p) // 2))

        @block.gpsimd
        def _(pool):
            g = nc.gpsimd
            g.memset(ident[:, :], 0.0).then_inc(zeroed, 1)
            g.memset(head_blocks[:, :], 1.0).then_inc(zeroed, 1)
            g.memset(band[:, :], 0.0).then_inc(zeroed, 1)
            g.memset(neg_half[:, :], -0.5).then_inc(consts, 1)
            for i in range(2):
                g.memset(kT[i][:, :, JM:J + 1].bitcast(F32), 0.0).then_inc(consts, 1)
            pool.wait_ge(zeroed, 3)
            g.affine_select(out=ident[:, :], in_=ident[:, :], compare_op=ALU.not_equal, fill=1.0, base=0,
                            pattern=[[-1, P]], channel_multiplier=1).then_inc(consts, 1)
            g.affine_select(out=head_blocks[:, :], in_=head_blocks[:, :], compare_op=ALU.is_ge, fill=0.0, base=0,
                            pattern=[[-HD, 8]], channel_multiplier=1).then_inc(zeroed, 1)
            pool.wait_ge(zeroed, 4)
            g.affine_select(out=head_blocks[:, :], in_=head_blocks[:, :], compare_op=ALU.is_ge, fill=0.0, base=HD - 1,
                            pattern=[[HD, 8]], channel_multiplier=-1).then_inc(zeroed, 1)
            pool.wait_ge(zeroed, 5)
            g.tensor_tensor(head_mask[:, :], head_blocks[:, 0:HG], head_blocks[:, HG:2 * HG], ALU.add).then_inc(consts, 1)
            n = 5
            for base, mult, pattern in ((2, 1, [[-1, P]]), (2, -1, [[1, P]]),
                                        (0, 1, [[-S, BT], [0, S]]), (S - 1, -1, [[S, BT], [0, S]])):
                view = band[:, :] if len(pattern) == 1 else band[:, :].rearrange("p (a b) -> p a b", b=S)
                g.affine_select(out=view, in_=view, compare_op=ALU.is_ge, fill=MASKED, base=base,
                                pattern=pattern, channel_multiplier=mult).then_inc(zeroed, 1)
                n += 1
                pool.wait_ge(zeroed, n)
            g.memset(last_v[:, :, :], 0.0).then_inc(consts, 1)
            pool.wait_ge(kv_in, 16 * 7)
            g.tensor_copy(wkv_hi[:, :, :, :], wkv[:, :, :, :]).then_inc(wkv_split, 1)
            pool.wait_ge(wkv_split, 1)
            g.tensor_tensor(wkv_lo[:, :, :, :], wkv[:, :, :, :], wkv_hi[:, :, :, :].bitcast(F32), ALU.subtract).then_inc(wkv_split, 1)

            g.memset(fill_row[:, 0:ID], 0.0).then_inc(fill_done, 1)
            g.memset(fill_row[:, ID:ROW].bitcast(I32), 2 * N_TOKENS).then_inc(fill_done, 1)
            g.iota(expert_rank[:, :], pattern=[[-1, E]], base=E, channel_multiplier=0,
                   allow_small_or_imprecise_dtypes=True).then_inc(router_consts, 1)
            g.iota(slot_number[:, :], pattern=[[1, SLOTS]], base=0, channel_multiplier=0,
                   allow_small_or_imprecise_dtypes=True).then_inc(router_consts, 1)
            g.memset(ones_row[:, :], 1.0).then_inc(router_consts, 1)
            g.memset(ones_bf[:, :], 1.0).then_inc(router_consts, 1)
            g.memset(restart[:, :, 0:1], 0.0).then_inc(router_consts, 1)
            g.memset(restart[:, :, 1:TILES], 1.0).then_inc(router_consts, 1)
            pool.wait_ge(router_consts, 6)
            g.affine_select(out=before[:, :], in_=ones_bf[:, :], compare_op=ALU.is_gt, fill=0.0, base=0,
                            pattern=[[1, P]], channel_multiplier=-1).then_inc(router_consts, 1)
            g.iota(rows[:, :, ID:ROW].bitcast(I32), pattern=[[P, TILES], [0, ROW - ID]], base=0,
                   channel_multiplier=1).then_inc(router_consts, 1)

            def split_ctx(T, b):
                n = BT * T + b
                pool.wait_ge(ctx_in[b], 32 * (T + 1))
                alone(pool)
                hi = ctx_split[:, b, :, 0:C]
                g.tensor_copy(hi, ctx_raw[:, b, :, :]).then_inc(split_hi, 1)
                pool.wait_ge(split_hi, n + 1)
                g.tensor_tensor(ctx_split[:, b, :, C:2 * P], ctx_raw[:, b, :, P:C],
                                ctx_split[:, b, :, P:C].bitcast(F32), ALU.subtract)
                g.tensor_tensor(ctx_split[:, b, :, 2 * P:3 * P], ctx_raw[:, b, :, 0:P],
                                ctx_split[:, b, :, 0:P].bitcast(F32), ALU.subtract).then_inc(split_done, 1)

            def mask_rows(T, b):
                g.tensor_scalar(mask_add[:, b, 0:JM].rearrange("p (t m) -> p t m", t=2),
                                mask_raw[:, b, 0:JM].rearrange("p (m t) -> p t m", t=2),
                                1.0, -MASKED, ALU.subtract, ALU.mult)
                g.tensor_scalar(mask_add[:, b, JM:J], mask_raw[:, b, JM:J], 1.0, -MASKED,
                                ALU.subtract, ALU.mult).then_inc(mask_done, 1)

            def place_queries(b):
                for i in range(2):
                    last = g.tensor_tensor(
                        qd[i][:, b, :, :].rearrange("p c (h s) -> p c h s", h=HG),
                        q[i][:, :, b * S:(b + 1) * S].bitcast(F32).unsqueeze(2).to_broadcast([P, 2, HG, S]),
                        head_mask[:, :].unsqueeze(1).unsqueeze(3).to_broadcast([P, 2, HG, S]), ALU.mult)
                last.then_inc(qd_done, 1)

            def scale_of(i, t):
                pool.wait_ge(ln_moments[i], t + 1)
                alone(pool)
                g.tensor_scalar(var_eps[i][:, :], moments[i][:, 1:2], EPS, None, ALU.add).then_inc(ln_eps[i], 1)
                pool.wait_ge(ln_eps[i], t + 1)
                g.tensor_tensor(rstd[i][:, :], var_eps[i][:, :], neg_half[:, :], ALU.pow).then_inc(ln_rstd[i], 1)

            def normalise(i, t, src, dst, done):
                scale_of(i, t)
                pool.wait_ge(ln_rstd[i], t + 1)
                alone(pool)
                g.tensor_scalar(dst[:, :], src[:, :], moments[i][:, 0:1], rstd[i][:, 0:1],
                                ALU.subtract, ALU.mult).then_inc(done, 1)

            def iteration(T):
                has_q, has_out, has_local = parts(T)
                if isinstance(T, int) and T < 0:
                    for b in range(BT):
                        split_ctx(0, b)
                        mask_rows(0, b)
                    pool.wait_ge(last_copied, 4)
                    for i in range(2):
                        last = g.tensor_copy(kT[i][:, :, JM:J], last_k[i][:, :, 0:1])
                    last.then_inc(k_last_done, 1)
                for k in range(BT):
                    n = BT * T + k
                    if k == 0 and has_q:
                        normalise(0, T + 1, xt, xn1, xn1_done)
                    if k == 2 and has_out:
                        normalise(1, T - 1, x2, xn2, xn2_done)
                    if in_tiles(T) and exists(T, k + 1):
                        pool.wait_ge(s_filled, 2 * n + 2)
                        alone(pool)
                        for i in range(2):
                            last = g.tensor_copy(kT[i][:, :, JM:J], last_k[i][:, :, bass.ds(n + 1, 1)])
                        last.then_inc(k_last_done, 1)
                    if k == 1 and has_local:
                        scale_of(2, T - 2)
                    if k == 2 and has_local:
                        pool.wait_ge(xn3_done, T - 1)
                        alone(pool)
                        g.tensor_copy(rows[:, bass.ds(T - 2, 1), 0:2 * D].rearrange("p o d -> p (o d)"), x3n[:, :]).then_inc(rows_done, 1)
                    if has_q and k >= 1:
                        if k == 1:
                            pool.wait_ge(m_emptied, turn(T, 2) + 1)
                        for b in range(0 if k == 1 else k, k + 1):
                            if in_tiles(T):
                                pool.wait_ge(s_filled, 2 * (BT * T + b) + 2)
                            place_queries(b)
                    if in_tiles(T) and has_q:
                        split_ctx(T + 1, k)
                        pool.wait_ge(s_masked, GROUPS * (n + 1))
                        alone(pool)
                        mask_rows(T + 1, k)

            over_tiles(pool, iteration)

            pool.wait_ge(rows_done, TILES)
            pool.wait_ge(filled, 16 * (SLOTS + 1))
            pool.wait_ge(route, ROUTED)
            for T in range(TILES):
                g.indirect_dma_start(out=sorted_dram, out_offset=bass.IndirectOffsetOnAxis(ap=target_int[:, T:T + 1], axis=0),
                                     in_=rows[:, T, :], in_offset=None,
                                     bounds_check=SLOTS * P - 1, oob_is_err=False).then_inc(scattered, 16)

            pool.wait_ge(bias_in, 48)

            def add_bias(i, pair, p):
                pool.wait_ge(slot_in[p], 16 * (pair + 1))
                alone(pool)
                e = pool.value_load(slot_expert_int[0:1, bass.ds(i, 1)], min_val=0, max_val=E - 1)
                g.tensor_tensor(residual[:, p, :], slot_x[:, p, 0:D], b3_rows[:, bass.ds(e, 1), :].rearrange("p o d -> p (o d)"),
                                ALU.add).then_inc(residual_done, 1)

            def slot(i, pair, p, follows):
                add_bias(i, pair, p)
                pool.wait_ge(y_done, i + 1)
                alone(pool)
                g.indirect_dma_start(out=out_rows, out_offset=bass.IndirectOffsetOnAxis(ap=slot_x[:, p, ID:ID + 1].bitcast(I32), axis=0),
                                     in_=y[:, p, :], in_offset=None, bounds_check=N_TOKENS - 1, oob_is_err=False).then_inc(y_stored[p], 16)

            over_slots(pool, slot)

        @block.scalar
        def _(act):
            a = nc.scalar

            def copy_ctxT(n, jt):
                act.wait_ge(ctxT_filled, 2 * n + jt + 1)
                a.copy(ctxT[:, :, jt * P:(jt + 1) * P], ps_ctx[:, 0:3 * P].rearrange("p (c j) -> p c j", c=3)).then_inc(ctxT_copied, 1)

            def exponentials(n, k, half):
                for g in (2 * half, 2 * half + 1):
                    act.wait_ge(s_masked, GROUPS * n + g + 1)
                    last = a.activation(prob[:, g, :], prob[:, g, :], ACT.Exp, bias=neg_max[:, g:g + 1], scale=-1.0,
                                        accum_out=row_sum[:, k % 2, g:g + 1])
                    last.then_inc(exp_done, 1)

            def copy_k(n):
                act.wait_ge(k_filled, n + 1)
                a.copy(kT[0][:, :, 0:JM], ps_k[:, :].rearrange("p (c j) -> p c j", c=2)).then_inc(k_hi_done, 1)

            def copy_v(n, k):
                act.wait_ge(v_filled, n + 1)
                a.copy(v[:, k % 2, :, :].rearrange("p t d -> p (t d)"), ps_v[:, :]).then_inc(v_copied, 1)

            def middle(T, k):
                has_q, has_out, has_local = parts(T)
                if k == 1 and has_q:
                    act.wait_ge(m_filled, turn(T, 2) + 1)
                    if not (isinstance(T, int) and T < 0):
                        act.wait_ge(qd_done, BT * (T + 1))
                    a.copy(q[0][:, :, :].rearrange("p c s -> p (c s)"), ps_m[:, 0:2 * P]).then_inc(q_hi_done, 1)
                if k == 2 and (has_out or has_local):
                    act.wait_ge(m_filled, turn(T, 4) + 1)
                    lo, hi = (0 if has_out else 2 * P), (4 * P if has_local else 2 * P)
                    a.copy(turned4[:, lo:hi], ps_m[:, lo:hi]).then_inc(m_emptied, 1)

            def end(T, k):
                has_q, has_out, has_local = parts(T)
                if k == 0 and has_out:
                    act.wait_ge(m_filled, turn(T, 1) + 1)
                    a.copy(attnT[:, :, :].rearrange("p c s -> p (c s)"), ps_m[:, 0:2 * P]).then_inc(m_emptied, 1)
                if k == 3 and has_out:
                    act.wait_ge(m_emptied, turn(T, 7) + 1)
                    a.activation(lprob[:, :], lprob[:, :], ACT.Exp, bias=lneg_max[:, 0:1], scale=-1.0,
                                 accum_out=lrow_sum[:, 0:1]).then_inc(lexp_done, 1)

            def iteration(T):
                if isinstance(T, int) and T < 0:
                    copy_ctxT(0, 0)
                    copy_ctxT(0, 1)
                    copy_k(0)
                    copy_v(0, 0)
                for k in range(BT):
                    n = BT * T + k
                    ahead = in_tiles(T) and exists(T, k + 1)
                    if ahead:
                        copy_ctxT(n + 1, 0)
                    if in_tiles(T):
                        exponentials(n, k, 0)
                    if ahead:
                        copy_ctxT(n + 1, 1)
                    if in_tiles(T):
                        exponentials(n, k, 1)
                    if ahead:
                        copy_k(n + 1)
                    middle(T, k)
                    if ahead:
                        copy_v(n + 1, k + 1)
                    end(T, k)

            over_tiles(act, iteration)

            def load_slot(i, pair, p):
                act.dma_start(slot_x[:, p, :], sorted_dram.rearrange("(s p) d -> s p d", p=P)[i]).then_inc(slot_in[p], 16)

            def first_layer(i, e):
                for half in range(2):
                    act.wait_ge(t1_filled, 2 * i + half + 1)
                    alone(act)
                    for c in range(4):
                        f = 4 * half + c
                        last = a.activation(h1[:, f, :], ps_t1[half][:, c * P:(c + 1) * P], ACT.Gelu,
                                            bias=bias_cols[:, bass.ds(e * (F1 // P) + f, 1)])
                    last.then_inc(h1_done, 1)

            def second_layer(i, e):
                act.wait_ge(t2_filled, i + 1)
                alone(act)
                for c in range(F2 // P):
                    last = a.activation(h2[:, c, :], ps_t2[:, c * P:(c + 1) * P], ACT.Gelu,
                                        bias=bias_cols[:, bass.ds(e * (F2 // P) + E * F1 // P + c, 1)])
                last.then_inc(h2_done, 1)

            def copy_z1(i):
                act.wait_ge(z1_filled, 2 * i + 2)
                a.copy(z1[:, F1 // 2:F1], ps_z1[1][:, :]).then_inc(z1_copied[1], 1)

            def expert_of(i):
                return act.value_load(slot_expert_int[0:1, bass.ds(i, 1)], min_val=0, max_val=E - 1)

            act.wait_ge(bias_turned, 1)
            a.copy(bias_cols[:, :], ps_p[:, 0:E * (F1 + F2) // P]).then_inc(bias_done, 1)
            act.wait_ge(bias_done, 1)
            act.wait_ge(scattered, 16 * TILES)
            act.wait_ge(route, ROUTED)
            load_slot(0, 0, 0)
            load_slot(1, 0, 1)
            copy_z1(0)
            first_layer(0, expert_of(0))

            def slot(i, pair, p, follows):
                if follows:
                    copy_z1(i + 1)
                second_layer(i, expert_of(i))
                if follows:
                    first_layer(i + 1, expert_of(i + 1))
                if not isinstance(i, int) or i < 2:
                    act.wait_ge(y_stored[p], 16 * (pair + 1))
                    load_slot(i + 2, pair + 1, p)

            over_slots(act, slot)
            act.wait_ge(slot_in[1], 16 * (SLOTS // 2 + 1))

        @block.vector
        def _(dve):
            d = nc.vector

            def f32(ap):
                return ap.bitcast(F32)

            dve.wait_ge(last_step, 1)
            d.tensor_copy(last_ctxT[:, 0, :], ps_m[:, 0:B]).then_inc(last_copied, 1)
            d.tensor_copy(last_ctxT[0:C2, 1, :], ps_m[0:C2, B:2 * B]).then_inc(last_copied, 1)
            dve.wait_ge(last_step, 2)
            d.tensor_copy(last_k[0][:, :, :], ps_k[:, 0:2 * B].rearrange("p (c b) -> p c b", c=2)).then_inc(last_copied, 1)
            dve.wait_ge(last_copied, 3)
            d.tensor_tensor(last_k[1][:, :, :], ps_k[:, 0:2 * B].rearrange("p (c b) -> p c b", c=2), f32(last_k[0][:, :, :]),
                            ALU.subtract).then_inc(last_copied, 1)
            dve.wait_ge(consts, 6)
            for g in range(GROUPS):
                last = d.tensor_copy(last_v[:, g, g * GC:(g + 1) * GC], ps_v[0:B, g * GC:(g + 1) * GC])
            last.then_inc(last_copied, 1)

            def moments_of(i, t, src):
                d.bn_stats(stats[i][:, :], src).then_inc(ln_stats[i], 1)
                dve.wait_ge(ln_stats[i], t + 1)
                alone(dve)
                d.bn_aggr(moments[i][:, :], stats[i][:, :]).then_inc(ln_moments[i], 1)

            def mask_scores(n, k, half):
                dve.wait_ge(s_filled, 2 * n + half + 1)
                if half == 0:
                    dve.wait_ge(mask_done, n + 1)
                alone(dve)
                for r in range(2):
                    g = 2 * half + r
                    d.tensor_tensor_reduce(prob[:, g, :], ps_s[r][:, 0:J], mask_add[:, k, :], -(HD ** -0.5), 3.0e38,
                                           ALU.add, ALU.min, neg_max[:, g:g + 1]).then_inc(s_masked, 1)

            def finish_batch(T, k):
                n = BT * T + k
                dve.wait_ge(exp_done, GROUPS * (n + 1))
                d.reciprocal(row_inv[:, :], row_sum[:, k % 2, :]).then_inc(inv_done, 1)
                dve.wait_ge(inv_done, n + 1)
                dve.wait_ge(o_filled, n + 1)
                if k == 0 and not (isinstance(T, int) and T < 1):
                    dve.wait_ge(m_filled, turn(T, 1) + 1)
                for h in range(HG):
                    p0 = h * S
                    last = d.tensor_tensor(
                        attn[k * S:(k + 1) * S, :].rearrange("p (g h e) -> p g h e", g=GROUPS, h=HG)[:, :, h, :],
                        ps_o[p0:p0 + S, 0:D].rearrange("p (g h e) -> p g h e", g=GROUPS, h=HG)[:, :, h, :],
                        row_inv[p0:p0 + S, :].unsqueeze(2).to_broadcast([S, GROUPS, HD]), ALU.mult)
                last.then_inc(o_done, 1)

            def copy_probT(n):
                dve.wait_ge(lastp_filled, n + 1)
                d.tensor_copy(last_probT[:, :], ps_o[0:GROUPS, D:D + P])
                for jt in range(2):
                    dve.wait_ge(p_filled, 2 * n + jt + 1)
                    d.tensor_copy(probT[:, jt, :], ps_p[:, :]).then_inc(p_copied, 1)

            def middle(T, k):
                has_q, has_out, has_local = parts(T)
                if k == 0 and (has_q or has_local):
                    dve.wait_ge(m_filled, turn(T, 0) + 1)
                    lo, hi = (0 if has_q else 2 * P), (3 * P if has_local else 2 * P)
                    d.tensor_copy(turned0[:, lo:hi], ps_m[:, lo:hi]).then_inc(m_emptied, 1)
                if k == 1 and (has_q or has_local):
                    dve.wait_ge(m_filled, turn(T, 2) + 1)
                    if has_q:
                        dve.wait_ge(q_hi_done, T + 2)
                        last = d.tensor_tensor(q[1][:, :, :].rearrange("p c s -> p (c s)"), ps_m[:, 0:2 * P],
                                               f32(q[0][:, :, :].rearrange("p c s -> p (c s)")), ALU.subtract)
                        if not has_local:
                            last.then_inc(m_emptied, 1)
                    if has_local:
                        t = T - 2
                        dve.wait_ge(lexp_done, t + 1)
                        d.reciprocal(lrow_inv[:, :], lrow_sum[:, :]).then_inc(linv_done, 1)
                        dve.wait_ge(linv_done, t + 1)
                        x3 = x3n[:, 0:D]
                        dve.wait_ge(rows_done, t)
                        d.scalar_tensor_tensor(out=x3, in0=ps_m[:, 2 * P:4 * P], scalar=lrow_inv[:, 0:1], in1=x2[:, :],
                                               op0=ALU.mult, op1=ALU.add).then_inc(m_emptied, 1)
                        dve.wait_ge(m_emptied, turn(T, 2) + 1)
                        d.bn_stats(stats[2][:, :], x3).then_inc(ln_stats[2], 1)
                        dve.wait_ge(ln_stats[2], t + 1)
                        alone(dve)
                        d.bn_aggr(moments[2][:, :], stats[2][:, :]).then_inc(ln_moments[2], 1)
                if k == 3 and (has_out or has_local):
                    dve.wait_ge(m_filled, turn(T, 6) + 1)
                    if has_out:
                        last = d.tensor_tensor(lv[:, :], ps_m[:, 0:D], bv_rows[:, :], ALU.add)
                    if has_local:
                        last = d.tensor_tensor(logits[:, :, bass.ds(T - 2, 1)].rearrange("p e o -> p (e o)"), ps_m[:, D:D + E],
                                               br_rows[:, :], ALU.add)
                    last.then_inc(m_emptied, 1)

            def end(T, k):
                has_q, has_out, has_local = parts(T)
                if k == 1 and has_local:
                    dve.wait_ge(ln_rstd[2], T - 1)
                    d.tensor_scalar(x3n[:, D:2 * D], x3n[:, 0:D], moments[2][:, 0:1], rstd[2][:, 0:1], ALU.subtract, ALU.mult).then_inc(xn3_done, 1)
                if k == 1 and has_out:
                    t = T - 1
                    dve.wait_ge(m_filled, turn(T, 3) + 1)
                    dve.wait_ge(xr_in, 16 * (t + 1))
                    d.tensor_tensor(x2[:, :], ps_m[:, 0:D], xr[:, :], ALU.add).then_inc(m_emptied, 1)
                    dve.wait_ge(m_emptied, turn(T, 3) + 1)
                    moments_of(1, t, x2[:, :])
                if k == 2 and has_out:
                    if isinstance(T, int) and T == 1:
                        dve.wait_ge(w_in, 16 * 10)
                    dve.wait_ge(m_filled, turn(T, 5) + 1)
                    d.tensor_tensor(lqk[:, :, :], ps_m[:, :].rearrange("p (w s) -> p w s", w=4),
                                    lbias[:, :].unsqueeze(2).to_broadcast([P, 4, P]), ALU.add).then_inc(m_emptied, 1)
                if k == 3 and has_out:
                    dve.wait_ge(m_filled, turn(T, 7) + 1)
                    alone(dve)
                    d.tensor_tensor_reduce(lprob[:, :], ps_m[:, 0:P], band[:, :], -(D ** -0.5), 3.0e38,
                                           ALU.add, ALU.min, lneg_max[:, 0:1]).then_inc(m_emptied, 1)

            def lo_keys(n):
                dve.wait_ge(k_hi_done, n + 1)
                d.tensor_tensor(kT[1][:, :, 0:JM], ps_k[:, :].rearrange("p (c j) -> p c j", c=2), f32(kT[0][:, :, 0:JM]),
                                ALU.subtract).then_inc(k_lo_done, 1)

            def iteration(T):
                has_q, has_out, has_local = parts(T)
                first = isinstance(T, int) and T < 0
                if first:
                    lo_keys(0)
                for k in range(BT):
                    n = BT * T + k
                    if k == 0 and has_q:
                        dve.wait_ge(x_in, 16 * (T + 2))
                        moments_of(0, T + 1, xt[:, :])
                    if in_tiles(T):
                        mask_scores(n, k, 0)
                    if not first and exists(T, k - 1) and not (isinstance(T, int) and BT * T + k > B):
                        finish_batch(T if k else T - 1, (k - 1) % BT)
                    if in_tiles(T):
                        mask_scores(n, k, 1)
                        if exists(T, k + 1):
                            lo_keys(n + 1)
                    middle(T, k)
                    if in_tiles(T):
                        copy_probT(n)
                    end(T, k)

            over_tiles(dve, iteration)

            steps = [0]

            def then(ins):
                steps[0] += 1
                ins.then_inc(route, 1)
                dve.wait_ge(route, steps[0])

            def by_tile(ap):
                return ap.rearrange("p e t -> p t e")

            def over_experts(ap):
                return ap.unsqueeze(1).to_broadcast([P, E, TILES])

            def over_all_tiles(ap):
                return ap.unsqueeze(2).to_broadcast([P, E, TILES])

            dve.wait_ge(router_consts, 8)
            dve.wait_ge(m_emptied, turn(TILES + 1, 6) + 1)
            then(d.tensor_reduce(top[:, :], by_tile(logits[:, :, :]), AX.X, ALU.max))
            then(d.tensor_tensor(tied[:, :, :], logits[:, :, :], over_experts(top[:, :]), ALU.is_ge))
            then(d.tensor_tensor(tied[:, :, :], tied[:, :, :], over_all_tiles(expert_rank[:, :]), ALU.mult))
            then(d.tensor_reduce(first[:, :], by_tile(tied[:, :, :]), AX.X, ALU.max))
            then(d.tensor_tensor(chosen[:, :, :], tied[:, :, :], over_experts(first[:, :]), ALU.is_equal))
            then(d.tensor_copy(chosen_bf[:, :, :], chosen[:, :, :]))
            dve.wait_ge(chosen_counted, 1)
            n_et = E * TILES
            earlier = ps_m[:, 0:n_et].rearrange("p (e t) -> p e t", e=E)
            then(d.tensor_copy(tile_counts[:, :, :], ps_m[:, n_et:2 * n_et].rearrange("p (e t) -> p e t", e=E)))
            flat = lambda ap: ap.rearrange("p e t -> p (e t)")
            then(d.tensor_tensor_scan(flat(counts[:, :, :]), flat(restart[:, :, :]), flat(tile_counts[:, :, :]), 0.0, ALU.mult, ALU.add))
            then(d.tensor_scalar(padded[:, :], counts[:, :, TILES - 1:TILES].rearrange("p e o -> p (e o)"), 1.0, float(P - 1), ALU.max, ALU.add))
            then(d.tensor_scalar(slots_int[:, :], padded[:, :], 7, None, ALU.logical_shift_right))
            then(d.tensor_copy(slots[:, :], slots_int[:, :]))
            then(d.tensor_tensor_scan(slot_end[:, :], ones_row[:, :], slots[:, :], 0.0, ALU.mult, ALU.add))
            then(d.tensor_tensor(slot_start[:, :], slot_end[:, :], slots[:, :], ALU.subtract))
            then(d.tensor_tensor(place[:, :, :], counts[:, :, :], tile_counts[:, :, :], ALU.subtract))
            then(d.tensor_tensor(place[:, :, :], place[:, :, :], earlier, ALU.add))
            then(d.scalar_tensor_tensor(out=place[:, :, :], in0=over_all_tiles(slot_start[:, :]), scalar=float(P), in1=place[:, :, :],
                                        op0=ALU.mult, op1=ALU.add))
            then(d.tensor_tensor(place[:, :, :], place[:, :, :], chosen[:, :, :], ALU.mult))
            then(d.tensor_reduce(target[:, :], by_tile(place[:, :, :]), AX.X, ALU.add))
            then(d.tensor_tensor(past[:, :, :], slot_number[:, :].unsqueeze(2).to_broadcast([P, SLOTS, E]),
                                 slot_end[:, :].unsqueeze(1).to_broadcast([P, SLOTS, E]), ALU.is_ge))
            then(d.tensor_reduce(slot_expert[:, :], past[:, :, :], AX.X, ALU.add))
            d.tensor_copy(target_int[:, :], target[:, :])
            d.tensor_copy(slot_end_int[:, :], slot_end[:, :])
            d.tensor_scalar(slot_expert_int[:, :], slot_expert[:, :], float(E - 1), None, ALU.min).then_inc(route, 1)
            dve.wait_ge(route, steps[0] + 1)
            assert steps[0] + 2 == ROUTED
            d.tensor_scalar(slot_buffer_int[:, :], slot_expert_int[:, :], 1, None, ALU.bitwise_and).then_inc(route, 1)

            def slot_inputs(i):
                dve.wait_ge(xT_filled, i + 1)
                d.tensor_copy(slot_xT[:, :, :].rearrange("p c s -> p (c s)"), ps_xT[:, 0:D]).then_inc(xT_copied, 1)
                dve.wait_ge(z1_filled, 2 * i + 1)
                d.tensor_copy(z1[:, 0:F1 // 2], ps_z1[0][:, :]).then_inc(z1_copied[0], 1)

            slot_inputs(0)

            def slot(i, pair, p, follows):
                dve.wait_ge(z2_filled, i + 1)
                d.tensor_copy(z2[:, :], ps_z2[:, :]).then_inc(z2_copied, 1)
                if follows:
                    slot_inputs(i + 1)
                dve.wait_ge(y_filled, i + 1)
                dve.wait_ge(residual_done, i + 1)
                if not (isinstance(pair, int) and pair == 0):
                    dve.wait_ge(y_stored[p], 16 * pair)
                d.tensor_tensor(y[:, p, :], ps_y[:, 0:D], residual[:, p, :], ALU.add).then_inc(y_done, 1)

            over_slots(dve, slot)

        @block.tensor
        def _(pe):
            t = nc.tensor
            chunks = lambda hi, lo: ((0, hi, 0), (1, hi, 1), (2, hi, 0), (0, lo, 0), (1, lo, 1))

            def transpose_ctx(T, b, jt):
                n = BT * T + b
                if jt == 0:
                    pe.wait_ge(split_done, n + 1)
                pe.wait_ge(ctxT_copied, 2 * n + jt)
                for c in range(3):
                    last = t.transpose(ps_ctx[:, c * P:(c + 1) * P], ctx_split[:, b, jt, c * P:(c + 1) * P].bitcast(F32), ident[:, :])
                last.then_inc(ctxT_filled, 1)

            def keys(n):
                pe.wait_ge(ctxT_copied, 2 * n + 2)
                pe.wait_ge(k_lo_done, n)
                for half in range(2):
                    for i, (c, w, r) in enumerate(chunks(wkv_hi, wkv_lo)):
                        last = t.matmul(ps_k[:, half * JM:(half + 1) * JM], w[:, 0, r, half * P:(half + 1) * P], ctxT[:, c, :],
                                        start=(i == 0), stop=(i == 4))
                last.then_inc(k_filled, 1)

            def values(n):
                pe.wait_ge(v_copied, n)
                for jt in range(2):
                    for i, (c, w, r) in enumerate(chunks(wkv_hi, wkv_lo)):
                        last = t.matmul(ps_v[:, jt * D:(jt + 1) * D], ctxT[:, c, jt * P:(jt + 1) * P], w[:, 1, r, :],
                                        start=(i == 0), stop=(i == 4))
                last.then_inc(v_filled, 1)

            def scores(n, k, half):
                if half == 0:
                    pe.wait_ge(k_lo_done, n + 1)
                    pe.wait_ge(k_last_done, n + 1)
                    pe.wait_ge(qd_done, n + 1)
                pe.wait_ge(s_masked, GROUPS * n + 2 * half)
                for i, (qi, ki) in enumerate(((0, 0), (0, 1), (1, 0))):
                    for r in range(2):
                        rs = slice(r * 64, r * 64 + 64)
                        last = t.matmul(ps_s[r][:, 0:J + 1], qd[qi][rs, k, half, :], kT[ki][rs, half, :],
                                        start=(i == 0), stop=(i == 2))
                last.then_inc(s_filled, 1)

            def weigh(T, k):
                n = BT * T + k
                pe.wait_ge(p_copied, 2 * n + 2)
                pe.wait_ge(v_copied, n + 1)
                pe.wait_ge(lastv_in[k], 16 * (T + 1))
                t.matmul(ps_o[:, 0:D], last_probT[:, :], last_v_rows[:, k, :], start=True, stop=False, skip_group_check=True)
                for g in range(GROUPS):
                    for jt in range(2):
                        last = t.matmul(ps_o[:, g * GC:(g + 1) * GC], probT[:, jt, g * P:(g + 1) * P],
                                        v[:, k % 2, jt, g * GC:(g + 1) * GC], start=False,
                                        stop=(g == GROUPS - 1 and jt == 1), skip_group_check=True)
                last.then_inc(o_filled, 1)

            def transpose_probs(n, jt):
                if jt == 0:
                    pe.wait_ge(exp_done, GROUPS * (n + 1))
                    pe.wait_ge(o_done, n)
                    t.transpose(ps_o[0:GROUPS, D:D + P], prob[:, :, JM:J].rearrange("p g o -> p (g o)"), ident[:, :]).then_inc(lastp_filled, 1)
                pe.wait_ge(p_copied, 2 * n + jt)
                for g in range(GROUPS):
                    last = t.transpose(ps_p[:, g * P:(g + 1) * P], prob[:, g, jt * P:(jt + 1) * P], ident[:, :])
                last.then_inc(p_filled, 1)

            def my_turn(T, e):
                pe.wait_ge(m_emptied, turn(T, e))

            def middle(T, k):
                has_q, has_out, has_local = parts(T)
                last = None
                if k == 0 and (has_q or has_local):
                    my_turn(T, 0)
                    if isinstance(T, int) and T < 0:
                        pe.wait_ge(w_in, 16 * 10)
                    if has_q:
                        pe.wait_ge(xn1_done, T + 2)
                        for c in range(2):
                            last = t.transpose(ps_m[:, c * P:(c + 1) * P], xn1[:, c * P:(c + 1) * P], ident[:, :])
                    if has_local:
                        pe.wait_ge(lexp_done, T - 1)
                        last = t.transpose(ps_m[:, 2 * P:3 * P], lprob[:, :], ident[:, :])
                if k == 1 and (has_q or has_local):
                    my_turn(T, 2)
                    if has_q:
                        for half in range(2):
                            for c in range(2):
                                last = t.matmul(ps_m[:, half * P:(half + 1) * P], wq[:, c, half * P:(half + 1) * P],
                                                turned0[:, c * P:(c + 1) * P], start=(c == 0), stop=(c == 1))
                    if has_local:
                        last = t.matmul(ps_m[:, 2 * P:4 * P], turned0[:, 2 * P:3 * P], lv[:, :], start=True, stop=True)
                if k == 2 and (has_out or has_local):
                    my_turn(T, 4)
                    if has_out:
                        pe.wait_ge(xn2_done, T)
                        for c in range(2):
                            last = t.transpose(ps_m[:, c * P:(c + 1) * P], xn2[:, c * P:(c + 1) * P], ident[:, :])
                    if has_local:
                        pe.wait_ge(xn3_done, T - 1)
                        for c in range(2):
                            last = t.transpose(ps_m[:, (2 + c) * P:(3 + c) * P], x3n[:, D + c * P:D + (c + 1) * P], ident[:, :])
                if k == 3 and (has_out or has_local):
                    my_turn(T, 6)
                    if has_out:
                        for c in range(2):
                            last = t.matmul(ps_m[:, 0:D], turned4[:, c * P:(c + 1) * P], lw[:, 2, c, :], start=(c == 0), stop=(c == 1))
                    if has_local:
                        for c in range(2):
                            last = t.matmul(ps_m[:, D:D + E], turned4[:, (2 + c) * P:(3 + c) * P], wr[:, c, :], start=(c == 0), stop=(c == 1))
                if last is not None:
                    last.then_inc(m_filled, 1)

            def end(T, k):
                has_q, has_out, has_local = parts(T)
                if not has_out:
                    return
                my_turn(T, 2 * k + 1)
                if k == 0:
                    pe.wait_ge(o_done, BT * T)
                    for c in range(2):
                        last = t.transpose(ps_m[:, c * P:(c + 1) * P], attn[:, c * P:(c + 1) * P], ident[:, :])
                if k == 1:
                    for c in range(2):
                        last = t.matmul(ps_m[:, 0:D], attnT[:, c, :], wo[:, c, :], start=(c == 0), stop=(c == 1))
                if k == 2:
                    for w in range(4):
                        half = w % 2
                        for c in range(2):
                            last = t.matmul(ps_m[:, w * P:(w + 1) * P], lw[:, w // 2, c, half * P:(half + 1) * P],
                                            turned4[:, c * P:(c + 1) * P], start=(c == 0), stop=(c == 1))
                if k == 3:
                    for c in range(2):
                        last = t.matmul(ps_m[:, 0:P], lqk[:, c, :], lqk[:, 2 + c, :], start=(c == 0), stop=(c == 1))
                last.then_inc(m_filled, 1)

            pe.wait_ge(consts, 6)
            pe.wait_ge(kv_in, 16 * 7)
            t.transpose(ps_m[:, 0:B], last_ctx[:, 0:P], ident[0:B, 0:B])
            t.transpose(ps_m[0:C2, B:2 * B], last_ctx[:, P:C], ident[0:B, 0:B]).then_inc(last_step, 1)
            pe.wait_ge(last_copied, 2)
            for half in range(2):
                for c, rows_c in ((0, P), (1, C2)):
                    t.matmul(ps_k[:, half * B:(half + 1) * B], wkv[0:rows_c, 0, c, half * P:(half + 1) * P],
                             last_ctxT[0:rows_c, c, :], start=(c == 0), stop=(c == 1))
            for c, rows_c in ((0, P), (1, C2)):
                last = t.matmul(ps_v[0:B, 0:D], last_ctxT[0:rows_c, c, :], wkv[0:rows_c, 1, c, :], start=(c == 0), stop=(c == 1))
            last.then_inc(last_step, 1)
            pe.wait_ge(wkv_split, 2)
            pe.wait_ge(last_copied, 5)

            def iteration(T):
                first = isinstance(T, int) and T < 0
                if first:
                    transpose_ctx(0, 0, 0)
                    transpose_ctx(0, 0, 1)
                    keys(0)
                    values(0)
                for k in range(BT):
                    n = BT * T + k
                    ahead = in_tiles(T) and exists(T, k + 1)
                    Ta, ba = (T, k + 1) if k + 1 < BT else (T + 1, 0)
                    if ahead:
                        transpose_ctx(Ta, ba, 0)
                    if in_tiles(T):
                        scores(n, k, 0)
                    if ahead:
                        transpose_ctx(Ta, ba, 1)
                    if not first and exists(T, k - 1) and not (isinstance(T, int) and BT * T + k > B):
                        weigh(T if k else T - 1, (k - 1) % BT)
                    if in_tiles(T):
                        scores(n, k, 1)
                    if ahead:
                        keys(n + 1)
                    middle(T, k)
                    if in_tiles(T):
                        transpose_probs(n, 0)
                    if ahead:
                        values(n + 1)
                    if in_tiles(T):
                        transpose_probs(n, 1)
                    end(T, k)

            over_tiles(pe, iteration)

            pe.wait_ge(bias_in, 48)
            n_b = E * (F1 + F2) // P
            pe.wait_ge(route, 6)
            n_et = E * TILES
            chosen_flat = chosen_bf[:, :, :].rearrange("p e t -> p (e t)")
            t.matmul(ps_m[:, 0:n_et], before[:, :], chosen_flat, start=True, stop=True)
            t.matmul(ps_m[:, n_et:2 * n_et], ones_bf[:, :], chosen_flat, start=True, stop=True).then_inc(chosen_counted, 1)
            t.transpose(ps_p[:, 0:n_b], bias_rows[:, :], ident[0:n_b, 0:n_b]).then_inc(bias_turned, 1)

            def weight(buffer, at, n):
                return weights[:, bass.ds(buffer, 1), at:at + n].rearrange("p o n -> p (o n)")

            def turn_x(i, pair, p):
                pe.wait_ge(slot_in[p], 16 * (pair + 1))
                pe.wait_ge(xT_copied, i)
                for c in range(2):
                    last = t.transpose(ps_xT[:, c * P:(c + 1) * P], slot_x[:, p, D + c * P:D + (c + 1) * P], ident[:, :])
                last.then_inc(xT_filled, 1)

            def layer1(i, buffer):
                pe.wait_ge(xT_copied, i + 1)
                for half in range(2):
                    pe.wait_ge(z1_copied[half], i)
                    for c in range(2):
                        last = t.matmul(ps_z1[half][:, :], slot_xT[:, c, :], weight(buffer, c * F1 + half * 512, 512),
                                        start=(c == 0), stop=(c == 1))
                    last.then_inc(z1_filled, 1)

            def turn_z1(i):
                for half in range(2):
                    pe.wait_ge(z1_copied[half], i + 1)
                    pe.wait_ge(h1_done, 2 * i)
                    for c in range(4):
                        f = 4 * half + c
                        last = t.transpose(ps_t1[half][:, c * P:(c + 1) * P], z1[:, f * P:(f + 1) * P], ident[:, :])
                    last.then_inc(t1_filled, 1)

            def layer2(i, buffer):
                pe.wait_ge(z2_copied, i)
                for f in range(F1 // P):
                    if f % 4 == 0:
                        pe.wait_ge(h1_done, 2 * i + f // 4 + 1)
                    last = t.matmul(ps_z2[:, :], h1[:, f, :], weight(buffer, W2_AT + f * F2, F2), start=(f == 0), stop=(f == F1 // P - 1))
                last.then_inc(z2_filled, 1)

            def turn_z2(i):
                pe.wait_ge(z2_copied, i + 1)
                pe.wait_ge(h2_done, i)
                for c in range(F2 // P):
                    last = t.transpose(ps_t2[:, c * P:(c + 1) * P], z2[:, c * P:(c + 1) * P], ident[:, :])
                last.then_inc(t2_filled, 1)

            def layer3(i, buffer):
                pe.wait_ge(h2_done, i + 1)
                pe.wait_ge(y_done, i)
                for c in range(F2 // P):
                    last = t.matmul(ps_y[:, 0:D], h2[:, c, :], weight(buffer, W3_AT + c * D, D), start=(c == 0), stop=(c == F2 // P - 1))
                last.then_inc(y_filled, 1)

            def expert_of(i):
                e = pe.value_load(slot_expert_int[0:1, bass.ds(i, 1)], min_val=0, max_val=E - 1)
                buffer = buffer_of(i)
                pe.wait_ge(expert_ready, e + 1)
                return buffer

            def buffer_of(i):
                return pe.value_load(slot_buffer_int[0:1, bass.ds(i, 1)], min_val=0, max_val=1)

            pe.wait_ge(route, ROUTED)
            turn_x(0, 0, 0)
            layer1(0, expert_of(0))
            turn_z1(0)

            def slot(i, pair, p, follows):
                buffer = buffer_of(i)
                layer2(i, buffer)
                if follows:
                    turn_x(i + 1, pair + p, 1 - p)
                    layer1(i + 1, expert_of(i + 1))
                turn_z2(i)
                if follows:
                    turn_z1(i + 1)
                layer3(i, buffer)

            over_slots(pe, slot)


_INS = ['x', 'ctx_768', 'mask_BxS2_bf1', 'L0_xattn_Wq', 'L0_xattn_Wk', 'L0_xattn_Wv', 'L0_xattn_Wo',
        'L0_attn_Wq', 'L0_attn_bq', 'L0_attn_Wk', 'L0_attn_bk', 'L0_attn_Wv', 'L0_attn_bv',
        'L0_ffn_Wr', 'L0_ffn_br', 'L0_ffn_W1', 'L0_ffn_b1', 'L0_ffn_W2', 'L0_ffn_b2', 'L0_ffn_W3', 'L0_ffn_b3']
_OUTS = [((64, 32, 256), 'float32')]


def kernel(**inputs):
    import numpy as _np
    import concourse.bacc as _bacc
    from concourse import mybir as _mybir
    from concourse.bass_utils import run_bass_kernel_spmd as _run

    nc = _bacc.Bacc("TRN2", target_bir_lowering=False, num_devices=1)
    arrays, args = {}, []
    for name in _INS:
        a = _np.ascontiguousarray(inputs[name])
        if a.dtype == _np.bool_:
            a = a.view(_np.uint8)
        arrays[f"in_{name}_dram"] = a
        args.append(nc.dram_tensor(f"in_{name}_dram", a.shape, _mybir.dt.from_np(a.dtype), kind="ExternalInput").ap())
    for i, (shape, dtype) in enumerate(_OUTS):
        dt = _mybir.dt.from_np(_np.dtype(dtype))
        args.append(nc.dram_tensor(f"out_{i}_dram", shape, dt, kind="ExternalOutput").ap())
    perceiver_kernel(nc, *args)
    r = _run(nc, [arrays], core_ids=[0])
    got = tuple(r.results[0][f"out_{i}_dram"] for i in range(len(_OUTS)))
    return got[0]
```

```python
from contextlib import ExitStack

import concourse.bass as bass
from concourse import mybir

F32 = mybir.dt.float32
F32R = mybir.dt.float32r
BF16 = mybir.dt.bfloat16
I32 = mybir.dt.int32
U8 = mybir.dt.uint8
ACT = mybir.ActivationFunctionType
ALU = mybir.AluOpType
AX = mybir.AxisListType

P = 128
EPS = 1e-5
MASKED = -1.0e30


def perceiver_kernel(nc, x, ctx_768, mask, Wq, Wk, Wv, Wo, lWq, lbq, lWk, lbk, lWv, lbv,
                     Wr, br, W1, b1, W2, b2, W3, b3, out):
    B, S, D = x.shape
    J, C = ctx_768.shape[1:]
    HEADS, HD = 16, D // 16
    GROUPS = HEADS * S // P
    HG = HEADS // GROUPS
    GC = HG * HD
    BT = P // S
    TILES = B * S // P
    C2 = C - P
    JM = J - 1
    E = Wr.shape[1]

    F1, F2 = W1.shape[2], W2.shape[2]
    SLOTS = (B * S + E * (P - 1)) // P
    AHEAD, BUFFERS = 5, 3
    ROW = 2 * D + 4
    ID = 2 * D
    N_TOKENS = B * S
    W_COLS = 2 * F1 + F1 // P * F2 + F2 // P * D
    W2_AT, W3_AT = 2 * F1, 2 * F1 + F1 // P * F2

    x_rows = x.rearrange("b s d -> (b s) d")
    out_rows = out.rearrange("b s d -> (b s) d")

    with ExitStack() as stack:
        def sb(name, shape, dt=F32):
            return stack.enter_context(nc.sbuf_tensor(name, shape, dt))

        def sem(name):
            return stack.enter_context(nc.semaphore(name))

        def bank(name):
            return stack.enter_context(nc.psum_tensor(name, [P, 512], F32))

        ps_ctx = bank("ps_ctx")
        ps_k = bank("ps_k")
        ps_v = bank("ps_v")
        ps_s = [bank("ps_s0"), bank("ps_s1")]
        ps_p = bank("ps_p")
        ps_o = bank("ps_o")
        ps_m = bank("ps_m")

        ident = sb("ident", [P, P])
        head_blocks = sb("head_blocks", [P, 8])
        head_mask = sb("head_mask", [P, HG])
        band = sb("band", [P, P])
        neg_half = sb("neg_half", [P, 1])
        wq = sb("wq", [P, 2, D])
        wo = sb("wo", [P, 2, D])
        lw = sb("lw", [P, 3, 2, D])
        wr = sb("wr", [P, 2, E])
        lbias = sb("lbias", [P, 4])
        bv_rows = sb("bv_rows", [P, D])
        br_rows = sb("br_rows", [P, E])
        wkv = sb("wkv", [P, 2, 2, D])
        wkv_hi = sb("wkv_hi", [P, 2, 2, D], F32R)
        wkv_lo = sb("wkv_lo", [P, 2, 2, D], F32R)

        last_ctx = sb("last_ctx", [B, C])
        last_ctxT = sb("last_ctxT", [P, 2, B])
        last_k = [sb("last_k_hi", [P, 2, B], F32R), sb("last_k_lo", [P, 2, B], F32R)]
        last_v_dram = nc.dram_tensor("last_v_dram", (B, GROUPS, D), F32, kind="Internal").ap()

        ctx_raw = sb("ctx_raw", [P, BT, 2, C])
        mask_bytes = sb("mask_bytes", [B, J], U8)
        mask_rows = sb("mask_rows", [B, J])
        mask_dram = nc.dram_tensor("mask_dram", (B, J), F32, kind="Internal").ap()
        ctx_split = sb("ctx_split", [P, BT, 2, 3 * P], F32R)
        ctxT = sb("ctxT", [P, 3, 2 * P], F32R)
        kT = [sb("kT_hi", [P, 2, J + 1], F32R), sb("kT_lo", [P, 2, J + 1], F32R)]
        v = sb("v", [P, 2, 2, D])
        mask_add = sb("mask_add", [P, BT, J])
        xt = sb("xt", [P, D])
        xn1 = sb("xn1", [P, D])
        turned0 = sb("turned0", [P, 3 * P])
        q = [sb("q_hi", [P, 2, P], F32R), sb("q_lo", [P, 2, P], F32R)]
        qd = [sb("qd_hi", [P, BT, 2, P], F32R), sb("qd_lo", [P, BT, 2, P], F32R)]
        prob = sb("prob", [P, GROUPS, J])
        neg_max = sb("neg_max", [P, GROUPS])
        row_sum = sb("row_sum", [P, 2, GROUPS])
        row_inv = sb("row_inv", [P, GROUPS])
        probT = sb("probT", [P, 2, GROUPS * P])
        last_probT = sb("last_probT", [GROUPS, P])
        last_v_rows = sb("last_v_rows", [GROUPS, BT, D])
        attn = sb("attn", [P, D])

        attnT = sb("attnT", [P, 2, P])
        xr = sb("xr", [P, D])
        x2 = sb("x2", [P, D])
        xn2 = sb("xn2", [P, D])
        turned4 = sb("turned4", [P, 4 * P])
        lqk = sb("lqk", [P, 4, P])
        lv = sb("lv", [P, D])
        lprob = sb("lprob", [P, P])
        lneg_max = sb("lneg_max", [P, 1])
        lrow_sum = sb("lrow_sum", [P, 1])
        lrow_inv = sb("lrow_inv", [P, 1])
        x3n = sb("x3n", [P, 2 * D])
        arena = sb("arena", [P, (BUFFERS - 1) * W_COLS + max(TILES * ROW, W_COLS)])
        rows_at = (BUFFERS - 1) * W_COLS
        rows = arena[:, rows_at:rows_at + TILES * ROW].rearrange("p (t d) -> p t d", t=TILES)
        weights = arena[:, 0:BUFFERS * W_COLS].rearrange("p (b n) -> p b n", b=BUFFERS)
        logits = sb("logits", [P, E, TILES])
        stats = [sb(f"stats{i}", [P, 6]) for i in range(3)]
        moments = [sb(f"moments{i}", [P, 2]) for i in range(3)]
        var_eps = [sb(f"var_eps{i}", [P, 1]) for i in range(3)]
        rstd = [sb(f"rstd{i}", [P, 1]) for i in range(3)]

        fill_row = sb("fill_row", [P, ROW])
        before = sb("before", [P, P], BF16)
        ones_bf = sb("ones_bf", [P, P], BF16)
        expert_rank = sb("expert_rank", [P, E])
        slot_number = sb("slot_number", [P, SLOTS])
        restart = sb("restart", [P, E, TILES])
        ones_row = sb("ones_row", [P, E])
        top = sb("top", [P, TILES])
        tied = sb("tied", [P, E, TILES])
        first = sb("first", [P, TILES])
        chosen = sb("chosen", [P, E, TILES])
        chosen_bf = sb("chosen_bf", [P, E, TILES], BF16)
        tile_counts = sb("tile_counts", [P, E, TILES])
        counts = sb("counts", [P, E, TILES])
        padded = sb("padded", [P, E], I32)
        slots_int = sb("slots_int", [P, E], I32)
        slots = sb("slots", [P, E])
        slot_end = sb("slot_end", [P, E])
        slot_start = sb("slot_start", [P, E])
        place = sb("place", [P, E, TILES])
        target = sb("target", [P, TILES])
        target_int = sb("target_int", [P, TILES], I32)
        past = sb("past", [P, SLOTS, E])
        slot_expert = sb("slot_expert", [P, SLOTS])
        slot_buffer = sb("slot_buffer", [P, SLOTS])
        wraps = sb("wraps", [P, SLOTS])
        slot_expert_int = sb("slot_expert_int", [P, SLOTS], I32)
        slot_buffer_int = sb("slot_buffer_int", [P, SLOTS], I32)
        slot_end_int = sb("slot_end_int", [P, E], I32)
        FILLS = -(-SLOTS // (TILES - 2))
        sorted_dram = nc.dram_tensor("sorted_dram", (FILLS * (TILES - 2) * P, ROW), F32, kind="Internal").ap()
        sorted_slots = sorted_dram.rearrange("(s p) d -> s p d", p=P)

        bias_rows = sb("bias_rows", [E * (F1 + F2) // P, P])
        bias_cols = sb("bias_cols", [P, E * (F1 + F2) // P])
        b3_rows = sb("b3_rows", [P, E, D])
        slot_x = ctx_split[:, :, :, :].bitcast(F32).rearrange("p b t c -> p (b t c)")[:, 0:AHEAD * ROW].rearrange("p (s d) -> p s d", s=AHEAD)
        slot_xT = attnT
        z1 = prob[:, :, :].rearrange("p g j -> p (g j)")
        h1 = probT[:, :, :].rearrange("p t (f s) -> p (t f) s", s=P)
        z2 = turned4
        h2 = lqk
        y = ctx_raw[:, :, :, :].rearrange("p b t c -> p (b t c)")[:, 0:AHEAD * D].rearrange("p (s d) -> p s d", s=AHEAD)
        last_v = weights[0:B, 0, 0:GROUPS * D].rearrange("b (g d) -> b g d", g=GROUPS)
        ps_z1 = [ps_ctx, ps_k]
        ps_t1 = [ps_v, ps_s[0]]
        ps_z2, ps_t2, ps_y, ps_xT = ps_s[1], ps_p, ps_o, ps_m

        fill_done = sem("fill_done")
        filled = sem("filled")
        router_consts = sem("router_consts")
        route = sem("route")
        chosen_counted = sem("chosen_counted")
        scattered = sem("scattered")
        expert_in = sem("expert_in")
        expert_ready = sem("expert_ready")
        bias_in = sem("bias_in")
        bias_turned = sem("bias_turned")
        bias_done = sem("bias_done")
        slot_in = [sem(f"slot_in{i}") for i in range(AHEAD)]
        xT_filled = sem("xT_filled")
        xT_copied = sem("xT_copied")
        z1_filled = sem("z1_filled")
        z1_copied = [sem("z1_copied_dve"), sem("z1_copied_act")]
        t1_filled = sem("t1_filled")
        h1_done = sem("h1_done")
        z2_filled = sem("z2_filled")
        z2_copied = sem("z2_copied")
        t2_filled = sem("t2_filled")
        h2_done = sem("h2_done")
        residual_done = sem("residual_done")
        y_filled = sem("y_filled")
        y_done = sem("y_done")
        y_stored = [sem(f"y_stored{i}") for i in range(AHEAD)]
        w_in = sem("w_in")
        wq_in = sem("wq_in")
        kv_in = sem("kv_in")
        consts = sem("consts")
        zeroed = sem("zeroed")
        wkv_split = sem("wkv_split")
        last_step = sem("last_step")
        last_copied = sem("last_copied")
        last_stored = sem("last_stored")
        x_in = sem("x_in")
        xr_in = sem("xr_in")
        ctx_in = [sem(f"ctx_in{i}") for i in range(BT)]
        lastv_in = [sem(f"lastv_in{i}") for i in range(BT)]
        split_hi = sem("split_hi")
        split_done = sem("split_done")
        mask_bytes_in = sem("mask_bytes_in")
        mask_done = sem("mask_done")
        mask_stored = sem("mask_stored")
        mask_in = [sem(f"mask_in{i}") for i in range(BT)]
        ctxT_filled = sem("ctxT_filled")
        ctxT_copied = sem("ctxT_copied")
        k_filled = sem("k_filled")
        k_hi_done = sem("k_hi_done")
        k_lo_done = sem("k_lo_done")
        k_last_done = sem("k_last_done")
        v_filled = sem("v_filled")
        v_copied = sem("v_copied")
        q_hi_done = sem("q_hi_done")
        qd_done = sem("qd_done")
        s_filled = sem("s_filled")
        s_masked = sem("s_masked")
        exp_done = sem("exp_done")
        lastp_filled = sem("lastp_filled")
        p_filled = sem("p_filled")
        p_copied = sem("p_copied")
        o_filled = sem("o_filled")
        inv_done = sem("inv_done")
        o_done = sem("o_done")
        m_filled = sem("m_filled")
        m_emptied = sem("m_emptied")
        xn1_done = sem("xn1_done")
        xn2_done = sem("xn2_done")
        xn3_done = sem("xn3_done")
        rows_done = sem("rows_done")
        linv_done = sem("linv_done")
        lexp_done = sem("lexp_done")
        ln_stats = [sem(f"ln_stats{i}") for i in range(3)]
        ln_moments = [sem(f"ln_moments{i}") for i in range(3)]
        ln_eps = [sem(f"ln_eps{i}") for i in range(3)]
        ln_rstd = [sem(f"ln_rstd{i}") for i in range(3)]
        waits_ended = sem("waits_ended")
        out_stored = sem("out_stored")

        def alone(eng):
            eng.sem_inc(waits_ended, 1)

        def turn(T, e):
            if isinstance(T, int) and T < 1:
                return 2 * (T + 1) + {0: 0, 2: 1}[e]
            if isinstance(T, int) and T == TILES + 1:
                return 8 * T - 4 + e // 2
            return 8 * T - 4 + e

        def parts(T):
            if not isinstance(T, int):
                return True, True, True
            return T + 1 < TILES, 1 <= T <= TILES, 2 <= T <= TILES + 1

        def over_tiles(eng, iteration):
            for T in (-1, 0, 1):
                iteration(T)
            with eng.Fori(2, TILES - 1) as T:
                iteration(T)
            for T in (TILES - 1, TILES, TILES + 1):
                iteration(T)

        def in_tiles(T):
            return not isinstance(T, int) or 0 <= T < TILES

        def exists(T, k):
            return not isinstance(T, int) or 0 <= BT * T + k < B

        def over_slots(eng, step):
            for q in range(AHEAD):
                step(q, 0, q)
            with eng.Fori(1, SLOTS // AHEAD) as run:
                for q in range(AHEAD):
                    step(AHEAD * run + q, run, q)
            for i in range(SLOTS // AHEAD * AHEAD, SLOTS):
                step(i, i // AHEAD, i % AHEAD)

        def follows(i, n):
            return not isinstance(i, int) or i + n < SLOTS

        def before_by(n, i, run, q):
            if isinstance(i, int) and i < n:
                return None
            return (run, q - n) if q >= n else (run - 1, q - n + AHEAD)

        PLACED, ROUTED = 19, 27
        block = stack.enter_context(nc.Block())

        @block.sync
        def _(sp):
            def load_ctx(T, b):
                n = BT * T + b
                sp.dma_start(ctx_raw[:, b, :, :], ctx_768[n, 0:JM, :].rearrange("(p t) c -> p t c", t=2)).then_inc(ctx_in[b], 16)

            def load_mask(T, b):
                sp.dma_start(mask_add[:, b, :], mask_dram[bass.ds(BT * T + b, 1), :].to_broadcast([P, J])).then_inc(mask_in[b], 16)

            def load_last_v(T, b):
                sp.dma_start(last_v_rows[:, b, :], last_v_dram[BT * T + b]).then_inc(lastv_in[b], 16)

            def load_x(dst, T, s):
                sp.dma_start(dst[:, :], x_rows.rearrange("(t p) d -> t p d", p=P)[T]).then_inc(s, 16)

            load_x(xt, 0, x_in)
            sp.dma_start(last_ctx[:, :], ctx_768[:, JM, :]).then_inc(kv_in, 16)
            for i, w in enumerate((Wk, Wv)):
                sp.dma_start(wkv[:, i, 0, :], w[0:P, :]).then_inc(kv_in, 16)
                sp.dma_start(wkv[0:C2, i, 1, :], w[P:C, :]).then_inc(kv_in, 16)
                sp.dma_start(wkv[C2:P, i, 1, :], w[P:C, :]).then_inc(kv_in, 16)
            load_ctx(0, 0)
            sp.dma_start(wq[:, :, :], Wq.rearrange("(c p) n -> p c n", p=P)).then_inc(wq_in, 16)
            sp.dma_start(mask_bytes[:, :], mask).then_inc(mask_bytes_in, 16)
            for b in range(1, BT):
                load_ctx(0, b)
            sp.wait_ge(mask_done, 2)
            sp.dma_start(mask_dram, mask_rows[:, :]).then_inc(mask_stored, 16)
            for dst, w in ((wo, Wo), (wr, Wr)):
                sp.dma_start(dst[:, :, :], w.rearrange("(c p) n -> p c n", p=P)).then_inc(w_in, 16)
            sp.wait_ge(mask_stored, 16)
            for b in range(BT):
                load_mask(0, b)
            for i, w in enumerate((lWq, lWk, lWv)):
                sp.dma_start(lw[:, i, :, :], w.rearrange("(c p) n -> p c n", p=P)).then_inc(w_in, 16)
            for i, w in enumerate((lbq, lbk)):
                sp.dma_start(lbias[:, 2 * i:2 * i + 2], w.rearrange("(c p) -> p c", p=P), allow_slow_non_contiguous=True).then_inc(w_in, 16)
            sp.dma_start(bv_rows[:, :], lbv.rearrange("(o n) -> o n", o=1).to_broadcast([P, D])).then_inc(w_in, 16)
            sp.dma_start(br_rows[:, :], br.rearrange("(o n) -> o n", o=1).to_broadcast([P, E])).then_inc(w_in, 16)

            def ahead(T):
                sp.wait_ge(xn1_done, T)
                load_x(xt, T, x_in)
                for b in range(BT):
                    n = BT * (T - 1) + b
                    sp.wait_ge(split_done, n + 1)
                    load_ctx(T, b)
                    sp.wait_ge(s_masked, GROUPS * (n + 1))
                    load_mask(T, b)
                    if isinstance(T, int) and T == 1:
                        if b == 0:
                            sp.wait_ge(last_copied, 5)
                            sp.dma_start(last_v_dram, last_v[:, :, :]).then_inc(last_stored, 16)
                            sp.wait_ge(last_stored, 16)
                    else:
                        sp.wait_ge(o_filled, BT * (T - 2) + b + 1)
                    load_last_v(T - 1, b)
                    if b == 1 and not (isinstance(T, int) and T == 1):
                        sp.wait_ge(m_emptied, turn(T - 2, 3) + 1)
                        load_x(xr, T - 2, xr_in)
            ahead(1)
            sp.dma_start(bias_rows[0:E * F1 // P, :], b1.rearrange("e (c p) -> (e c) p", p=P)).then_inc(bias_in, 16)
            sp.dma_start(bias_rows[E * F1 // P:, :], b2.rearrange("e (c p) -> (e c) p", p=P)).then_inc(bias_in, 16)
            sp.dma_start(b3_rows[:, :, :].rearrange("p e d -> p (e d)"),
                         b3.rearrange("(o e) d -> o (e d)", o=1).to_broadcast([P, E * D])).then_inc(bias_in, 16)
            sp.wait_ge(fill_done, 2)
            with sp.Fori(2, TILES) as T:
                ahead(T)
                for i in range(FILLS):
                    sp.dma_start(sorted_slots[FILLS * (T - 2) + i], fill_row[:, :]).then_inc(filled, 16)
            for b in range(BT):
                sp.wait_ge(o_filled, BT * (TILES - 2) + b + 1)
                load_last_v(TILES - 1, b)
            for T in (TILES - 2, TILES - 1):
                sp.wait_ge(m_emptied, turn(T, 3) + 1)
                load_x(xr, T, xr_in)

            def load_expert(e):
                for w, at, n in ((W1, 0, F1), (W2, W2_AT, F2), (W3, W3_AT, D)):
                    k = w.shape[1] // P
                    sp.dma_start(weights[:, e % BUFFERS, at:at + k * n].rearrange("p (k n) -> p k n", k=k),
                                 w[e].rearrange("(k p) n -> p k n", p=P)).then_inc(expert_in, 16)
                sp.wait_ge(expert_in, 48 * (e + 1))
                sp.sem_inc(expert_ready, 1)
            for e in range(BUFFERS - 1):
                load_expert(e)
            sp.wait_ge(scattered, 16 * TILES)
            for q in range(AHEAD):
                sp.wait_ge(slot_in[q], 16)
            load_expert(BUFFERS - 1)
            sp.wait_ge(route, ROUTED)
            for e in range(BUFFERS, E):
                last_slot = sp.value_load(slot_end_int[0:1, e - BUFFERS:e - BUFFERS + 1], min_val=1, max_val=SLOTS)
                sp.wait_ge(y_filled, last_slot)
                load_expert(e)
            for q in range(AHEAD):
                sp.wait_ge(y_stored[q], 16 * len(range(q, SLOTS, AHEAD)))

        @block.gpsimd
        def _(pool):
            g = nc.gpsimd
            g.memset(ident[:, :], 0.0).then_inc(zeroed, 1)
            g.memset(head_blocks[:, :], 1.0).then_inc(zeroed, 1)
            g.memset(band[:, :], 0.0).then_inc(zeroed, 1)
            g.memset(neg_half[:, :], -0.5).then_inc(consts, 1)
            for i in range(2):
                g.memset(kT[i][:, :, JM:J + 1].bitcast(F32), 0.0).then_inc(consts, 1)
            pool.wait_ge(zeroed, 3)
            g.affine_select(out=ident[:, :], in_=ident[:, :], compare_op=ALU.not_equal, fill=1.0, base=0,
                            pattern=[[-1, P]], channel_multiplier=1).then_inc(consts, 1)
            g.affine_select(out=head_blocks[:, :], in_=head_blocks[:, :], compare_op=ALU.is_ge, fill=0.0, base=0,
                            pattern=[[-HD, 8]], channel_multiplier=1).then_inc(zeroed, 1)
            pool.wait_ge(zeroed, 4)
            g.affine_select(out=head_blocks[:, :], in_=head_blocks[:, :], compare_op=ALU.is_ge, fill=0.0, base=HD - 1,
                            pattern=[[HD, 8]], channel_multiplier=-1).then_inc(zeroed, 1)
            pool.wait_ge(zeroed, 5)
            g.tensor_tensor(head_mask[:, :], head_blocks[:, 0:HG], head_blocks[:, HG:2 * HG], ALU.add).then_inc(consts, 1)
            n = 5
            for base, mult, pattern in ((2, 1, [[-1, P]]), (2, -1, [[1, P]]),
                                        (0, 1, [[-S, BT], [0, S]]), (S - 1, -1, [[S, BT], [0, S]])):
                view = band[:, :] if len(pattern) == 1 else band[:, :].rearrange("p (a b) -> p a b", b=S)
                g.affine_select(out=view, in_=view, compare_op=ALU.is_ge, fill=MASKED, base=base,
                                pattern=pattern, channel_multiplier=mult).then_inc(zeroed, 1)
                n += 1
                pool.wait_ge(zeroed, n)
            g.memset(last_v[:, :, :], 0.0).then_inc(consts, 1)
            def prepare_routing():
                g.memset(fill_row[:, 0:ID], 0.0).then_inc(fill_done, 1)
                g.memset(fill_row[:, ID:ROW].bitcast(I32), 2 * N_TOKENS).then_inc(fill_done, 1)
                g.iota(expert_rank[:, :], pattern=[[-1, E]], base=E, channel_multiplier=0,
                       allow_small_or_imprecise_dtypes=True).then_inc(router_consts, 1)
                g.iota(slot_number[:, :], pattern=[[1, SLOTS]], base=0, channel_multiplier=0,
                       allow_small_or_imprecise_dtypes=True).then_inc(router_consts, 1)
                g.memset(ones_row[:, :], 1.0).then_inc(router_consts, 1)
                g.memset(ones_bf[:, :], 1.0).then_inc(router_consts, 1)
                g.memset(restart[:, :, 0:1], 0.0).then_inc(router_consts, 1)
                g.memset(restart[:, :, 1:TILES], 1.0).then_inc(router_consts, 1)
                pool.wait_ge(router_consts, 6)
                g.affine_select(out=before[:, :], in_=ones_bf[:, :], compare_op=ALU.is_gt, fill=0.0, base=0,
                                pattern=[[1, P]], channel_multiplier=-1).then_inc(router_consts, 1)
                g.iota(rows[:, :, ID:ROW].bitcast(I32), pattern=[[P, TILES], [0, ROW - ID]], base=0,
                       channel_multiplier=1).then_inc(router_consts, 1)

            def split_ctx(T, b):
                n = BT * T + b
                pool.wait_ge(split_hi, n + 1)
                g.tensor_tensor(ctx_split[:, b, :, C:2 * P], ctx_raw[:, b, :, P:C],
                                ctx_split[:, b, :, P:C].bitcast(F32), ALU.subtract)
                g.tensor_tensor(ctx_split[:, b, :, 2 * P:3 * P], ctx_raw[:, b, :, 0:P],
                                ctx_split[:, b, :, 0:P].bitcast(F32), ALU.subtract).then_inc(split_done, 1)

            def place_queries(b):
                for i in range(2):
                    last = g.tensor_tensor(
                        qd[i][:, b, :, :].rearrange("p c (h s) -> p c h s", h=HG),
                        q[i][:, :, b * S:(b + 1) * S].bitcast(F32).unsqueeze(2).to_broadcast([P, 2, HG, S]),
                        head_mask[:, :].unsqueeze(1).unsqueeze(3).to_broadcast([P, 2, HG, S]), ALU.mult)
                last.then_inc(qd_done, 1)

            def scale_of(i, t):
                pool.wait_ge(ln_moments[i], t + 1)
                alone(pool)
                g.tensor_scalar(var_eps[i][:, :], moments[i][:, 1:2], EPS, None, ALU.add).then_inc(ln_eps[i], 1)
                pool.wait_ge(ln_eps[i], t + 1)
                g.tensor_tensor(rstd[i][:, :], var_eps[i][:, :], neg_half[:, :], ALU.pow).then_inc(ln_rstd[i], 1)

            def iteration(T):
                has_q, has_out, has_local = parts(T)
                if isinstance(T, int) and T < 0:
                    scale_of(0, 0)
                    split_ctx(0, 0)
                    pool.wait_ge(mask_bytes_in, 16)
                    g.tensor_scalar(mask_rows[:, 0:JM].rearrange("b (t m) -> b t m", t=2),
                                    mask_bytes[:, 0:JM].rearrange("b (m t) -> b t m", t=2),
                                    1.0, -MASKED, ALU.subtract, ALU.mult).then_inc(mask_done, 1)
                    g.tensor_scalar(mask_rows[:, JM:J], mask_bytes[:, JM:J], 1.0, -MASKED,
                                    ALU.subtract, ALU.mult).then_inc(mask_done, 1)
                    for b in range(1, BT):
                        split_ctx(0, b)
                for k in range(BT):
                    n = BT * T + k
                    if k == 0 and has_q and in_tiles(T):
                        scale_of(0, T + 1)
                    if k == 2 and has_local:
                        scale_of(2, T - 2)
                    if k == 2 and has_out:
                        scale_of(1, T - 1)
                    if in_tiles(T) and exists(T, k + 1):
                        pool.wait_ge(s_filled, 2 * n + 2)
                        alone(pool)
                        for i in range(2):
                            last = g.tensor_copy(kT[i][:, :, JM:J], last_k[i][:, :, bass.ds(n + 1, 1)])
                        last.then_inc(k_last_done, 1)
                    if has_q and k >= 1:
                        if k == 1:
                            pool.wait_ge(m_emptied, turn(T, 2) + 1)
                        for b in range(0 if k == 1 else k, k + 1):
                            if in_tiles(T):
                                pool.wait_ge(s_filled, 2 * (BT * T + b) + 2)
                            place_queries(b)
                    if in_tiles(T) and has_q:
                        split_ctx(T + 1, k)
                    if isinstance(T, int) and T < 0 and k == 1:
                        pool.wait_ge(last_copied, 4)
                        for i in range(2):
                            last = g.tensor_copy(kT[i][:, :, JM:J], last_k[i][:, :, 0:1])
                        last.then_inc(k_last_done, 1)
                if isinstance(T, int) and T == 0:
                    prepare_routing()

            over_tiles(pool, iteration)

            pool.wait_ge(rows_done, TILES)
            pool.wait_ge(filled, 16 * FILLS * (TILES - 2))
            pool.wait_ge(route, PLACED)
            for T in range(TILES):
                g.indirect_dma_start(out=sorted_dram, out_offset=bass.IndirectOffsetOnAxis(ap=target_int[:, T:T + 1], axis=0),
                                     in_=rows[:, T, :], in_offset=None,
                                     bounds_check=SLOTS * P - 1, oob_is_err=False).then_inc(scattered, 16)

            pool.wait_ge(bias_in, 48)
            pool.wait_ge(route, ROUTED)

            def slot(i, run, q):
                pool.wait_ge(slot_in[q], 16 * (run + 1))
                alone(pool)
                e = pool.value_load(slot_expert_int[0:1, bass.ds(i, 1)], min_val=0, max_val=E - 1)
                g.tensor_tensor(y[:, q, :], slot_x[:, q, 0:D], b3_rows[:, bass.ds(e, 1), :].rearrange("p o d -> p (o d)"),
                                ALU.add).then_inc(residual_done, 1)
                pool.wait_ge(y_done, i + 1)
                alone(pool)
                g.indirect_dma_start(out=out_rows, out_offset=bass.IndirectOffsetOnAxis(ap=slot_x[:, q, ID:ID + 1].bitcast(I32), axis=0),
                                     in_=y[:, q, :], in_offset=None, bounds_check=N_TOKENS - 1, oob_is_err=False).then_inc(y_stored[q], 16)

            over_slots(pool, slot)

        @block.scalar
        def _(act):
            a = nc.scalar

            def copy_ctxT(n, jt):
                act.wait_ge(ctxT_filled, 2 * n + jt + 1)
                a.copy(ctxT[:, :, jt * P:(jt + 1) * P], ps_ctx[:, 0:3 * P].rearrange("p (c j) -> p c j", c=3)).then_inc(ctxT_copied, 1)

            def round_ctx(T, b):
                act.wait_ge(ctx_in[b], 16 * (T + 1))
                a.copy(ctx_split[:, b, :, 0:C], ctx_raw[:, b, :, :]).then_inc(split_hi, 1)

            def exponentials(n, k, half):
                for g in (2 * half, 2 * half + 1):
                    act.wait_ge(s_masked, GROUPS * n + g + 1)
                    last = a.activation(prob[:, g, :], prob[:, g, :], ACT.Exp, bias=neg_max[:, g:g + 1], scale=-1.0,
                                        accum_out=row_sum[:, k % 2, g:g + 1])
                    last.then_inc(exp_done, 1)

            def copy_k(n):
                act.wait_ge(k_filled, n + 1)
                a.copy(kT[0][:, :, 0:JM], ps_k[:, :].rearrange("p (c j) -> p c j", c=2)).then_inc(k_hi_done, 1)

            def copy_v(n, k):
                act.wait_ge(v_filled, n + 1)
                a.copy(v[:, k % 2, :, :].rearrange("p t d -> p (t d)"), ps_v[:, :]).then_inc(v_copied, 1)

            def middle(T, k):
                has_q, has_out, has_local = parts(T)
                if k == 1 and has_q:
                    act.wait_ge(m_filled, turn(T, 2) + 1)
                    if not (isinstance(T, int) and T < 0):
                        act.wait_ge(qd_done, BT * (T + 1))
                    a.copy(q[0][:, :, :].rearrange("p c s -> p (c s)"), ps_m[:, 0:2 * P]).then_inc(q_hi_done, 1)
                if k == 2 and (has_out or has_local):
                    act.wait_ge(m_filled, turn(T, 4) + 1)
                    lo, hi = (0 if has_out else 2 * P), (4 * P if has_local else 2 * P)
                    a.copy(turned4[:, lo:hi], ps_m[:, lo:hi]).then_inc(m_emptied, 1)

            def end(T, k):
                has_q, has_out, has_local = parts(T)
                if k == 0 and has_out:
                    act.wait_ge(m_filled, turn(T, 1) + 1)
                    a.copy(attnT[:, :, :].rearrange("p c s -> p (c s)"), ps_m[:, 0:2 * P]).then_inc(m_emptied, 1)

            def local_exponentials(T):
                act.wait_ge(m_emptied, turn(T - 1, 7) + 1)
                a.activation(lprob[:, :], lprob[:, :], ACT.Exp, bias=lneg_max[:, 0:1], scale=-1.0,
                             accum_out=lrow_sum[:, 0:1]).then_inc(lexp_done, 1)

            def keep_rows(T):
                act.wait_ge(xn3_done, T - 1)
                alone(act)
                a.copy(rows[:, bass.ds(T - 2, 1), 0:2 * D].rearrange("p o d -> p (o d)"), x3n[:, :]).then_inc(rows_done, 1)

            def iteration(T):
                has_q, has_out, has_local = parts(T)
                if isinstance(T, int) and T < 0:
                    act.wait_ge(kv_in, 16 * 7)
                    a.copy(wkv_hi[:, :, :, :], wkv[:, :, :, :]).then_inc(wkv_split, 1)
                    round_ctx(0, 0)
                    copy_ctxT(0, 0)
                    copy_ctxT(0, 1)
                    for b in range(1, BT):
                        round_ctx(0, b)
                    copy_k(0)
                    copy_v(0, 0)
                for k in range(BT):
                    n = BT * T + k
                    ahead = in_tiles(T) and exists(T, k + 1)
                    if ahead:
                        copy_ctxT(n + 1, 0)
                    if in_tiles(T):
                        exponentials(n, k, 0)
                    if ahead:
                        copy_ctxT(n + 1, 1)
                    if k == 0 and has_local:
                        local_exponentials(T)
                    if in_tiles(T):
                        exponentials(n, k, 1)
                    middle(T, k)
                    if ahead:
                        copy_k(n + 1)
                    if in_tiles(T) and has_q:
                        round_ctx(T + 1, k)
                    if k == 2 and has_local:
                        keep_rows(T)
                    if ahead:
                        copy_v(n + 1, k + 1)
                    end(T, k)

            over_tiles(act, iteration)

            def load_slot(i, q):
                act.dma_start(slot_x[:, q, :], sorted_slots[i]).then_inc(slot_in[q], 16)

            def first_layer(i, e):
                for half in range(2):
                    act.wait_ge(t1_filled, 2 * i + half + 1)
                    alone(act)
                    for c in range(4):
                        f = 4 * half + c
                        last = a.activation(h1[:, f, :], ps_t1[half][:, c * P:(c + 1) * P], ACT.Gelu,
                                            bias=bias_cols[:, bass.ds(e * (F1 // P) + f, 1)])
                    last.then_inc(h1_done, 1)

            def second_layer(i, e):
                act.wait_ge(t2_filled, i + 1)
                alone(act)
                for c in range(F2 // P):
                    last = a.activation(h2[:, c, :], ps_t2[:, c * P:(c + 1) * P], ACT.Gelu,
                                        bias=bias_cols[:, bass.ds(e * (F2 // P) + E * F1 // P + c, 1)])
                last.then_inc(h2_done, 1)

            def copy_z1(i):
                act.wait_ge(z1_filled, 2 * i + 2)
                a.copy(z1[:, F1 // 2:F1], ps_z1[1][:, :]).then_inc(z1_copied[1], 1)

            def expert_of(i):
                return act.value_load(slot_expert_int[0:1, bass.ds(i, 1)], min_val=0, max_val=E - 1)

            act.wait_ge(bias_turned, 1)
            a.copy(bias_cols[:, :], ps_p[:, 0:E * (F1 + F2) // P]).then_inc(bias_done, 1)
            act.wait_ge(bias_done, 1)
            act.wait_ge(scattered, 16 * TILES)
            act.wait_ge(route, ROUTED)
            for i in range(AHEAD):
                load_slot(i, i)
            copy_z1(0)
            first_layer(0, expert_of(0))
            copy_z1(1)

            def slot(i, run, q):
                if follows(i, 1):
                    first_layer(i + 1, expert_of(i + 1))
                second_layer(i, expert_of(i))
                if follows(i, 2):
                    copy_z1(i + 2)
                last = before_by(2, i, run, q)
                if last and follows(i, AHEAD - 2):
                    act.wait_ge(y_stored[last[1]], 16 * (last[0] + 1))
                    load_slot(i + AHEAD - 2, last[1])

            over_slots(act, slot)

        @block.vector
        def _(dve):
            d = nc.vector

            def f32(ap):
                return ap.bitcast(F32)

            def last_rows():
                dve.wait_ge(last_step, 2)
                d.tensor_copy(last_k[0][:, :, :], ps_p[:, 0:2 * B].rearrange("p (c b) -> p c b", c=2)).then_inc(last_copied, 1)
                dve.wait_ge(last_copied, 3)
                d.tensor_tensor(last_k[1][:, :, :], ps_p[:, 0:2 * B].rearrange("p (c b) -> p c b", c=2), f32(last_k[0][:, :, :]),
                                ALU.subtract).then_inc(last_copied, 1)
                dve.wait_ge(consts, 6)
                for g in range(GROUPS):
                    last = d.tensor_copy(last_v[:, g, g * GC:(g + 1) * GC], ps_o[0:B, g * GC:(g + 1) * GC])
                last.then_inc(last_copied, 1)

            def moments_of(i, t, src):
                d.bn_stats(stats[i][:, :], src).then_inc(ln_stats[i], 1)
                dve.wait_ge(ln_stats[i], t + 1)
                alone(dve)
                d.bn_aggr(moments[i][:, :], stats[i][:, :]).then_inc(ln_moments[i], 1)

            def normalise(i, t, src, dst, done):
                dve.wait_ge(ln_rstd[i], t + 1)
                d.tensor_scalar(dst, src, moments[i][:, 0:1], rstd[i][:, 0:1], ALU.subtract, ALU.mult).then_inc(done, 1)

            def mask_scores(T, n, k, half):
                dve.wait_ge(s_filled, 2 * n + half + 1)
                if half == 0:
                    dve.wait_ge(mask_in[k], 16 * (T + 1))
                alone(dve)
                for r in range(2):
                    g = 2 * half + r
                    d.tensor_tensor_reduce(prob[:, g, :], ps_s[r][:, 0:J], mask_add[:, k, :], -(HD ** -0.5), 3.0e38,
                                           ALU.add, ALU.min, neg_max[:, g:g + 1]).then_inc(s_masked, 1)

            def finish_batch(T, k):
                n = BT * T + k
                dve.wait_ge(exp_done, GROUPS * (n + 1))
                d.reciprocal(row_inv[:, :], row_sum[:, k % 2, :]).then_inc(inv_done, 1)
                dve.wait_ge(inv_done, n + 1)
                dve.wait_ge(o_filled, n + 1)
                if k == 0 and not (isinstance(T, int) and T < 1):
                    dve.wait_ge(m_filled, turn(T, 1) + 1)
                for h in range(HG):
                    p0 = h * S
                    last = d.tensor_tensor(
                        attn[k * S:(k + 1) * S, :].rearrange("p (g h e) -> p g h e", g=GROUPS, h=HG)[:, :, h, :],
                        ps_o[p0:p0 + S, 0:D].rearrange("p (g h e) -> p g h e", g=GROUPS, h=HG)[:, :, h, :],
                        row_inv[p0:p0 + S, :].unsqueeze(2).to_broadcast([S, GROUPS, HD]), ALU.mult)
                last.then_inc(o_done, 1)

            def copy_probT(n, jt):
                if jt == 0:
                    dve.wait_ge(lastp_filled, n + 1)
                    d.tensor_copy(last_probT[:, :], ps_o[0:GROUPS, D:D + P])
                dve.wait_ge(p_filled, 2 * n + jt + 1)
                d.tensor_copy(probT[:, jt, :], ps_p[:, :]).then_inc(p_copied, 1)

            def middle(T, k):
                has_q, has_out, has_local = parts(T)
                if k == 0 and (has_q or has_local):
                    dve.wait_ge(m_filled, turn(T, 0) + 1)
                    lo, hi = (0 if has_q else 2 * P), (3 * P if has_local else 2 * P)
                    d.tensor_copy(turned0[:, lo:hi], ps_m[:, lo:hi]).then_inc(m_emptied, 1)
                if k == 1 and (has_q or has_local):
                    dve.wait_ge(m_filled, turn(T, 2) + 1)
                    if has_q:
                        dve.wait_ge(q_hi_done, T + 2)
                        last = d.tensor_tensor(q[1][:, :, :].rearrange("p c s -> p (c s)"), ps_m[:, 0:2 * P],
                                               f32(q[0][:, :, :].rearrange("p c s -> p (c s)")), ALU.subtract)
                        if not has_local:
                            last.then_inc(m_emptied, 1)
                    if has_local:
                        t = T - 2
                        dve.wait_ge(lexp_done, t + 1)
                        d.reciprocal(lrow_inv[:, :], lrow_sum[:, :]).then_inc(linv_done, 1)
                        dve.wait_ge(linv_done, t + 1)
                        x3 = x3n[:, 0:D]
                        dve.wait_ge(rows_done, t)
                        d.scalar_tensor_tensor(out=x3, in0=ps_m[:, 2 * P:4 * P], scalar=lrow_inv[:, 0:1], in1=x2[:, :],
                                               op0=ALU.mult, op1=ALU.add).then_inc(m_emptied, 1)
                if k == 3 and (has_out or has_local):
                    dve.wait_ge(m_filled, turn(T, 6) + 1)
                    if has_out:
                        last = d.tensor_tensor(lv[:, :], ps_m[:, 0:D], bv_rows[:, :], ALU.add)
                    if has_local:
                        last = d.tensor_tensor(logits[:, :, bass.ds(T - 2, 1)].rearrange("p e o -> p (e o)"), ps_m[:, D:D + E],
                                               br_rows[:, :], ALU.add)
                    last.then_inc(m_emptied, 1)

            def end(T, k):
                has_q, has_out, has_local = parts(T)
                if k == 1 and has_local:
                    dve.wait_ge(m_emptied, turn(T, 2) + 1)
                    moments_of(2, T - 2, x3n[:, 0:D])
                if k == 1 and has_out:
                    t = T - 1
                    dve.wait_ge(m_filled, turn(T, 3) + 1)
                    dve.wait_ge(xr_in, 16 * (t + 1))
                    d.tensor_tensor(x2[:, :], ps_m[:, 0:D], xr[:, :], ALU.add).then_inc(m_emptied, 1)
                    dve.wait_ge(m_emptied, turn(T, 3) + 1)
                    moments_of(1, t, x2[:, :])
                if k == 2 and has_out:
                    if isinstance(T, int) and T == 1:
                        dve.wait_ge(w_in, 16 * 9)
                    dve.wait_ge(m_filled, turn(T, 5) + 1)
                    d.tensor_tensor(lqk[:, :, :], ps_m[:, :].rearrange("p (w s) -> p w s", w=4),
                                    lbias[:, :].unsqueeze(2).to_broadcast([P, 4, P]), ALU.add).then_inc(m_emptied, 1)
                if k == 3 and has_out:
                    dve.wait_ge(m_filled, turn(T, 7) + 1)
                    alone(dve)
                    d.tensor_tensor_reduce(lprob[:, :], ps_m[:, 0:P], band[:, :], -(D ** -0.5), 3.0e38,
                                           ALU.add, ALU.min, lneg_max[:, 0:1]).then_inc(m_emptied, 1)

            def lo_keys(n):
                dve.wait_ge(k_hi_done, n + 1)
                d.tensor_tensor(kT[1][:, :, 0:JM], ps_k[:, :].rearrange("p (c j) -> p c j", c=2), f32(kT[0][:, :, 0:JM]),
                                ALU.subtract).then_inc(k_lo_done, 1)

            def iteration(T):
                has_q, has_out, has_local = parts(T)
                first = isinstance(T, int) and T < 0
                if first:
                    dve.wait_ge(x_in, 16)
                    moments_of(0, 0, xt[:, :])
                    dve.wait_ge(wkv_split, 1)
                    d.tensor_tensor(wkv_lo[:, :, :, :], wkv[:, :, :, :], f32(wkv_hi[:, :, :, :]), ALU.subtract).then_inc(wkv_split, 1)
                    dve.wait_ge(last_step, 1)
                    d.tensor_copy(last_ctxT[:, 0, :], ps_m[:, 0:B]).then_inc(last_copied, 1)
                    d.tensor_copy(last_ctxT[0:C2, 1, :], ps_m[0:C2, B:2 * B]).then_inc(last_copied, 1)
                    normalise(0, 0, xt[:, :], xn1[:, :], xn1_done)
                    lo_keys(0)
                    middle(T, 0)
                    middle(T, 1)
                    last_rows()
                    return
                for k in range(BT):
                    n = BT * T + k
                    if k == 0 and has_q:
                        dve.wait_ge(x_in, 16 * (T + 2))
                        moments_of(0, T + 1, xt[:, :])
                    if in_tiles(T):
                        mask_scores(T, n, k, 0)
                    if k == 0 and has_q:
                        normalise(0, T + 1, xt[:, :], xn1[:, :], xn1_done)
                    if k == 2 and has_local:
                        normalise(2, T - 2, x3n[:, 0:D], x3n[:, D:2 * D], xn3_done)
                    if k == 2 and has_out:
                        normalise(1, T - 1, x2[:, :], xn2[:, :], xn2_done)
                    if not first and exists(T, k - 1) and not (isinstance(T, int) and BT * T + k > B):
                        finish_batch(T if k else T - 1, (k - 1) % BT)
                    if in_tiles(T):
                        mask_scores(T, n, k, 1)
                    middle(T, k)
                    if in_tiles(T):
                        copy_probT(n, 0)
                        if exists(T, k + 1):
                            lo_keys(n + 1)
                        copy_probT(n, 1)
                    end(T, k)

            over_tiles(dve, iteration)

            steps = [0]

            def then(ins):
                steps[0] += 1
                ins.then_inc(route, 1)
                dve.wait_ge(route, steps[0])

            def by_tile(ap):
                return ap.rearrange("p e t -> p t e")

            def over_experts(ap):
                return ap.unsqueeze(1).to_broadcast([P, E, TILES])

            def over_all_tiles(ap):
                return ap.unsqueeze(2).to_broadcast([P, E, TILES])

            dve.wait_ge(router_consts, 8)
            dve.wait_ge(m_emptied, turn(TILES + 1, 6) + 1)
            then(d.tensor_reduce(top[:, :], by_tile(logits[:, :, :]), AX.X, ALU.max))
            then(d.tensor_tensor(tied[:, :, :], logits[:, :, :], over_experts(top[:, :]), ALU.is_ge))
            then(d.tensor_tensor(tied[:, :, :], tied[:, :, :], over_all_tiles(expert_rank[:, :]), ALU.mult))
            then(d.tensor_reduce(first[:, :], by_tile(tied[:, :, :]), AX.X, ALU.max))
            then(d.tensor_tensor(chosen[:, :, :], tied[:, :, :], over_experts(first[:, :]), ALU.is_equal))
            then(d.tensor_copy(chosen_bf[:, :, :], chosen[:, :, :]))
            dve.wait_ge(chosen_counted, 1)
            n_et = E * TILES
            earlier = ps_m[:, 0:n_et].rearrange("p (e t) -> p e t", e=E)
            then(d.tensor_copy(tile_counts[:, :, :], ps_m[:, n_et:2 * n_et].rearrange("p (e t) -> p e t", e=E)))
            flat = lambda ap: ap.rearrange("p e t -> p (e t)")
            then(d.tensor_tensor_scan(flat(counts[:, :, :]), flat(restart[:, :, :]), flat(tile_counts[:, :, :]), 0.0, ALU.mult, ALU.add))
            then(d.tensor_scalar(padded[:, :], counts[:, :, TILES - 1:TILES].rearrange("p e o -> p (e o)"), 1.0, float(P - 1), ALU.max, ALU.add))
            then(d.tensor_scalar(slots_int[:, :], padded[:, :], 7, None, ALU.logical_shift_right))
            then(d.tensor_copy(slots[:, :], slots_int[:, :]))
            then(d.tensor_tensor_scan(slot_end[:, :], ones_row[:, :], slots[:, :], 0.0, ALU.mult, ALU.add))
            then(d.tensor_tensor(slot_start[:, :], slot_end[:, :], slots[:, :], ALU.subtract))
            then(d.tensor_tensor(place[:, :, :], counts[:, :, :], tile_counts[:, :, :], ALU.subtract))
            then(d.tensor_tensor(place[:, :, :], place[:, :, :], earlier, ALU.add))
            then(d.scalar_tensor_tensor(out=place[:, :, :], in0=over_all_tiles(slot_start[:, :]), scalar=float(P), in1=place[:, :, :],
                                        op0=ALU.mult, op1=ALU.add))
            then(d.tensor_tensor(place[:, :, :], place[:, :, :], chosen[:, :, :], ALU.mult))
            then(d.tensor_reduce(target[:, :], by_tile(place[:, :, :]), AX.X, ALU.add))
            then(d.tensor_copy(target_int[:, :], target[:, :]))
            assert steps[0] == PLACED
            then(d.tensor_tensor(past[:, :, :], slot_number[:, :].unsqueeze(2).to_broadcast([P, SLOTS, E]),
                                 slot_end[:, :].unsqueeze(1).to_broadcast([P, SLOTS, E]), ALU.is_ge))
            then(d.tensor_reduce(slot_expert[:, :], past[:, :, :], AX.X, ALU.add))
            then(d.tensor_scalar(slot_expert[:, :], slot_expert[:, :], float(E - 1), None, ALU.min))
            slot_buffer_of = slot_expert
            for m in range(BUFFERS, E, BUFFERS):
                then(d.tensor_scalar(wraps[:, :], slot_expert[:, :], float(m), -float(BUFFERS), ALU.is_ge, ALU.mult))
                then(d.tensor_tensor(slot_buffer[:, :], slot_buffer_of[:, :], wraps[:, :], ALU.add))
                slot_buffer_of = slot_buffer
            d.tensor_copy(slot_end_int[:, :], slot_end[:, :])
            d.tensor_copy(slot_expert_int[:, :], slot_expert[:, :])
            d.tensor_copy(slot_buffer_int[:, :], slot_buffer[:, :]).then_inc(route, 1)
            assert steps[0] + 1 == ROUTED

            def copy_xT(i):
                dve.wait_ge(xT_filled, i + 1)
                d.tensor_copy(slot_xT[:, :, :].rearrange("p c s -> p (c s)"), ps_xT[:, 0:D]).then_inc(xT_copied, 1)

            def copy_z1(i):
                dve.wait_ge(z1_filled, 2 * i + 1)
                d.tensor_copy(z1[:, 0:F1 // 2], ps_z1[0][:, :]).then_inc(z1_copied[0], 1)

            for i in range(2):
                copy_xT(i)
                copy_z1(i)

            def slot(i, run, q):
                dve.wait_ge(z2_filled, i + 1)
                d.tensor_copy(z2[:, :], ps_z2[:, :]).then_inc(z2_copied, 1)
                if follows(i, 2):
                    copy_xT(i + 2)
                    copy_z1(i + 2)
                dve.wait_ge(y_filled, i + 1)
                dve.wait_ge(residual_done, i + 1)
                d.tensor_tensor(y[:, q, :], ps_y[:, 0:D], y[:, q, :], ALU.add).then_inc(y_done, 1)

            over_slots(dve, slot)

        @block.tensor
        def _(pe):
            t = nc.tensor
            chunks = lambda hi, lo: ((0, hi, 0), (1, hi, 1), (2, hi, 0), (0, lo, 0), (1, lo, 1))

            def transpose_ctx(T, b, jt):
                n = BT * T + b
                if jt == 0:
                    pe.wait_ge(split_done, n + 1)
                pe.wait_ge(ctxT_copied, 2 * n + jt)
                for c in range(3):
                    last = t.transpose(ps_ctx[:, c * P:(c + 1) * P], ctx_split[:, b, jt, c * P:(c + 1) * P].bitcast(F32), ident[:, :])
                last.then_inc(ctxT_filled, 1)

            def keys(n):
                pe.wait_ge(ctxT_copied, 2 * n + 2)
                pe.wait_ge(k_lo_done, n)
                for half in range(2):
                    for i, (c, w, r) in enumerate(chunks(wkv_hi, wkv_lo)):
                        last = t.matmul(ps_k[:, half * JM:(half + 1) * JM], w[:, 0, r, half * P:(half + 1) * P], ctxT[:, c, :],
                                        start=(i == 0), stop=(i == 4))
                last.then_inc(k_filled, 1)

            def values(n):
                pe.wait_ge(v_copied, n)
                for jt in range(2):
                    for i, (c, w, r) in enumerate(chunks(wkv_hi, wkv_lo)):
                        last = t.matmul(ps_v[:, jt * D:(jt + 1) * D], ctxT[:, c, jt * P:(jt + 1) * P], w[:, 1, r, :],
                                        start=(i == 0), stop=(i == 4))
                last.then_inc(v_filled, 1)

            def scores(n, k, half):
                if half == 0:
                    pe.wait_ge(k_lo_done, n + 1)
                    pe.wait_ge(k_last_done, n + 1)
                    pe.wait_ge(qd_done, n + 1)
                pe.wait_ge(s_masked, GROUPS * n + 2 * half)
                for i, (qi, ki) in enumerate(((0, 0), (0, 1), (1, 0))):
                    for r in range(2):
                        rs = slice(r * 64, r * 64 + 64)
                        last = t.matmul(ps_s[r][:, 0:J + 1], qd[qi][rs, k, half, :], kT[ki][rs, half, :],
                                        start=(i == 0), stop=(i == 2))
                last.then_inc(s_filled, 1)

            def weigh(T, k):
                n = BT * T + k
                pe.wait_ge(p_copied, 2 * n + 2)
                pe.wait_ge(v_copied, n + 1)
                pe.wait_ge(lastv_in[k], 16 * (T + 1))
                t.matmul(ps_o[:, 0:D], last_probT[:, :], last_v_rows[:, k, :], start=True, stop=False, skip_group_check=True)
                for g in range(GROUPS):
                    for jt in range(2):
                        last = t.matmul(ps_o[:, g * GC:(g + 1) * GC], probT[:, jt, g * P:(g + 1) * P],
                                        v[:, k % 2, jt, g * GC:(g + 1) * GC], start=False,
                                        stop=(g == GROUPS - 1 and jt == 1), skip_group_check=True)
                last.then_inc(o_filled, 1)

            def transpose_probs(n, jt):
                if jt == 0:
                    pe.wait_ge(exp_done, GROUPS * (n + 1))
                    pe.wait_ge(o_done, n)
                    t.transpose(ps_o[0:GROUPS, D:D + P], prob[:, :, JM:J].rearrange("p g o -> p (g o)"), ident[:, :]).then_inc(lastp_filled, 1)
                pe.wait_ge(p_copied, 2 * n + jt)
                for g in range(GROUPS):
                    last = t.transpose(ps_p[:, g * P:(g + 1) * P], prob[:, g, jt * P:(jt + 1) * P], ident[:, :])
                last.then_inc(p_filled, 1)

            def my_turn(T, e):
                pe.wait_ge(m_emptied, turn(T, e))

            def middle(T, k):
                has_q, has_out, has_local = parts(T)
                last = None
                if k == 0 and (has_q or has_local):
                    my_turn(T, 0)
                    if isinstance(T, int) and T < 0:
                        pe.wait_ge(wq_in, 16)
                    if has_q:
                        pe.wait_ge(xn1_done, T + 2)
                        for c in range(2):
                            last = t.transpose(ps_m[:, c * P:(c + 1) * P], xn1[:, c * P:(c + 1) * P], ident[:, :])
                    if has_local:
                        pe.wait_ge(lexp_done, T - 1)
                        last = t.transpose(ps_m[:, 2 * P:3 * P], lprob[:, :], ident[:, :])
                if k == 1 and (has_q or has_local):
                    my_turn(T, 2)
                    if has_q:
                        for half in range(2):
                            for c in range(2):
                                last = t.matmul(ps_m[:, half * P:(half + 1) * P], wq[:, c, half * P:(half + 1) * P],
                                                turned0[:, c * P:(c + 1) * P], start=(c == 0), stop=(c == 1))
                    if has_local:
                        last = t.matmul(ps_m[:, 2 * P:4 * P], turned0[:, 2 * P:3 * P], lv[:, :], start=True, stop=True)
                if k == 2 and (has_out or has_local):
                    my_turn(T, 4)
                    if has_out:
                        pe.wait_ge(xn2_done, T)
                        for c in range(2):
                            last = t.transpose(ps_m[:, c * P:(c + 1) * P], xn2[:, c * P:(c + 1) * P], ident[:, :])
                    if has_local:
                        pe.wait_ge(xn3_done, T - 1)
                        for c in range(2):
                            last = t.transpose(ps_m[:, (2 + c) * P:(3 + c) * P], x3n[:, D + c * P:D + (c + 1) * P], ident[:, :])
                if k == 3 and (has_out or has_local):
                    my_turn(T, 6)
                    if has_out:
                        for c in range(2):
                            last = t.matmul(ps_m[:, 0:D], turned4[:, c * P:(c + 1) * P], lw[:, 2, c, :], start=(c == 0), stop=(c == 1))
                    if has_local:
                        for c in range(2):
                            last = t.matmul(ps_m[:, D:D + E], turned4[:, (2 + c) * P:(3 + c) * P], wr[:, c, :], start=(c == 0), stop=(c == 1))
                if last is not None:
                    last.then_inc(m_filled, 1)

            def end(T, k):
                has_q, has_out, has_local = parts(T)
                if not has_out:
                    return
                my_turn(T, 2 * k + 1)
                if k == 0:
                    if isinstance(T, int) and T == 1:
                        pe.wait_ge(w_in, 16 * 9)
                    pe.wait_ge(o_done, BT * T)
                    for c in range(2):
                        last = t.transpose(ps_m[:, c * P:(c + 1) * P], attn[:, c * P:(c + 1) * P], ident[:, :])
                if k == 1:
                    for c in range(2):
                        last = t.matmul(ps_m[:, 0:D], attnT[:, c, :], wo[:, c, :], start=(c == 0), stop=(c == 1))
                if k == 2:
                    for w in range(4):
                        half = w % 2
                        for c in range(2):
                            last = t.matmul(ps_m[:, w * P:(w + 1) * P], lw[:, w // 2, c, half * P:(half + 1) * P],
                                            turned4[:, c * P:(c + 1) * P], start=(c == 0), stop=(c == 1))
                if k == 3:
                    for c in range(2):
                        last = t.matmul(ps_m[:, 0:P], lqk[:, c, :], lqk[:, 2 + c, :], start=(c == 0), stop=(c == 1))
                last.then_inc(m_filled, 1)

            def last_rows():
                for half in range(2):
                    for c, rows_c in ((0, P), (1, C2)):
                        t.matmul(ps_p[:, half * B:(half + 1) * B], wkv[0:rows_c, 0, c, half * P:(half + 1) * P],
                                 last_ctxT[0:rows_c, c, :], start=(c == 0), stop=(c == 1))
                for c, rows_c in ((0, P), (1, C2)):
                    last = t.matmul(ps_o[0:B, 0:D], last_ctxT[0:rows_c, c, :], wkv[0:rows_c, 1, c, :], start=(c == 0), stop=(c == 1))
                last.then_inc(last_step, 1)

            def iteration(T):
                first = isinstance(T, int) and T < 0
                if first:
                    pe.wait_ge(consts, 6)
                    pe.wait_ge(kv_in, 16 * 7)
                    t.transpose(ps_m[:, 0:B], last_ctx[:, 0:P], ident[0:B, 0:B])
                    t.transpose(ps_m[0:C2, B:2 * B], last_ctx[:, P:C], ident[0:B, 0:B]).then_inc(last_step, 1)
                    transpose_ctx(0, 0, 0)
                    transpose_ctx(0, 0, 1)
                    pe.wait_ge(wkv_split, 2)
                    keys(0)
                    pe.wait_ge(last_copied, 2)
                    middle(T, 0)
                    values(0)
                    middle(T, 1)
                    last_rows()
                    return
                if isinstance(T, int) and T == 0:
                    pe.wait_ge(last_copied, 5)
                for k in range(BT):
                    n = BT * T + k
                    ahead = in_tiles(T) and exists(T, k + 1)
                    Ta, ba = (T, k + 1) if k + 1 < BT else (T + 1, 0)
                    if ahead:
                        transpose_ctx(Ta, ba, 0)
                    if in_tiles(T):
                        scores(n, k, 0)
                    if ahead:
                        transpose_ctx(Ta, ba, 1)
                    if not first and exists(T, k - 1) and not (isinstance(T, int) and BT * T + k > B):
                        weigh(T if k else T - 1, (k - 1) % BT)
                    if in_tiles(T):
                        scores(n, k, 1)
                    middle(T, k)
                    if ahead:
                        keys(n + 1)
                    if in_tiles(T):
                        transpose_probs(n, 0)
                    if ahead:
                        values(n + 1)
                    if in_tiles(T):
                        transpose_probs(n, 1)
                    end(T, k)

            over_tiles(pe, iteration)

            pe.wait_ge(bias_in, 48)
            n_b = E * (F1 + F2) // P
            pe.wait_ge(route, 6)
            n_et = E * TILES
            chosen_flat = chosen_bf[:, :, :].rearrange("p e t -> p (e t)")
            t.matmul(ps_m[:, 0:n_et], before[:, :], chosen_flat, start=True, stop=True)
            t.matmul(ps_m[:, n_et:2 * n_et], ones_bf[:, :], chosen_flat, start=True, stop=True).then_inc(chosen_counted, 1)
            t.transpose(ps_p[:, 0:n_b], bias_rows[:, :], ident[0:n_b, 0:n_b]).then_inc(bias_turned, 1)

            def weight(buffer, at, n):
                return weights[:, bass.ds(buffer, 1), at:at + n].rearrange("p o n -> p (o n)")

            def turn_x(i, run, q):
                pe.wait_ge(slot_in[q], 16 * (run + 1))
                pe.wait_ge(xT_copied, i)
                for c in range(2):
                    last = t.transpose(ps_xT[:, c * P:(c + 1) * P], slot_x[:, q, D + c * P:D + (c + 1) * P], ident[:, :])
                last.then_inc(xT_filled, 1)

            def layer1(i, buffer):
                pe.wait_ge(xT_copied, i + 1)
                for half in range(2):
                    pe.wait_ge(z1_copied[half], i)
                    for c in range(2):
                        last = t.matmul(ps_z1[half][:, :], slot_xT[:, c, :], weight(buffer, c * F1 + half * 512, 512),
                                        start=(c == 0), stop=(c == 1))
                    last.then_inc(z1_filled, 1)

            def turn_z1(i):
                for half in range(2):
                    pe.wait_ge(z1_copied[half], i + 1)
                    pe.wait_ge(h1_done, 2 * i)
                    for c in range(4):
                        f = 4 * half + c
                        last = t.transpose(ps_t1[half][:, c * P:(c + 1) * P], z1[:, f * P:(f + 1) * P], ident[:, :])
                    last.then_inc(t1_filled, 1)

            def layer2(i, buffer):
                pe.wait_ge(z2_copied, i)
                for f in range(F1 // P):
                    if f % 4 == 0:
                        pe.wait_ge(h1_done, 2 * i + f // 4 + 1)
                    last = t.matmul(ps_z2[:, :], h1[:, f, :], weight(buffer, W2_AT + f * F2, F2), start=(f == 0), stop=(f == F1 // P - 1))
                last.then_inc(z2_filled, 1)

            def turn_z2(i):
                pe.wait_ge(z2_copied, i + 1)
                pe.wait_ge(h2_done, i)
                for c in range(F2 // P):
                    last = t.transpose(ps_t2[:, c * P:(c + 1) * P], z2[:, c * P:(c + 1) * P], ident[:, :])
                last.then_inc(t2_filled, 1)

            def layer3(i, buffer):
                pe.wait_ge(h2_done, i + 1)
                pe.wait_ge(y_done, i)
                for c in range(F2 // P):
                    last = t.matmul(ps_y[:, 0:D], h2[:, c, :], weight(buffer, W3_AT + c * D, D), start=(c == 0), stop=(c == F2 // P - 1))
                last.then_inc(y_filled, 1)

            def expert_of(i):
                return pe.value_load(slot_expert_int[0:1, bass.ds(i, 1)], min_val=0, max_val=E - 1)

            def buffer_of(i):
                return pe.value_load(slot_buffer_int[0:1, bass.ds(i, 1)], min_val=0, max_val=BUFFERS - 1)

            pe.wait_ge(route, ROUTED)
            experts, buffers = [expert_of(i) for i in range(2)], [buffer_of(i) for i in range(2)]
            turn_x(0, 0, 0)
            pe.wait_ge(expert_ready, experts[0] + 1)
            layer1(0, buffers[0])
            turn_x(1, 0, 1)
            turn_z1(0)
            pe.wait_ge(expert_ready, experts[1] + 1)
            layer1(1, buffers[1])

            def slot(i, run, q):
                buffer = buffer_of(i)
                if follows(i, 2):
                    ahead_expert, ahead_buffer = expert_of(i + 2), buffer_of(i + 2)
                layer2(i, buffer)
                if follows(i, 2):
                    turn_x(i + 2, run + (q + 2) // AHEAD, (q + 2) % AHEAD)
                if follows(i, 1):
                    turn_z1(i + 1)
                turn_z2(i)
                if follows(i, 2):
                    pe.wait_ge(expert_ready, ahead_expert + 1)
                    layer1(i + 2, ahead_buffer)
                layer3(i, buffer)

            over_slots(pe, slot)


_INS = ['x', 'ctx_768', 'mask_BxS2_bf1', 'L0_xattn_Wq', 'L0_xattn_Wk', 'L0_xattn_Wv', 'L0_xattn_Wo',
        'L0_attn_Wq', 'L0_attn_bq', 'L0_attn_Wk', 'L0_attn_bk', 'L0_attn_Wv', 'L0_attn_bv',
        'L0_ffn_Wr', 'L0_ffn_br', 'L0_ffn_W1', 'L0_ffn_b1', 'L0_ffn_W2', 'L0_ffn_b2', 'L0_ffn_W3', 'L0_ffn_b3']
_OUTS = [((64, 32, 256), 'float32')]


def kernel(**inputs):
    import numpy as _np
    import concourse.bacc as _bacc
    from concourse import mybir as _mybir
    from concourse.bass_utils import run_bass_kernel_spmd as _run

    nc = _bacc.Bacc("TRN2", target_bir_lowering=False, num_devices=1)
    arrays, args = {}, []
    for name in _INS:
        a = _np.ascontiguousarray(inputs[name])
        if a.dtype == _np.bool_:
            a = a.view(_np.uint8)
        arrays[f"in_{name}_dram"] = a
        args.append(nc.dram_tensor(f"in_{name}_dram", a.shape, _mybir.dt.from_np(a.dtype), kind="ExternalInput").ap())
    for i, (shape, dtype) in enumerate(_OUTS):
        dt = _mybir.dt.from_np(_np.dtype(dtype))
        args.append(nc.dram_tensor(f"out_{i}_dram", shape, dt, kind="ExternalOutput").ap())
    perceiver_kernel(nc, *args)
    r = _run(nc, [arrays], core_ids=[0])
    got = tuple(r.results[0][f"out_{i}_dram"] for i in range(len(_OUTS)))
    return got[0]
```

```python
import math
from contextlib import ExitStack

import concourse.bass as bass
from concourse import mybir

F32 = mybir.dt.float32
F32R = mybir.dt.float32r
BF16 = mybir.dt.bfloat16
I32 = mybir.dt.int32
U8 = mybir.dt.uint8
ACT = mybir.ActivationFunctionType
ALU = mybir.AluOpType
AX = mybir.AxisListType

P = 128
EPS = 1e-5
MASKED = -1.0e30


def perceiver_kernel(nc, x, ctx_768, mask, Wq, Wk, Wv, Wo, lWq, lbq, lWk, lbk, lWv, lbv,
                     Wr, br, W1, b1, W2, b2, W3, b3, out):
    B, S, D = x.shape
    J, C = ctx_768.shape[1:]
    HEADS, HD = 16, D // 16
    GROUPS = HEADS * S // P
    HG = HEADS // GROUPS
    GC = HG * HD
    BT = P // S
    TILES = B * S // P
    C2 = C - P
    JM = J - 1
    E = Wr.shape[1]

    F1, F2 = W1.shape[2], W2.shape[2]
    SLOTS = (B * S + E * (P - 1)) // P
    AHEAD = 5
    ROW = 2 * D
    N_TOKENS = B * S
    COLS1, COLS23 = D // P * F1, F1 // P * F2 + F2 // P * D
    W3_AT = F1 // P * F2
    BUFFERS1, BUFFERS23 = 3, 2
    HI, LO = 0, 1

    x_rows = x.rearrange("b s d -> (b s) d")
    out_rows = out.rearrange("b s d -> (b s) d")

    with ExitStack() as stack:
        address = {}

        def sb(name, shape, dt=F32):
            address[name] = -(-nc.sbuf_base // 32) * 32
            return stack.enter_context(nc.sbuf_tensor(name, shape, dt))

        def over(name, place, at, shape, dt=F32):
            return nc.alloc_sbuf_tensor_at(name, shape, dt, offset=address[place] + 4 * at, align_bytes=4)

        def sem(name):
            return stack.enter_context(nc.semaphore(name))

        def bank(name):
            return stack.enter_context(nc.psum_tensor(name, [P, 512], F32))

        ps_ctx = bank("ps_ctx")
        ps_k = bank("ps_k")
        ps_v = bank("ps_v")
        ps_s = [bank("ps_s0"), bank("ps_s1")]
        ps_p = bank("ps_p")
        ps_o = bank("ps_o")
        ps_m = bank("ps_m")

        sb("area", [P, 2 * (BUFFERS1 * COLS1 + BUFFERS23 * COLS23)])
        at23 = 2 * BUFFERS1 * COLS1
        w1 = over("w1", "area", 0, [P, BUFFERS1, 2, COLS1], F32R)
        w23 = over("w23", "area", at23, [P, BUFFERS23, 2, COLS23], F32R)
        w1_raw = over("w1_raw", "area", 0, [P, BUFFERS1, 2, COLS1])[:, :, LO, :]
        w23_raw = over("w23_raw", "area", at23, [P, BUFFERS23, 2, COLS23])[:, :, LO, :]

        def place1(b, part):
            return (2 * b + part) * COLS1

        def place23(b, part):
            return at23 + (2 * b + part) * COLS23

        ident = sb("ident", [P, P])
        ident_r = sb("ident_r", [P, P], F32R)
        head_blocks = sb("head_blocks", [P, 8])
        head_mask = sb("head_mask", [P, HG])
        band = sb("band", [P, P])
        neg_half = sb("neg_half", [P, 1])
        lw = over("lw", "area", place23(0, HI), [P, 3, 2, D])
        wq = over("wq", "area", place23(0, HI) + 6 * D, [P, 2, D])
        wo = over("wo", "area", place1(1, HI), [P, 2, D])
        wr = sb("wr", [P, 2, E])
        lbias = sb("lbias", [P, 4])
        bv_rows = sb("bv_rows", [P, D])
        br_rows = sb("br_rows", [P, E])
        wkv = over("wkv", "area", place23(0, HI) + 8 * D, [P, 2, 2, D])
        wkv_hi = over("wkv_hi", "area", place23(0, HI) + 12 * D, [P, 2, 2, D], F32R)
        wkv_lo = over("wkv_lo", "area", place23(0, HI) + 16 * D, [P, 2, 2, D], F32R)

        last_ctx = sb("last_ctx", [B, C])
        last_ctxT = sb("last_ctxT", [P, 2, B])
        last_k = [sb("last_k_hi", [P, 2, B], F32R), sb("last_k_lo", [P, 2, B], F32R)]
        last_v_dram = nc.dram_tensor("last_v_dram", (B, GROUPS, D), F32, kind="Internal").ap()

        ctx_raw = over("ctx_raw", "area", place1(0, HI), [P, BT, 2, C])
        mask_bytes = sb("mask_bytes", [B, J], U8)
        mask_rows = sb("mask_rows", [B, J])
        mask_dram = nc.dram_tensor("mask_dram", (B, J), F32, kind="Internal").ap()
        ctx_split = over("ctx_split", "area", place1(2, HI), [P, BT, 2, 3 * P], F32R)
        ctxT = sb("ctxT", [P, 3, 2 * P], F32R)
        kT = [sb("kT_hi", [P, 2, J + 1], F32R), sb("kT_lo", [P, 2, J + 1], F32R)]
        v = sb("v", [P, 2, 2, D])
        mask_add = over("mask_add", "area", place1(1, HI) + 2 * D, [P, BT, J])
        xt = sb("xt", [P, D])
        xn1 = sb("xn1", [P, D])
        turned0 = over("turned0", "area", place1(1, HI) + 2 * D + BT * J, [P, 3 * P])
        q = [sb("q_hi", [P, 2, P], F32R), sb("q_lo", [P, 2, P], F32R)]
        qd_parts = sb("qd_parts", [P, 2, BT, 2, P], F32R)
        qd = [qd_parts[:, i, :, :, :] for i in range(2)]
        prob = sb("prob", [P, GROUPS, J])
        neg_max = sb("neg_max", [P, GROUPS])
        row_sum = sb("row_sum", [P, 2, GROUPS])
        row_inv = sb("row_inv", [P, GROUPS])
        probT = over("probT", "area", place1(2, HI) + BT * 6 * P, [P, 2, GROUPS * P])
        last_probT = sb("last_probT", [GROUPS, P])
        last_v_place = sb("last_v_place", [P, BT, D])
        last_v_rows = last_v_place[0:GROUPS, :, :]
        attn = sb("attn", [P, D])

        attnT = sb("attnT", [P, 2, P])
        xr = sb("xr", [P, D])
        x2 = sb("x2", [P, D])
        xn2 = sb("xn2", [P, D])
        turned4 = over("turned4", "area", place1(0, HI) + BT * 2 * C, [P, 4 * P])
        lqk = sb("lqk", [P, 4, P])
        lv = sb("lv", [P, D])
        lprob = sb("lprob", [P, P])
        lneg_max = sb("lneg_max", [P, 1])
        lrow_sum = sb("lrow_sum", [P, 1])
        lrow_inv = sb("lrow_inv", [P, 1])
        x3n = sb("x3n", [P, 2 * D])
        rows_dram = nc.dram_tensor("rows_dram", (N_TOKENS, ROW), F32, kind="Internal").ap()
        last_v = over("last_v", "area", place23(1, HI), [P, GROUPS, D])[0:B, :, :]
        logits = sb("logits", [P, E, TILES])
        stats = [sb(f"stats{i}", [P, 6]) for i in range(3)]
        moments = [sb(f"moments{i}", [P, 2]) for i in range(3)]
        var_eps = [sb(f"var_eps{i}", [P, 1]) for i in range(3)]
        rstd = [sb(f"rstd{i}", [P, 1]) for i in range(3)]

        row_number = sb("row_number", [P, P])
        token_row = sb("token_row", [P, 1])
        tile_base = sb("tile_base", [P, TILES])
        before = sb("before", [P, P], BF16)
        ones_bf = sb("ones_bf", [P, P], BF16)
        expert_rank = sb("expert_rank", [P, E])
        slot_number = sb("slot_number", [P, SLOTS])
        restart = sb("restart", [P, E, TILES])
        ones_row = sb("ones_row", [P, E])
        top = sb("top", [P, TILES])
        tied = sb("tied", [P, E, TILES])
        first = sb("first", [P, TILES])
        chosen = sb("chosen", [P, E, TILES])
        chosen_bf = sb("chosen_bf", [P, E, TILES], BF16)
        tile_counts = sb("tile_counts", [P, E, TILES])
        counts = sb("counts", [P, E, TILES])
        padded = sb("padded", [P, E], I32)
        slots_int = sb("slots_int", [P, E], I32)
        slots = sb("slots", [P, E])
        slot_end = sb("slot_end", [P, E])
        slot_start = sb("slot_start", [P, E])
        place = sb("place", [P, E, TILES])
        target = sb("target", [P, TILES])
        target_int = sb("target_int", [P, TILES], I32)
        past = sb("past", [P, SLOTS, E])
        slot_expert = sb("slot_expert", [P, SLOTS])
        slot_expert_int = sb("slot_expert_int", [P, SLOTS], I32)
        slot_end_int = sb("slot_end_int", [P, E], I32)
        part_int = sb("part_int", [P, 2, TILES], I32)
        part_of = sb("part_of", [P, 2, TILES])
        at_routing = place23(1, HI) + GROUPS * D
        in_slot = over("in_slot", "area", at_routing, [P, TILES, SLOTS])
        in_slot_tokens = over("in_slot_tokens", "area", at_routing + TILES * SLOTS, [P, TILES, 2, SLOTS], BF16)
        in_row = over("in_row", "area", at_routing + 2 * TILES * SLOTS, [P, TILES, P], BF16)
        slot_token = sb("slot_token", [P, SLOTS])
        slot_empty = sb("slot_empty", [P, SLOTS])
        slot_ids = sb("slot_ids", [P, SLOTS + 1, 2], I32)

        bias_rows = sb("bias_rows", [E * (F1 + F2) // P, P])
        bias_cols = sb("bias_cols", [P, E * (F1 + F2) // P])
        slot_x = sb("slot_x", [P, AHEAD, ROW])
        slot_id = sb("slot_id", [P, AHEAD, 2], I32)
        y = sb("y", [P, AHEAD, D])
        h1_hi = sb("h1_hi", [P, F1 // P, P], F32R)
        b3_rows = over("b3_rows", "qd_parts", 0, [P, E, D])
        xT_parts = [over("xT_hi", "attn", 0, [P, 2, P], F32R), over("xT_lo", "lv", 0, [P, 2, P], F32R)]
        xT_raw = over("xT_raw", "lv", 0, [P, 2, P])
        z1 = prob[:, :, :].rearrange("p g j -> p (g j)")
        h1 = v[:, :, :, :].rearrange("p k t d -> p (k t d)").rearrange("p (f s) -> p f s", s=P)
        z2 = lqk[:, :, :].rearrange("p w s -> p (w s)")
        h1_parts = [h1_hi, over("h1_lo", "last_v_place", 0, [P, F1 // P, P], F32R)]
        h2 = x3n[:, :].rearrange("p (f s) -> p f s", s=P)
        h2_parts = [part[:, :, :].rearrange("p c j -> p (c j)")[:, 0:F2].rearrange("p (f s) -> p f s", s=P) for part in kT]
        ps_z1 = [ps_ctx, ps_k]
        ps_t1 = [ps_v, ps_s[0]]
        ps_z2, ps_t2, ps_y, ps_xT = ps_s[1], ps_p, ps_o, ps_m

        router_consts = sem("router_consts")
        route = sem("route")
        chosen_counted = sem("chosen_counted")
        rows_matched = sem("rows_matched")
        tokens_found = sem("tokens_found")
        ids_copied = sem("ids_copied")
        w1_in = [sem(f"w1_in{i}") for i in range(BUFFERS1)]
        w23_in = [[sem(f"w23_in{i}_{piece}") for piece in range(3)] for i in range(BUFFERS23)]
        rounded = sem("rounded")
        w1_ready = sem("w1_ready")
        w23_ready = sem("w23_ready")
        b3_in = sem("b3_in")
        bias_in = sem("bias_in")
        bias_turned = sem("bias_turned")
        bias_done = sem("bias_done")
        slot_in = [sem(f"slot_in{i}") for i in range(AHEAD)]
        xT_filled = sem("xT_filled")
        xT_hi_done = sem("xT_hi_done")
        xT_copied = sem("xT_copied")
        xT_done = sem("xT_done")
        z1_filled = sem("z1_filled")
        z1_copied = sem("z1_copied")
        t1_filled = sem("t1_filled")
        gelu1_done = sem("gelu1_done")
        h1_hi_done = sem("h1_hi_done")
        h1_done = sem("h1_done")
        z2_filled = sem("z2_filled")
        z2_copied = sem("z2_copied")
        t2_filled = sem("t2_filled")
        gelu2_done = sem("gelu2_done")
        h2_hi_done = sem("h2_hi_done")
        h2_done = sem("h2_done")
        residual_done = sem("residual_done")
        y_filled = sem("y_filled")
        y_copied = sem("y_copied")
        y_done = sem("y_done")
        y_stored = [sem(f"y_stored{i}") for i in range(AHEAD)]
        w_in = sem("w_in")
        wq_in = sem("wq_in")
        kv_in = sem("kv_in")
        consts = sem("consts")
        zeroed = sem("zeroed")
        wkv_split = sem("wkv_split")
        last_step = sem("last_step")
        last_copied = sem("last_copied")
        last_stored = sem("last_stored")
        x_in = sem("x_in")
        xr_in = sem("xr_in")
        ctx_in = [sem(f"ctx_in{i}") for i in range(BT)]
        lastv_in = [sem(f"lastv_in{i}") for i in range(BT)]
        split_hi = sem("split_hi")
        split_done = sem("split_done")
        mask_bytes_in = sem("mask_bytes_in")
        mask_done = sem("mask_done")
        mask_stored = sem("mask_stored")
        mask_in = [sem(f"mask_in{i}") for i in range(BT)]
        ctxT_filled = sem("ctxT_filled")
        ctxT_copied = sem("ctxT_copied")
        k_filled = sem("k_filled")
        k_hi_done = sem("k_hi_done")
        k_lo_done = sem("k_lo_done")
        k_last_done = sem("k_last_done")
        v_filled = sem("v_filled")
        v_copied = sem("v_copied")
        q_hi_done = sem("q_hi_done")
        qd_done = sem("qd_done")
        s_filled = sem("s_filled")
        s_masked = sem("s_masked")
        exp_done = sem("exp_done")
        lastp_filled = sem("lastp_filled")
        p_filled = sem("p_filled")
        p_copied = sem("p_copied")
        o_filled = sem("o_filled")
        inv_done = sem("inv_done")
        o_done = sem("o_done")
        m_filled = sem("m_filled")
        m_emptied = sem("m_emptied")
        xn1_done = sem("xn1_done")
        xn2_done = sem("xn2_done")
        xn3_done = sem("xn3_done")
        rows_done = sem("rows_done")
        linv_done = sem("linv_done")
        lexp_done = sem("lexp_done")
        ln_stats = [sem(f"ln_stats{i}") for i in range(3)]
        ln_moments = [sem(f"ln_moments{i}") for i in range(3)]
        ln_eps = [sem(f"ln_eps{i}") for i in range(3)]
        ln_rstd = [sem(f"ln_rstd{i}") for i in range(3)]
        waits_ended = sem("waits_ended")
        out_stored = sem("out_stored")

        def alone(eng):
            eng.sem_inc(waits_ended, 1)

        def turn(T, e):
            if isinstance(T, int) and T < 1:
                return 2 * (T + 1) + {0: 0, 2: 1}[e]
            if isinstance(T, int) and T == TILES + 1:
                return 8 * T - 4 + e // 2
            return 8 * T - 4 + e

        def parts(T):
            if not isinstance(T, int):
                return True, True, True
            return T + 1 < TILES, 1 <= T <= TILES, 2 <= T <= TILES + 1

        def over_tiles(eng, iteration):
            for T in (-1, 0, 1):
                iteration(T)
            with eng.Fori(2, TILES - 1) as T:
                iteration(T)
            for T in (TILES - 1, TILES, TILES + 1):
                iteration(T)

        def in_tiles(T):
            return not isinstance(T, int) or 0 <= T < TILES

        def exists(T, k):
            return not isinstance(T, int) or 0 <= BT * T + k < B

        def over_slots(eng, step):
            for q in range(AHEAD):
                step(q, 0, q)
            with eng.Fori(1, SLOTS // AHEAD) as run:
                for q in range(AHEAD):
                    step(AHEAD * run + q, run, q)
            for i in range(SLOTS // AHEAD * AHEAD, SLOTS):
                step(i, i // AHEAD, i % AHEAD)

        def follows(i, n):
            return not isinstance(i, int) or i + n < SLOTS

        def last_but_one(i):
            return follows(i, 1) and not follows(i, 2)

        def before_by(n, i, run, q):
            if isinstance(i, int) and i < n:
                return None
            return (run, q - n) if q >= n else (run - 1, q - n + AHEAD)

        def flat3(ap):
            return ap.rearrange("p c s -> p (c s)")

        MAPPED, ROUTED = 25, 29
        PIECES = (slice(0, W3_AT // 2), slice(W3_AT // 2, W3_AT), slice(W3_AT, COLS23))
        EARLY = [(True, 0), (False, 0), (True, 1), (False, 1)]
        LATE = [(True, 2)]
        for e in range(2, E):
            LATE += [(True, e + 1)] * (e + 1 < E) + [(False, e)]
        block = stack.enter_context(nc.Block())

        @block.sync
        def _(sp):
            def load_ctx(T, b):
                n = BT * T + b
                sp.dma_start(ctx_raw[:, b, :, :], ctx_768[n, 0:JM, :].rearrange("(p t) c -> p t c", t=2)).then_inc(ctx_in[b], 16)

            def load_mask(T, b):
                sp.dma_start(mask_add[:, b, :], mask_dram[bass.ds(BT * T + b, 1), :].to_broadcast([P, J])).then_inc(mask_in[b], 16)

            def load_last_v(T, b):
                sp.dma_start(last_v_rows[:, b, :], last_v_dram[BT * T + b]).then_inc(lastv_in[b], 16)

            def load_x(dst, T, s):
                sp.dma_start(dst[:, :], x_rows.rearrange("(t p) d -> t p d", p=P)[T]).then_inc(s, 16)

            load_x(xt, 0, x_in)
            load_ctx(0, 0)
            sp.dma_start(last_ctx[:, :], ctx_768[:, JM, :]).then_inc(kv_in, 16)
            for i, w in enumerate((Wk, Wv)):
                sp.dma_start(wkv[:, i, 0, :], w[0:P, :]).then_inc(kv_in, 16)
                sp.dma_start(wkv[0:C2, i, 1, :], w[P:C, :]).then_inc(kv_in, 16)
                sp.dma_start(wkv[C2:P, i, 1, :], w[P:C, :]).then_inc(kv_in, 16)
            sp.dma_start(wq[:, :, :], Wq.rearrange("(c p) n -> p c n", p=P)).then_inc(wq_in, 16)
            sp.dma_start(mask_bytes[:, :], mask).then_inc(mask_bytes_in, 16)
            for b in range(1, BT):
                load_ctx(0, b)
            sp.wait_ge(mask_done, 2)
            sp.dma_start(mask_dram, mask_rows[:, :]).then_inc(mask_stored, 16)
            for dst, w in ((wo, Wo), (wr, Wr)):
                sp.dma_start(dst[:, :, :], w.rearrange("(c p) n -> p c n", p=P)).then_inc(w_in, 16)
            sp.wait_ge(mask_stored, 16)
            for b in range(BT):
                load_mask(0, b)
            for i, w in enumerate((lWq, lWk, lWv)):
                sp.dma_start(lw[:, i, :, :], w.rearrange("(c p) n -> p c n", p=P)).then_inc(w_in, 16)
            for i, w in enumerate((lbq, lbk)):
                sp.dma_start(lbias[:, 2 * i:2 * i + 2], w.rearrange("(c p) -> p c", p=P), allow_slow_non_contiguous=True).then_inc(w_in, 16)
            sp.dma_start(bv_rows[:, :], lbv.rearrange("(o n) -> o n", o=1).to_broadcast([P, D])).then_inc(w_in, 16)
            sp.dma_start(br_rows[:, :], br.rearrange("(o n) -> o n", o=1).to_broadcast([P, E])).then_inc(w_in, 16)

            def ahead(T):
                sp.wait_ge(xn1_done, T)
                load_x(xt, T, x_in)
                for b in range(BT):
                    n = BT * (T - 1) + b
                    if isinstance(T, int) and T == 1:
                        if b == 0:
                            sp.wait_ge(last_copied, 5)
                            sp.dma_start(last_v_dram, last_v[:, :, :]).then_inc(last_stored, 16)
                            sp.wait_ge(last_stored, 16)
                    else:
                        sp.wait_ge(o_filled, BT * (T - 2) + b + 1)
                    load_last_v(T - 1, b)
                    sp.wait_ge(split_done, n + 1)
                    load_ctx(T, b)
                    sp.wait_ge(s_masked, GROUPS * (n + 1))
                    load_mask(T, b)
                    if b == 1 and not (isinstance(T, int) and T == 1):
                        sp.wait_ge(m_emptied, turn(T - 2, 3) + 1)
                        load_x(xr, T - 2, xr_in)
            ahead(1)
            sp.dma_start(bias_rows[0:E * F1 // P, :], b1.rearrange("e (c p) -> (e c) p", p=P)).then_inc(bias_in, 16)
            sp.dma_start(bias_rows[E * F1 // P:, :], b2.rearrange("e (c p) -> (e c) p", p=P)).then_inc(bias_in, 16)
            with sp.Fori(2, TILES) as T:
                ahead(T)
            for b in range(BT):
                sp.wait_ge(o_filled, BT * (TILES - 2) + b + 1)
                load_last_v(TILES - 1, b)
            for T in (TILES - 2, TILES - 1):
                sp.wait_ge(m_emptied, turn(T, 3) + 1)
                load_x(xr, T, xr_in)

            def load_first(e):
                sp.dma_start(w1_raw[:, e % BUFFERS1, :].rearrange("p (k n) -> p k n", n=F1),
                             W1[e].rearrange("(k p) n -> p k n", p=P)).then_inc(w1_in[e % BUFFERS1], 16)

            def load_other(e, piece):
                b, w, n = e % BUFFERS23, W2 if piece < 2 else W3, F2 if piece < 2 else D
                rows_of = slice(piece * F1 // 2, (piece + 1) * F1 // 2) if piece < 2 else slice(0, F2)
                sp.dma_start(w23_raw[:, b, PIECES[piece]].rearrange("p (k n) -> p k n", n=n),
                             w[e][rows_of, :].rearrange("(k p) n -> p k n", p=P)).then_inc(w23_in[b][piece], 16)

            for first_matrix, e in EARLY:
                if first_matrix:
                    load_first(e)
                else:
                    for piece in range(3):
                        load_other(e, piece)
            for q in range(AHEAD):
                sp.wait_ge(slot_in[q], 16)
            sp.dma_start(b3_rows.rearrange("p e d -> p (e d)"),
                         b3.rearrange("(o e) d -> o (e d)", o=1).to_broadcast([P, E * D])).then_inc(b3_in, 16)
            sp.wait_ge(route, ROUTED)
            for first_matrix, e in LATE:
                before = e - (BUFFERS1 if first_matrix else BUFFERS23)
                last_slot = sp.value_load(slot_end_int[0:1, before:before + 1], min_val=1, max_val=SLOTS) if before >= 0 else None
                if first_matrix:
                    if before >= 0:
                        sp.wait_ge(z1_filled, 2 * last_slot)
                    load_first(e)
                else:
                    for piece in range(3):
                        if before >= 0 and piece == 0:
                            sp.wait_ge(z2_filled, last_slot)
                        if before >= 0 and piece == 2:
                            sp.wait_ge(y_filled, last_slot)
                        load_other(e, piece)
            for q in range(AHEAD):
                sp.wait_ge(y_stored[q], 16 * len(range(q, SLOTS, AHEAD)))

        @block.gpsimd
        def _(pool):
            g = nc.gpsimd
            g.memset(ident[:, :], 0.0).then_inc(zeroed, 1)
            g.memset(head_blocks[:, :], 1.0).then_inc(zeroed, 1)
            g.memset(band[:, :], 0.0).then_inc(zeroed, 1)
            g.memset(neg_half[:, :], -0.5).then_inc(consts, 1)
            for i in range(2):
                g.memset(kT[i][:, :, JM:J + 1].bitcast(F32), 0.0).then_inc(consts, 1)
            pool.wait_ge(zeroed, 3)
            g.affine_select(out=ident[:, :], in_=ident[:, :], compare_op=ALU.not_equal, fill=1.0, base=0,
                            pattern=[[-1, P]], channel_multiplier=1).then_inc(consts, 1)
            pool.wait_ge(consts, 4)
            g.tensor_copy(ident_r[:, :], ident[:, :]).then_inc(consts, 1)
            g.affine_select(out=head_blocks[:, :], in_=head_blocks[:, :], compare_op=ALU.is_ge, fill=0.0, base=0,
                            pattern=[[-HD, 8]], channel_multiplier=1).then_inc(zeroed, 1)
            pool.wait_ge(zeroed, 4)
            g.affine_select(out=head_blocks[:, :], in_=head_blocks[:, :], compare_op=ALU.is_ge, fill=0.0, base=HD - 1,
                            pattern=[[HD, 8]], channel_multiplier=-1).then_inc(zeroed, 1)
            pool.wait_ge(zeroed, 5)
            g.tensor_tensor(head_mask[:, :], head_blocks[:, 0:HG], head_blocks[:, HG:2 * HG], ALU.add).then_inc(consts, 1)
            n = 5
            for base, mult, pattern in ((2, 1, [[-1, P]]), (2, -1, [[1, P]]),
                                        (0, 1, [[-S, BT], [0, S]]), (S - 1, -1, [[S, BT], [0, S]])):
                view = band[:, :] if len(pattern) == 1 else band[:, :].rearrange("p (a b) -> p a b", b=S)
                g.affine_select(out=view, in_=view, compare_op=ALU.is_ge, fill=MASKED, base=base,
                                pattern=pattern, channel_multiplier=mult).then_inc(zeroed, 1)
                n += 1
                pool.wait_ge(zeroed, n)
            g.memset(last_v[:, :, :], 0.0).then_inc(consts, 1)
            def prepare_routing():
                g.iota(expert_rank[:, :], pattern=[[-1, E]], base=E, channel_multiplier=0,
                       allow_small_or_imprecise_dtypes=True).then_inc(router_consts, 1)
                g.iota(slot_number[:, :], pattern=[[1, SLOTS]], base=0, channel_multiplier=0,
                       allow_small_or_imprecise_dtypes=True).then_inc(router_consts, 1)
                g.memset(ones_row[:, :], 1.0).then_inc(router_consts, 1)
                g.memset(ones_bf[:, :], 1.0).then_inc(router_consts, 1)
                g.memset(restart[:, :, 0:1], 0.0).then_inc(router_consts, 1)
                g.memset(restart[:, :, 1:TILES], 1.0).then_inc(router_consts, 1)
                pool.wait_ge(router_consts, 6)
                g.affine_select(out=before[:, :], in_=ones_bf[:, :], compare_op=ALU.is_gt, fill=0.0, base=0,
                                pattern=[[1, P]], channel_multiplier=-1).then_inc(router_consts, 1)
                g.iota(row_number[:, :], pattern=[[1, P]], base=0, channel_multiplier=0,
                       allow_small_or_imprecise_dtypes=True).then_inc(router_consts, 1)
                g.iota(token_row[:, :], pattern=[[0, 1]], base=1, channel_multiplier=1,
                       allow_small_or_imprecise_dtypes=True).then_inc(router_consts, 1)
                g.iota(tile_base[:, :], pattern=[[P, TILES]], base=0, channel_multiplier=0,
                       allow_small_or_imprecise_dtypes=True).then_inc(router_consts, 1)
                g.memset(slot_ids[:, SLOTS:SLOTS + 1, :], 0).then_inc(router_consts, 1)

            def split_ctx(T, b):
                n = BT * T + b
                pool.wait_ge(split_hi, n + 1)
                g.tensor_tensor(ctx_split[:, b, :, C:2 * P], ctx_raw[:, b, :, P:C],
                                ctx_split[:, b, :, P:C].bitcast(F32), ALU.subtract)
                g.tensor_tensor(ctx_split[:, b, :, 2 * P:3 * P], ctx_raw[:, b, :, 0:P],
                                ctx_split[:, b, :, 0:P].bitcast(F32), ALU.subtract).then_inc(split_done, 1)

            def place_queries(b):
                for i in range(2):
                    last = g.tensor_tensor(
                        qd[i][:, b, :, :].rearrange("p c (h s) -> p c h s", h=HG),
                        q[i][:, :, b * S:(b + 1) * S].bitcast(F32).unsqueeze(2).to_broadcast([P, 2, HG, S]),
                        head_mask[:, :].unsqueeze(1).unsqueeze(3).to_broadcast([P, 2, HG, S]), ALU.mult)
                last.then_inc(qd_done, 1)

            def scale_of(i, t):
                pool.wait_ge(ln_moments[i], t + 1)
                alone(pool)
                g.tensor_scalar(var_eps[i][:, :], moments[i][:, 1:2], EPS, None, ALU.add).then_inc(ln_eps[i], 1)
                pool.wait_ge(ln_eps[i], t + 1)
                g.tensor_tensor(rstd[i][:, :], var_eps[i][:, :], neg_half[:, :], ALU.pow).then_inc(ln_rstd[i], 1)

            def iteration(T):
                has_q, has_out, has_local = parts(T)
                if isinstance(T, int) and T < 0:
                    scale_of(0, 0)
                    split_ctx(0, 0)
                    pool.wait_ge(mask_bytes_in, 16)
                    g.tensor_scalar(mask_rows[:, 0:JM].rearrange("b (t m) -> b t m", t=2),
                                    mask_bytes[:, 0:JM].rearrange("b (m t) -> b t m", t=2),
                                    1.0, -MASKED, ALU.subtract, ALU.mult).then_inc(mask_done, 1)
                    g.tensor_scalar(mask_rows[:, JM:J], mask_bytes[:, JM:J], 1.0, -MASKED,
                                    ALU.subtract, ALU.mult).then_inc(mask_done, 1)
                    for b in range(1, BT):
                        split_ctx(0, b)
                for k in range(BT):
                    n = BT * T + k
                    if k == 0 and has_q and in_tiles(T):
                        scale_of(0, T + 1)
                    if k == 2 and has_local:
                        scale_of(2, T - 2)
                    if k == 2 and has_out:
                        scale_of(1, T - 1)
                    if in_tiles(T) and exists(T, k + 1):
                        pool.wait_ge(s_filled, 2 * n + 2)
                        alone(pool)
                        for i in range(2):
                            last = g.tensor_copy(kT[i][:, :, JM:J], last_k[i][:, :, bass.ds(n + 1, 1)])
                        last.then_inc(k_last_done, 1)
                    if has_q and k >= 1:
                        if k == 1:
                            pool.wait_ge(m_emptied, turn(T, 2) + 1)
                        for b in range(0 if k == 1 else k, k + 1):
                            if in_tiles(T):
                                pool.wait_ge(s_filled, 2 * (BT * T + b) + 2)
                            place_queries(b)
                    if in_tiles(T) and has_q:
                        split_ctx(T + 1, k)
                    if isinstance(T, int) and T < 0 and k == 1:
                        pool.wait_ge(last_copied, 4)
                        for i in range(2):
                            last = g.tensor_copy(kT[i][:, :, JM:J], last_k[i][:, :, 0:1])
                        last.then_inc(k_last_done, 1)
                if isinstance(T, int) and T == 0:
                    prepare_routing()

            over_tiles(pool, iteration)

            def ids_of(i, q):
                return slot_ids[:, i, :] if isinstance(i, int) and i < AHEAD else slot_id[:, q, :]

            def gather_slot(i, run, q):
                if not (isinstance(i, int) and i < AHEAD):
                    pool.wait_ge(y_stored[q], 16 * run)
                    alone(pool)
                    g.tensor_copy(slot_id[:, q, :], slot_ids[:, bass.ds(i, 1), :].rearrange("p o w -> p (o w)")).then_inc(ids_copied, 1)
                    pool.wait_ge(ids_copied, i - AHEAD + 1)
                    alone(pool)
                g.indirect_dma_start(out=slot_x[:, q, :], out_offset=None, in_=rows_dram,
                                     in_offset=bass.IndirectOffsetOnAxis(ap=ids_of(i, q)[:, 0:1], axis=0),
                                     bounds_check=N_TOKENS - 1, oob_is_err=False).then_inc(slot_in[q], 16)

            pool.wait_ge(rows_done, 16 * TILES)
            pool.wait_ge(route, MAPPED)
            for i in range(AHEAD):
                gather_slot(i, 0, i)
            pool.wait_ge(route, ROUTED)

            def lo_xT(i):
                pool.wait_ge(xT_hi_done, i + 1)
                pool.wait_ge(xT_copied, i + 1)
                g.tensor_tensor(flat3(xT_parts[LO]), flat3(xT_raw[:, :, :]), flat3(xT_parts[HI]).bitcast(F32),
                                ALU.subtract).then_inc(xT_done, 1)

            def lo_h1(i):
                for half in range(2):
                    fs = slice(half * F1 // P // 2, (half + 1) * F1 // P // 2)
                    pool.wait_ge(h1_hi_done, 2 * i + half + 1)
                    g.tensor_tensor(h1_parts[LO][:, fs, :], h1[:, fs, :], h1_parts[HI][:, fs, :].bitcast(F32), ALU.subtract).then_inc(h1_done, 1)

            def lo_h2(i):
                pool.wait_ge(h2_hi_done, i + 1)
                g.tensor_tensor(h2_parts[LO], h2, h2_parts[HI].bitcast(F32), ALU.subtract).then_inc(h2_done, 1)

            def add_bias(i, run, q):
                if isinstance(i, int) and i == 0:
                    pool.wait_ge(b3_in, 16)
                pool.wait_ge(slot_in[q], 16 * (run + 1))
                alone(pool)
                e = pool.value_load(slot_expert_int[0:1, bass.ds(i, 1)], min_val=0, max_val=E - 1)
                g.tensor_tensor(slot_x[:, q, 0:D], slot_x[:, q, 0:D], b3_rows[:, bass.ds(e, 1), :].rearrange("p o d -> p (o d)"),
                                ALU.add).then_inc(residual_done, 1)

            lo_xT(0)
            lo_xT(1)
            lo_h1(0)

            def slot(i, run, q):
                if follows(i, 2):
                    lo_xT(i + 2)
                if not last_but_one(i):
                    lo_h2(i)
                if follows(i, 1):
                    lo_h1(i + 1)
                if last_but_one(i):
                    lo_h2(i)
                add_bias(i, run, q)
                pool.wait_ge(residual_done, i + 1)
                pool.wait_ge(y_copied, i + 1)
                alone(pool)
                g.tensor_tensor(y[:, q, :], y[:, q, :], slot_x[:, q, 0:D], ALU.add).then_inc(y_done, 1)
                pool.wait_ge(y_done, i + 1)
                alone(pool)
                g.indirect_dma_start(out=out_rows, out_offset=bass.IndirectOffsetOnAxis(ap=ids_of(i, q)[:, 1:2], axis=0),
                                     in_=y[:, q, :], in_offset=None, bounds_check=N_TOKENS - 1, oob_is_err=False).then_inc(y_stored[q], 16)
                last = before_by(1, i, run, q)
                if last and follows(i, AHEAD - 1):
                    gather_slot(i + AHEAD - 1, last[0] + 1, last[1])

            over_slots(pool, slot)
            pool.wait_ge(slot_in[SLOTS % AHEAD], 16 * (SLOTS // AHEAD + 1))

        @block.scalar
        def _(act):
            a = nc.scalar

            def copy_ctxT(n, jt):
                act.wait_ge(ctxT_filled, 2 * n + jt + 1)
                a.copy(ctxT[:, :, jt * P:(jt + 1) * P], ps_ctx[:, 0:3 * P].rearrange("p (c j) -> p c j", c=3)).then_inc(ctxT_copied, 1)

            def round_ctx(T, b):
                act.wait_ge(ctx_in[b], 16 * (T + 1))
                a.copy(ctx_split[:, b, :, 0:C], ctx_raw[:, b, :, :]).then_inc(split_hi, 1)

            def exponentials(n, k, half):
                for g in (2 * half, 2 * half + 1):
                    act.wait_ge(s_masked, GROUPS * n + g + 1)
                    last = a.activation(prob[:, g, :], prob[:, g, :], ACT.Exp, bias=neg_max[:, g:g + 1], scale=-1.0,
                                        accum_out=row_sum[:, k % 2, g:g + 1])
                    last.then_inc(exp_done, 1)

            def copy_k(n):
                act.wait_ge(k_filled, n + 1)
                a.copy(kT[0][:, :, 0:JM], ps_k[:, :].rearrange("p (c j) -> p c j", c=2)).then_inc(k_hi_done, 1)

            def copy_v(n, k):
                act.wait_ge(v_filled, n + 1)
                a.copy(v[:, k % 2, :, :].rearrange("p t d -> p (t d)"), ps_v[:, :]).then_inc(v_copied, 1)

            def middle(T, k):
                has_q, has_out, has_local = parts(T)
                if k == 1 and has_q:
                    act.wait_ge(m_filled, turn(T, 2) + 1)
                    if not (isinstance(T, int) and T < 0):
                        act.wait_ge(qd_done, BT * (T + 1))
                    a.copy(q[0][:, :, :].rearrange("p c s -> p (c s)"), ps_m[:, 0:2 * P]).then_inc(q_hi_done, 1)
                if k == 2 and (has_out or has_local):
                    act.wait_ge(m_filled, turn(T, 4) + 1)
                    lo, hi = (0 if has_out else 2 * P), (4 * P if has_local else 2 * P)
                    a.copy(turned4[:, lo:hi], ps_m[:, lo:hi]).then_inc(m_emptied, 1)

            def end(T, k):
                has_q, has_out, has_local = parts(T)
                if k == 0 and has_out:
                    act.wait_ge(m_filled, turn(T, 1) + 1)
                    a.copy(attnT[:, :, :].rearrange("p c s -> p (c s)"), ps_m[:, 0:2 * P]).then_inc(m_emptied, 1)

            def local_exponentials(T):
                act.wait_ge(m_emptied, turn(T - 1, 7) + 1)
                a.activation(lprob[:, :], lprob[:, :], ACT.Exp, bias=lneg_max[:, 0:1], scale=-1.0,
                             accum_out=lrow_sum[:, 0:1]).then_inc(lexp_done, 1)

            def keep_rows(T):
                act.wait_ge(xn3_done, T - 1)
                act.dma_start(rows_dram.rearrange("(t p) d -> t p d", p=P)[T - 2], x3n[:, :]).then_inc(rows_done, 16)

            def iteration(T):
                has_q, has_out, has_local = parts(T)
                if isinstance(T, int) and T < 0:
                    round_ctx(0, 0)
                    act.wait_ge(kv_in, 16 * 7)
                    a.copy(wkv_hi[:, :, :, :], wkv[:, :, :, :]).then_inc(wkv_split, 1)
                    copy_ctxT(0, 0)
                    copy_ctxT(0, 1)
                    for b in range(1, BT):
                        round_ctx(0, b)
                    copy_k(0)
                    copy_v(0, 0)
                if isinstance(T, int) and T == 0:
                    copy_ctxT(1, 0)
                for k in range(BT):
                    n = BT * T + k
                    ahead = in_tiles(T) and exists(T, k + 1)
                    if k == 0 and has_local:
                        local_exponentials(T)
                    if in_tiles(T):
                        exponentials(n, k, 0)
                    if ahead:
                        copy_ctxT(n + 1, 1)
                    if in_tiles(T):
                        exponentials(n, k, 1)
                    middle(T, k)
                    if ahead:
                        copy_k(n + 1)
                    if in_tiles(T) and has_q:
                        round_ctx(T + 1, k)
                    if k == 2 and has_local:
                        keep_rows(T)
                    if ahead:
                        copy_v(n + 1, k + 1)
                    if in_tiles(T) and exists(T, k + 2):
                        copy_ctxT(n + 2, 0)
                    end(T, k)

            over_tiles(act, iteration)

            def copy_xT(i):
                act.wait_ge(xT_filled, i + 1)
                a.copy(flat3(xT_parts[HI]), ps_xT[:, 0:D]).then_inc(xT_hi_done, 1)
                a.copy(flat3(xT_raw[:, :, :]), ps_xT[:, 0:D]).then_inc(xT_copied, 1)

            def copy_z1(i):
                for half in range(2):
                    act.wait_ge(z1_filled, 2 * i + half + 1)
                    a.copy(z1[:, half * F1 // 2:(half + 1) * F1 // 2], ps_z1[half][:, :]).then_inc(z1_copied, 1)

            def copy_y(i, q):
                act.wait_ge(y_filled, i + 1)
                alone(act)
                a.copy(y[:, q, :], ps_y[:, 0:D]).then_inc(y_copied, 1)

            def copy_z2(i):
                act.wait_ge(z2_filled, i + 1)
                a.copy(z2, ps_z2[:, :]).then_inc(z2_copied, 1)

            def first_layer(i, e):
                for half in range(2):
                    act.wait_ge(t1_filled, 2 * i + half + 1)
                    alone(act)
                    for c in range(4):
                        f = 4 * half + c
                        last = a.activation(h1[:, f, :], ps_t1[half][:, c * P:(c + 1) * P], ACT.Gelu,
                                            bias=bias_cols[:, bass.ds(e * (F1 // P) + f, 1)])
                    last.then_inc(gelu1_done, 1)
                    act.wait_ge(gelu1_done, 2 * i + half + 1)
                    a.copy(h1_parts[HI][:, 4 * half:4 * half + 4, :], h1[:, 4 * half:4 * half + 4, :]).then_inc(h1_hi_done, 1)

            def second_layer(i, e):
                act.wait_ge(t2_filled, i + 1)
                alone(act)
                for c in range(F2 // P):
                    last = a.activation(h2[:, c, :], ps_t2[:, c * P:(c + 1) * P], ACT.Gelu,
                                        bias=bias_cols[:, bass.ds(e * (F2 // P) + E * F1 // P + c, 1)])
                last.then_inc(gelu2_done, 1)
                act.wait_ge(gelu2_done, i + 1)
                a.copy(h2_parts[HI], h2).then_inc(h2_hi_done, 1)

            def expert_of(i):
                return act.value_load(slot_expert_int[0:1, bass.ds(i, 1)], min_val=0, max_val=E - 1)

            act.wait_ge(bias_turned, 1)
            a.copy(bias_cols[:, :], ps_p[:, 0:E * (F1 + F2) // P]).then_inc(bias_done, 1)
            act.wait_ge(bias_done, 1)
            act.wait_ge(route, ROUTED)
            copy_xT(0)
            copy_z1(0)
            copy_xT(1)
            first_layer(0, expert_of(0))
            copy_z1(1)

            def slot(i, run, q):
                copy_z2(i)
                if not follows(i, 1):
                    copy_y(i - 1, q - 1)
                if follows(i, 2):
                    copy_xT(i + 2)
                if not last_but_one(i):
                    second_layer(i, expert_of(i))
                if follows(i, 1):
                    first_layer(i + 1, expert_of(i + 1))
                if last_but_one(i):
                    second_layer(i, expert_of(i))
                if follows(i, 2):
                    copy_z1(i + 2)
                if not last_but_one(i):
                    copy_y(i, q)

            over_slots(act, slot)

        @block.vector
        def _(dve):
            d = nc.vector

            def f32(ap):
                return ap.bitcast(F32)

            def last_rows():
                dve.wait_ge(last_step, 2)
                d.tensor_copy(last_k[0][:, :, :], ps_p[:, 0:2 * B].rearrange("p (c b) -> p c b", c=2)).then_inc(last_copied, 1)
                dve.wait_ge(last_copied, 3)
                d.tensor_tensor(last_k[1][:, :, :], ps_p[:, 0:2 * B].rearrange("p (c b) -> p c b", c=2), f32(last_k[0][:, :, :]),
                                ALU.subtract).then_inc(last_copied, 1)
                dve.wait_ge(consts, 7)
                for g in range(GROUPS):
                    last = d.tensor_copy(last_v[:, g, g * GC:(g + 1) * GC], ps_o[0:B, g * GC:(g + 1) * GC])
                last.then_inc(last_copied, 1)

            def moments_of(i, t, src):
                d.bn_stats(stats[i][:, :], src).then_inc(ln_stats[i], 1)
                dve.wait_ge(ln_stats[i], t + 1)
                alone(dve)
                d.bn_aggr(moments[i][:, :], stats[i][:, :]).then_inc(ln_moments[i], 1)

            def normalise(i, t, src, dst, done):
                dve.wait_ge(ln_rstd[i], t + 1)
                d.tensor_scalar(dst, src, moments[i][:, 0:1], rstd[i][:, 0:1], ALU.subtract, ALU.mult).then_inc(done, 1)

            def mask_scores(T, n, k, half):
                dve.wait_ge(s_filled, 2 * n + half + 1)
                if half == 0:
                    dve.wait_ge(mask_in[k], 16 * (T + 1))
                alone(dve)
                for r in range(2):
                    g = 2 * half + r
                    d.tensor_tensor_reduce(prob[:, g, :], ps_s[r][:, 0:J], mask_add[:, k, :], -(HD ** -0.5), 3.0e38,
                                           ALU.add, ALU.min, neg_max[:, g:g + 1]).then_inc(s_masked, 1)

            def finish_batch(T, k):
                n = BT * T + k
                dve.wait_ge(exp_done, GROUPS * (n + 1))
                d.reciprocal(row_inv[:, :], row_sum[:, k % 2, :]).then_inc(inv_done, 1)
                dve.wait_ge(inv_done, n + 1)
                dve.wait_ge(o_filled, n + 1)
                if k == 0 and not (isinstance(T, int) and T < 1):
                    dve.wait_ge(m_filled, turn(T, 1) + 1)
                for h in range(HG):
                    p0 = h * S
                    last = d.tensor_tensor(
                        attn[k * S:(k + 1) * S, :].rearrange("p (g h e) -> p g h e", g=GROUPS, h=HG)[:, :, h, :],
                        ps_o[p0:p0 + S, 0:D].rearrange("p (g h e) -> p g h e", g=GROUPS, h=HG)[:, :, h, :],
                        row_inv[p0:p0 + S, :].unsqueeze(2).to_broadcast([S, GROUPS, HD]), ALU.mult)
                last.then_inc(o_done, 1)

            def copy_probT(n, jt):
                if jt == 0:
                    dve.wait_ge(lastp_filled, n + 1)
                    d.tensor_copy(last_probT[:, :], ps_o[0:GROUPS, D:D + P])
                dve.wait_ge(p_filled, 2 * n + jt + 1)
                d.tensor_copy(probT[:, jt, :], ps_p[:, :]).then_inc(p_copied, 1)

            def middle(T, k):
                has_q, has_out, has_local = parts(T)
                if k == 0 and (has_q or has_local):
                    dve.wait_ge(m_filled, turn(T, 0) + 1)
                    lo, hi = (0 if has_q else 2 * P), (3 * P if has_local else 2 * P)
                    d.tensor_copy(turned0[:, lo:hi], ps_m[:, lo:hi]).then_inc(m_emptied, 1)
                if k == 1 and (has_q or has_local):
                    dve.wait_ge(m_filled, turn(T, 2) + 1)
                    if has_q:
                        dve.wait_ge(q_hi_done, T + 2)
                        last = d.tensor_tensor(q[1][:, :, :].rearrange("p c s -> p (c s)"), ps_m[:, 0:2 * P],
                                               f32(q[0][:, :, :].rearrange("p c s -> p (c s)")), ALU.subtract)
                        if not has_local:
                            last.then_inc(m_emptied, 1)
                    if has_local:
                        t = T - 2
                        dve.wait_ge(lexp_done, t + 1)
                        d.reciprocal(lrow_inv[:, :], lrow_sum[:, :]).then_inc(linv_done, 1)
                        dve.wait_ge(linv_done, t + 1)
                        x3 = x3n[:, 0:D]
                        dve.wait_ge(rows_done, 16 * t)
                        d.scalar_tensor_tensor(out=x3, in0=ps_m[:, 2 * P:4 * P], scalar=lrow_inv[:, 0:1], in1=x2[:, :],
                                               op0=ALU.mult, op1=ALU.add).then_inc(m_emptied, 1)
                if k == 3 and (has_out or has_local):
                    dve.wait_ge(m_filled, turn(T, 6) + 1)
                    if has_out:
                        last = d.tensor_tensor(lv[:, :], ps_m[:, 0:D], bv_rows[:, :], ALU.add)
                    if has_local:
                        last = d.tensor_tensor(logits[:, :, bass.ds(T - 2, 1)].rearrange("p e o -> p (e o)"), ps_m[:, D:D + E],
                                               br_rows[:, :], ALU.add)
                    last.then_inc(m_emptied, 1)

            def end(T, k):
                has_q, has_out, has_local = parts(T)
                if k == 1 and has_local:
                    dve.wait_ge(m_emptied, turn(T, 2) + 1)
                    moments_of(2, T - 2, x3n[:, 0:D])
                if k == 1 and has_out:
                    t = T - 1
                    dve.wait_ge(m_filled, turn(T, 3) + 1)
                    dve.wait_ge(xr_in, 16 * (t + 1))
                    d.tensor_tensor(x2[:, :], ps_m[:, 0:D], xr[:, :], ALU.add).then_inc(m_emptied, 1)
                    dve.wait_ge(m_emptied, turn(T, 3) + 1)
                    moments_of(1, t, x2[:, :])
                if k == 2 and has_out:
                    if isinstance(T, int) and T == 1:
                        dve.wait_ge(w_in, 16 * 9)
                    dve.wait_ge(m_filled, turn(T, 5) + 1)
                    d.tensor_tensor(lqk[:, :, :], ps_m[:, :].rearrange("p (w s) -> p w s", w=4),
                                    lbias[:, :].unsqueeze(2).to_broadcast([P, 4, P]), ALU.add).then_inc(m_emptied, 1)
                if k == 3 and has_out:
                    dve.wait_ge(m_filled, turn(T, 7) + 1)
                    alone(dve)
                    d.tensor_tensor_reduce(lprob[:, :], ps_m[:, 0:P], band[:, :], -(D ** -0.5), 3.0e38,
                                           ALU.add, ALU.min, lneg_max[:, 0:1]).then_inc(m_emptied, 1)

            def lo_keys(n):
                dve.wait_ge(k_hi_done, n + 1)
                d.tensor_tensor(kT[1][:, :, 0:JM], ps_k[:, :].rearrange("p (c j) -> p c j", c=2), f32(kT[0][:, :, 0:JM]),
                                ALU.subtract).then_inc(k_lo_done, 1)

            def iteration(T):
                has_q, has_out, has_local = parts(T)
                first = isinstance(T, int) and T < 0
                if first:
                    dve.wait_ge(x_in, 16)
                    moments_of(0, 0, xt[:, :])
                    dve.wait_ge(wkv_split, 1)
                    d.tensor_tensor(wkv_lo[:, :, :, :], wkv[:, :, :, :], f32(wkv_hi[:, :, :, :]), ALU.subtract).then_inc(wkv_split, 1)
                    dve.wait_ge(last_step, 1)
                    d.tensor_copy(last_ctxT[:, 0, :], ps_m[:, 0:B]).then_inc(last_copied, 1)
                    d.tensor_copy(last_ctxT[0:C2, 1, :], ps_m[0:C2, B:2 * B]).then_inc(last_copied, 1)
                    normalise(0, 0, xt[:, :], xn1[:, :], xn1_done)
                    lo_keys(0)
                    middle(T, 0)
                    middle(T, 1)
                    last_rows()
                    return
                for k in range(BT):
                    n = BT * T + k
                    if k == 0 and has_q:
                        dve.wait_ge(x_in, 16 * (T + 2))
                        moments_of(0, T + 1, xt[:, :])
                    if in_tiles(T):
                        mask_scores(T, n, k, 0)
                    if k == 0 and has_q:
                        normalise(0, T + 1, xt[:, :], xn1[:, :], xn1_done)
                    if k == 2 and has_local:
                        normalise(2, T - 2, x3n[:, 0:D], x3n[:, D:2 * D], xn3_done)
                    if k == 2 and has_out:
                        normalise(1, T - 1, x2[:, :], xn2[:, :], xn2_done)
                    if not first and exists(T, k - 1) and not (isinstance(T, int) and BT * T + k > B):
                        finish_batch(T if k else T - 1, (k - 1) % BT)
                    if in_tiles(T):
                        mask_scores(T, n, k, 1)
                    middle(T, k)
                    if in_tiles(T):
                        copy_probT(n, 0)
                        if exists(T, k + 1):
                            lo_keys(n + 1)
                        copy_probT(n, 1)
                    end(T, k)

            over_tiles(dve, iteration)

            steps = [0]

            def then(ins):
                steps[0] += 1
                ins.then_inc(route, 1)
                dve.wait_ge(route, steps[0])

            def by_tile(ap):
                return ap.rearrange("p e t -> p t e")

            def over_experts(ap):
                return ap.unsqueeze(1).to_broadcast([P, E, TILES])

            def over_all_tiles(ap):
                return ap.unsqueeze(2).to_broadcast([P, E, TILES])

            dve.wait_ge(router_consts, 11)
            dve.wait_ge(m_emptied, turn(TILES + 1, 6) + 1)
            then(d.tensor_reduce(top[:, :], by_tile(logits[:, :, :]), AX.X, ALU.max))
            then(d.tensor_tensor(tied[:, :, :], logits[:, :, :], over_experts(top[:, :]), ALU.is_ge))
            then(d.tensor_tensor(tied[:, :, :], tied[:, :, :], over_all_tiles(expert_rank[:, :]), ALU.mult))
            then(d.tensor_reduce(first[:, :], by_tile(tied[:, :, :]), AX.X, ALU.max))
            then(d.tensor_tensor(chosen[:, :, :], tied[:, :, :], over_experts(first[:, :]), ALU.is_equal))
            then(d.tensor_copy(chosen_bf[:, :, :], chosen[:, :, :]))
            dve.wait_ge(chosen_counted, 1)
            n_et = E * TILES
            earlier = ps_m[:, 0:n_et].rearrange("p (e t) -> p e t", e=E)
            then(d.tensor_copy(tile_counts[:, :, :], ps_m[:, n_et:2 * n_et].rearrange("p (e t) -> p e t", e=E)))
            flat = lambda ap: ap.rearrange("p e t -> p (e t)")
            then(d.tensor_tensor_scan(flat(counts[:, :, :]), flat(restart[:, :, :]), flat(tile_counts[:, :, :]), 0.0, ALU.mult, ALU.add))
            then(d.tensor_scalar(padded[:, :], counts[:, :, TILES - 1:TILES].rearrange("p e o -> p (e o)"), 1.0, float(P - 1), ALU.max, ALU.add))
            then(d.tensor_scalar(slots_int[:, :], padded[:, :], 7, None, ALU.logical_shift_right))
            then(d.tensor_copy(slots[:, :], slots_int[:, :]))
            then(d.tensor_tensor_scan(slot_end[:, :], ones_row[:, :], slots[:, :], 0.0, ALU.mult, ALU.add))
            then(d.tensor_tensor(slot_start[:, :], slot_end[:, :], slots[:, :], ALU.subtract))
            then(d.tensor_tensor(place[:, :, :], counts[:, :, :], tile_counts[:, :, :], ALU.subtract))
            then(d.tensor_tensor(place[:, :, :], place[:, :, :], earlier, ALU.add))
            then(d.scalar_tensor_tensor(out=place[:, :, :], in0=over_all_tiles(slot_start[:, :]), scalar=float(P), in1=place[:, :, :],
                                        op0=ALU.mult, op1=ALU.add))
            then(d.tensor_tensor(place[:, :, :], place[:, :, :], chosen[:, :, :], ALU.mult))
            then(d.tensor_reduce(target[:, :], by_tile(place[:, :, :]), AX.X, ALU.add))
            then(d.tensor_copy(target_int[:, :], target[:, :]))
            d.tensor_scalar(part_int[:, 0, :], target_int[:, :], 7, None, ALU.logical_shift_right)
            then(d.tensor_scalar(part_int[:, 1, :], target_int[:, :], P - 1, None, ALU.bitwise_and))
            then(d.tensor_copy(part_of[:, :, :], part_int[:, :, :]))
            for T in range(0, TILES, 4):
                last = d.tensor_tensor(in_row[:, T:T + 4, :], row_number[:, :].unsqueeze(1).to_broadcast([P, 4, P]),
                                part_of[:, 1, T:T + 4].unsqueeze(2).to_broadcast([P, 4, P]), ALU.is_equal)
                if T == 0:
                    then(d.tensor_tensor(in_slot[:, :, :], slot_number[:, :].unsqueeze(1).to_broadcast([P, TILES, SLOTS]),
                                         part_of[:, 0, :].unsqueeze(2).to_broadcast([P, TILES, SLOTS]), ALU.is_equal))
                    d.tensor_scalar(in_slot_tokens[:, :, 0, :], in_slot[:, :, :], token_row[:, 0:1], None, ALU.mult)
                    last = d.tensor_tensor(in_slot_tokens[:, :, 1, :], in_slot[:, :, :],
                                           tile_base[:, :].unsqueeze(2).to_broadcast([P, TILES, SLOTS]), ALU.mult)
                last.then_inc(rows_matched, 1)
            dve.wait_ge(tokens_found, 1)
            then(d.tensor_reduce(slot_token[:, :], ps_m[:, 0:2 * SLOTS].rearrange("p (w s) -> p s w", w=2), AX.X, ALU.add))
            d.tensor_scalar(slot_empty[:, :], slot_token[:, :], 0.5, float(2 * N_TOKENS), ALU.is_lt, ALU.mult)
            then(d.tensor_scalar(slot_ids[:, 0:SLOTS, 0], slot_token[:, :], -1.0, 0.0, ALU.add, ALU.max))
            then(d.scalar_tensor_tensor(out=slot_ids[:, 0:SLOTS, 1], in0=slot_token[:, :], scalar=-1.0, in1=slot_empty[:, :],
                                        op0=ALU.add, op1=ALU.add))
            assert steps[0] == MAPPED
            then(d.tensor_tensor(past[:, :, :], slot_number[:, :].unsqueeze(2).to_broadcast([P, SLOTS, E]),
                                 slot_end[:, :].unsqueeze(1).to_broadcast([P, SLOTS, E]), ALU.is_ge))
            then(d.tensor_reduce(slot_expert[:, :], past[:, :, :], AX.X, ALU.add))
            then(d.tensor_scalar(slot_expert[:, :], slot_expert[:, :], float(E - 1), None, ALU.min))
            d.tensor_copy(slot_end_int[:, :], slot_end[:, :])
            d.tensor_copy(slot_expert_int[:, :], slot_expert[:, :]).then_inc(route, 1)
            assert steps[0] + 1 == ROUTED

            k = 0
            for first_matrix, e in EARLY + LATE:
                w, raw, buffers, w_in_buffer, ready = ((w1, w1_raw, BUFFERS1, w1_in, w1_ready) if first_matrix else
                                                      (w23, w23_raw, BUFFERS23, w23_in, w23_ready))
                b = e % buffers
                pieces = [(w_in_buffer[b], slice(0, COLS1))] if first_matrix else zip(w_in_buffer[b], PIECES)
                for piece_in, columns in pieces:
                    dve.wait_ge(piece_in, 16 * (e // buffers + 1))
                    d.tensor_copy(w[:, b, HI, columns], raw[:, b, columns]).then_inc(rounded, 1)
                    k += 1
                    dve.wait_ge(rounded, k)
                    d.tensor_tensor(w[:, b, LO, columns], raw[:, b, columns], f32(w[:, b, HI, columns]), ALU.subtract).then_inc(ready, 1)

        @block.tensor
        def _(pe):
            t = nc.tensor
            chunks = lambda hi, lo: ((0, hi, 0), (1, hi, 1), (2, hi, 0), (0, lo, 0), (1, lo, 1))

            def transpose_ctx(T, b, jt):
                n = BT * T + b
                if jt == 0:
                    pe.wait_ge(split_done, n + 1)
                pe.wait_ge(ctxT_copied, 2 * n + jt)
                for c in range(3):
                    last = t.transpose(ps_ctx[:, c * P:(c + 1) * P].bitcast(F32R), ctx_split[:, b, jt, c * P:(c + 1) * P], ident_r[:, :])
                last.then_inc(ctxT_filled, 1)

            def keys(n):
                pe.wait_ge(ctxT_copied, 2 * n + 2)
                pe.wait_ge(k_lo_done, n)
                for half in range(2):
                    for i, (c, w, r) in enumerate(chunks(wkv_hi, wkv_lo)):
                        last = t.matmul(ps_k[:, half * JM:(half + 1) * JM], w[:, 0, r, half * P:(half + 1) * P], ctxT[:, c, :],
                                        start=(i == 0), stop=(i == 4))
                last.then_inc(k_filled, 1)

            def values(n):
                pe.wait_ge(v_copied, n)
                for jt in range(2):
                    for i, (c, w, r) in enumerate(chunks(wkv_hi, wkv_lo)):
                        last = t.matmul(ps_v[:, jt * D:(jt + 1) * D], ctxT[:, c, jt * P:(jt + 1) * P], w[:, 1, r, :],
                                        start=(i == 0), stop=(i == 4))
                last.then_inc(v_filled, 1)

            def scores(n, k, half):
                if half == 0:
                    pe.wait_ge(k_lo_done, n + 1)
                    pe.wait_ge(k_last_done, n + 1)
                    pe.wait_ge(qd_done, n + 1)
                pe.wait_ge(s_masked, GROUPS * n + 2 * half)
                for i, (qi, ki) in enumerate(((0, 0), (0, 1), (1, 0))):
                    for r in range(2):
                        rs = slice(r * 64, r * 64 + 64)
                        last = t.matmul(ps_s[r][:, 0:J + 1], qd[qi][rs, k, half, :], kT[ki][rs, half, :],
                                        start=(i == 0), stop=(i == 2))
                last.then_inc(s_filled, 1)

            def weigh(T, k):
                n = BT * T + k
                pe.wait_ge(p_copied, 2 * n + 2)
                pe.wait_ge(v_copied, n + 1)
                pe.wait_ge(lastv_in[k], 16 * (T + 1))
                t.matmul(ps_o[:, 0:D], last_probT[:, :], last_v_rows[:, k, :], start=True, stop=False, skip_group_check=True)
                for g in range(GROUPS):
                    for jt in range(2):
                        last = t.matmul(ps_o[:, g * GC:(g + 1) * GC], probT[:, jt, g * P:(g + 1) * P],
                                        v[:, k % 2, jt, g * GC:(g + 1) * GC], start=False,
                                        stop=(g == GROUPS - 1 and jt == 1), skip_group_check=True)
                last.then_inc(o_filled, 1)

            def transpose_probs(n, jt):
                if jt == 0:
                    pe.wait_ge(exp_done, GROUPS * (n + 1))
                    pe.wait_ge(o_done, n)
                    t.transpose(ps_o[0:GROUPS, D:D + P], prob[:, :, JM:J].rearrange("p g o -> p (g o)"), ident[:, :]).then_inc(lastp_filled, 1)
                pe.wait_ge(p_copied, 2 * n + jt)
                for g in range(GROUPS):
                    last = t.transpose(ps_p[:, g * P:(g + 1) * P], prob[:, g, jt * P:(jt + 1) * P], ident[:, :])
                last.then_inc(p_filled, 1)

            def keep_clock(n):
                for _ in range(n):
                    t.transpose(ps_s[0][:, 0:P], ident[:, :], ident[:, :])

            def my_turn(T, e):
                pe.wait_ge(m_emptied, turn(T, e))

            def middle(T, k):
                has_q, has_out, has_local = parts(T)
                last = None
                if k == 0 and (has_q or has_local):
                    my_turn(T, 0)
                    if isinstance(T, int) and T < 0:
                        pe.wait_ge(wq_in, 16)
                    if has_q:
                        pe.wait_ge(xn1_done, T + 2)
                        for c in range(2):
                            last = t.transpose(ps_m[:, c * P:(c + 1) * P], xn1[:, c * P:(c + 1) * P], ident[:, :])
                    if has_local:
                        pe.wait_ge(lexp_done, T - 1)
                        last = t.transpose(ps_m[:, 2 * P:3 * P], lprob[:, :], ident[:, :])
                if k == 1 and (has_q or has_local):
                    my_turn(T, 2)
                    if has_q:
                        for half in range(2):
                            for c in range(2):
                                last = t.matmul(ps_m[:, half * P:(half + 1) * P], wq[:, c, half * P:(half + 1) * P],
                                                turned0[:, c * P:(c + 1) * P], start=(c == 0), stop=(c == 1))
                    if has_local:
                        last = t.matmul(ps_m[:, 2 * P:4 * P], turned0[:, 2 * P:3 * P], lv[:, :], start=True, stop=True)
                if k == 2 and (has_out or has_local):
                    my_turn(T, 4)
                    if has_out:
                        pe.wait_ge(xn2_done, T)
                        for c in range(2):
                            last = t.transpose(ps_m[:, c * P:(c + 1) * P], xn2[:, c * P:(c + 1) * P], ident[:, :])
                    if has_local:
                        pe.wait_ge(xn3_done, T - 1)
                        for c in range(2):
                            last = t.transpose(ps_m[:, (2 + c) * P:(3 + c) * P], x3n[:, D + c * P:D + (c + 1) * P], ident[:, :])
                if k == 3 and (has_out or has_local):
                    my_turn(T, 6)
                    if has_out:
                        for c in range(2):
                            last = t.matmul(ps_m[:, 0:D], turned4[:, c * P:(c + 1) * P], lw[:, 2, c, :], start=(c == 0), stop=(c == 1))
                    if has_local:
                        for c in range(2):
                            last = t.matmul(ps_m[:, D:D + E], turned4[:, (2 + c) * P:(3 + c) * P], wr[:, c, :], start=(c == 0), stop=(c == 1))
                if last is not None:
                    last.then_inc(m_filled, 1)
                    if isinstance(T, int) and T >= TILES:
                        keep_clock(9)

            def end(T, k):
                has_q, has_out, has_local = parts(T)
                if not has_out:
                    return
                my_turn(T, 2 * k + 1)
                if k == 0:
                    if isinstance(T, int) and T == 1:
                        pe.wait_ge(w_in, 16 * 9)
                    pe.wait_ge(o_done, BT * T)
                    for c in range(2):
                        last = t.transpose(ps_m[:, c * P:(c + 1) * P], attn[:, c * P:(c + 1) * P], ident[:, :])
                if k == 1:
                    for c in range(2):
                        last = t.matmul(ps_m[:, 0:D], attnT[:, c, :], wo[:, c, :], start=(c == 0), stop=(c == 1))
                if k == 2:
                    for w in range(4):
                        half = w % 2
                        for c in range(2):
                            last = t.matmul(ps_m[:, w * P:(w + 1) * P], lw[:, w // 2, c, half * P:(half + 1) * P],
                                            turned4[:, c * P:(c + 1) * P], start=(c == 0), stop=(c == 1))
                if k == 3:
                    for c in range(2):
                        last = t.matmul(ps_m[:, 0:P], lqk[:, c, :], lqk[:, 2 + c, :], start=(c == 0), stop=(c == 1))
                last.then_inc(m_filled, 1)
                if isinstance(T, int) and T >= TILES:
                    keep_clock(9)

            def last_rows():
                for half in range(2):
                    for c, rows_c in ((0, P), (1, C2)):
                        t.matmul(ps_p[:, half * B:(half + 1) * B], wkv[0:rows_c, 0, c, half * P:(half + 1) * P],
                                 last_ctxT[0:rows_c, c, :], start=(c == 0), stop=(c == 1))
                for c, rows_c in ((0, P), (1, C2)):
                    last = t.matmul(ps_o[0:B, 0:D], last_ctxT[0:rows_c, c, :], wkv[0:rows_c, 1, c, :], start=(c == 0), stop=(c == 1))
                last.then_inc(last_step, 1)

            def iteration(T):
                first = isinstance(T, int) and T < 0
                if first:
                    pe.wait_ge(consts, 4)
                    pe.wait_ge(consts, 7)
                    pe.wait_ge(kv_in, 16 * 7)
                    t.transpose(ps_m[:, 0:B], last_ctx[:, 0:P], ident[0:B, 0:B])
                    t.transpose(ps_m[0:C2, B:2 * B], last_ctx[:, P:C], ident[0:B, 0:B]).then_inc(last_step, 1)
                    transpose_ctx(0, 0, 0)
                    transpose_ctx(0, 0, 1)
                    pe.wait_ge(wkv_split, 2)
                    keys(0)
                    pe.wait_ge(last_copied, 2)
                    middle(T, 0)
                    values(0)
                    middle(T, 1)
                    last_rows()
                    transpose_ctx(0, 1, 0)
                    return
                if isinstance(T, int) and T == 0:
                    pe.wait_ge(last_copied, 5)
                for k in range(BT):
                    n = BT * T + k
                    ahead = in_tiles(T) and exists(T, k + 1)
                    Ta, ba = (T, k + 1) if k + 1 < BT else (T + 1, 0)
                    if in_tiles(T):
                        scores(n, k, 0)
                    if ahead:
                        transpose_ctx(Ta, ba, 1)
                    if not first and exists(T, k - 1) and not (isinstance(T, int) and BT * T + k > B):
                        weigh(T if k else T - 1, (k - 1) % BT)
                    if in_tiles(T):
                        scores(n, k, 1)
                    middle(T, k)
                    if ahead:
                        keys(n + 1)
                    if in_tiles(T):
                        transpose_probs(n, 0)
                    if ahead:
                        values(n + 1)
                    if in_tiles(T) and exists(T, k + 2):
                        transpose_ctx(*((T, k + 2) if k + 2 < BT else (T + 1, k + 2 - BT)), 0)
                    if in_tiles(T):
                        transpose_probs(n, 1)
                    end(T, k)

            over_tiles(pe, iteration)

            pe.wait_ge(bias_in, 32)
            n_b = E * (F1 + F2) // P
            pe.wait_ge(route, 6)
            n_et = E * TILES
            chosen_flat = chosen_bf[:, :, :].rearrange("p e t -> p (e t)")
            t.matmul(ps_m[:, 0:n_et], before[:, :], chosen_flat, start=True, stop=True)
            t.matmul(ps_m[:, n_et:2 * n_et], ones_bf[:, :], chosen_flat, start=True, stop=True).then_inc(chosen_counted, 1)
            t.transpose(ps_p[:, 0:n_b], bias_rows[:, :], ident[0:n_b, 0:n_b]).then_inc(bias_turned, 1)
            for T in range(TILES):
                pe.wait_ge(rows_matched, T // 4 + 1)
                last = t.matmul(ps_m[:, 0:2 * SLOTS], in_row[:, T, :], in_slot_tokens[:, T, :, :].rearrange("p w s -> p (w s)"),
                                start=(T == 0), stop=(T == TILES - 1))
            last.then_inc(tokens_found, 1)

            PRODUCTS = ((HI, HI), (HI, LO), (LO, HI))

            def weight(w, buffer, part, at, n):
                return w[:, bass.ds(buffer, 1), part, at:at + n].rearrange("p o n -> p (o n)")

            def turn_x(i, run, q):
                pe.wait_ge(slot_in[q], 16 * (run + 1))
                pe.wait_ge(xT_copied, i)
                for c in range(2):
                    last = t.transpose(ps_xT[:, c * P:(c + 1) * P], slot_x[:, q, D + c * P:D + (c + 1) * P], ident[:, :])
                last.then_inc(xT_filled, 1)

            def layer1(i, e):
                pe.wait_ge(w1_ready, e + 1)
                pe.wait_ge(xT_hi_done, i + 1)
                for half in range(2):
                    pe.wait_ge(z1_copied, 2 * i - 1 + half if follows_first(i) else 0)
                    for xp, wp in PRODUCTS:
                        if half == 0 and xp == LO:
                            pe.wait_ge(xT_done, i + 1)
                        for c in range(2):
                            last = t.matmul(ps_z1[half][:, :], xT_parts[xp][:, c, :], weight(w1, e % BUFFERS1, wp, c * F1 + half * 512, 512),
                                            start=(xp == HI and wp == HI and c == 0), stop=(xp == LO and c == 1))
                    last.then_inc(z1_filled, 1)

            def follows_first(i):
                return not isinstance(i, int) or i > 0

            def turn_z1(i):
                for half in range(2):
                    pe.wait_ge(z1_copied, 2 * i + half + 1)
                    pe.wait_ge(h1_hi_done, 2 * i)
                    for c in range(4):
                        f = 4 * half + c
                        last = t.transpose(ps_t1[half][:, c * P:(c + 1) * P], z1[:, f * P:(f + 1) * P], ident[:, :])
                    last.then_inc(t1_filled, 1)

            def layer2(i, e):
                pe.wait_ge(z2_copied, i)
                for products in (PRODUCTS[0:2], PRODUCTS[2:3]):
                    for half in range(2):
                        pe.wait_ge(w23_ready, 3 * e + half + 1)
                        for hp, wp in products:
                            for f in range(4 * half, 4 * half + 4):
                                if wp == HI and f == 4 * half:
                                    pe.wait_ge(h1_done if hp == LO else h1_hi_done, 2 * i + half + 1)
                                last = t.matmul(ps_z2[:, :], h1_parts[hp][:, f, :], weight(w23, e % BUFFERS23, wp, f * F2, F2),
                                                start=(hp == HI and wp == HI and f == 0), stop=(hp == LO and f == F1 // P - 1))
                last.then_inc(z2_filled, 1)

            def turn_z2(i):
                pe.wait_ge(z2_copied, i + 1)
                pe.wait_ge(h2_hi_done, i)
                for c in range(F2 // P):
                    last = t.transpose(ps_t2[:, c * P:(c + 1) * P], z2[:, c * P:(c + 1) * P], ident[:, :])
                last.then_inc(t2_filled, 1)

            def layer3(i, e):
                pe.wait_ge(w23_ready, 3 * e + 3)
                pe.wait_ge(h2_hi_done, i + 1)
                pe.wait_ge(y_copied, i)
                for hp, wp in PRODUCTS:
                    if hp == LO:
                        pe.wait_ge(h2_done, i + 1)
                    for c in range(F2 // P):
                        last = t.matmul(ps_y[:, 0:D], h2_parts[hp][:, c, :], weight(w23, e % BUFFERS23, wp, W3_AT + c * D, D),
                                        start=(hp == HI and wp == HI and c == 0), stop=(hp == LO and c == F2 // P - 1))
                last.then_inc(y_filled, 1)

            def expert_of(i):
                return pe.value_load(slot_expert_int[0:1, bass.ds(i, 1)], min_val=0, max_val=E - 1)

            pe.wait_ge(route, ROUTED)
            experts = [expert_of(i) for i in range(2)]
            turn_x(0, 0, 0)
            layer1(0, experts[0])
            turn_x(1, 0, 1)
            turn_z1(0)
            layer1(1, experts[1])

            def slot(i, run, q):
                expert = expert_of(i)
                layer2(i, expert)
                if postponed:
                    layer3(i - 1, postponed.pop())
                if follows(i, 2):
                    ahead = expert_of(i + 2)
                    turn_x(i + 2, run + (q + 2) // AHEAD, (q + 2) % AHEAD)
                if follows(i, 1):
                    turn_z1(i + 1)
                turn_z2(i)
                if follows(i, 2):
                    layer1(i + 2, ahead)
                if last_but_one(i):
                    postponed.append(expert)
                else:
                    layer3(i, expert)

            postponed = []
            over_slots(pe, slot)


_INS = ['x', 'ctx_768', 'mask_BxS2_bf1', 'L0_xattn_Wq', 'L0_xattn_Wk', 'L0_xattn_Wv', 'L0_xattn_Wo',
        'L0_attn_Wq', 'L0_attn_bq', 'L0_attn_Wk', 'L0_attn_bk', 'L0_attn_Wv', 'L0_attn_bv',
        'L0_ffn_Wr', 'L0_ffn_br', 'L0_ffn_W1', 'L0_ffn_b1', 'L0_ffn_W2', 'L0_ffn_b2', 'L0_ffn_W3', 'L0_ffn_b3']
_OUTS = [((64, 32, 256), 'float32')]


def kernel(**inputs):
    import numpy as _np
    import concourse.bacc as _bacc
    from concourse import mybir as _mybir
    from concourse.bass_utils import run_bass_kernel_spmd as _run

    nc = _bacc.Bacc("TRN2", target_bir_lowering=False, num_devices=1)
    arrays, args = {}, []
    for name in _INS:
        a = _np.ascontiguousarray(inputs[name])
        if a.dtype == _np.bool_:
            a = a.view(_np.uint8)
        arrays[f"in_{name}_dram"] = a
        args.append(nc.dram_tensor(f"in_{name}_dram", a.shape, _mybir.dt.from_np(a.dtype), kind="ExternalInput").ap())
    for i, (shape, dtype) in enumerate(_OUTS):
        dt = _mybir.dt.from_np(_np.dtype(dtype))
        args.append(nc.dram_tensor(f"out_{i}_dram", shape, dt, kind="ExternalOutput").ap())
    perceiver_kernel(nc, *args)
    r = _run(nc, [arrays], core_ids=[0])
    got = tuple(r.results[0][f"out_{i}_dram"] for i in range(len(_OUTS)))
    return got[0]
```
